# Optimizing a Trainium2 kernel written in Bass

```python
import numpy as np
import jax
import jax.numpy as jnp

def _softmax(x, axis=-1):
    return jax.nn.softmax(x, axis=axis)

def _gelu(x):
    return jax.nn.gelu(x, approximate=True)

def _silu(x):
    return jax.nn.silu(x)

def _sigmoid(x):
    return jax.nn.sigmoid(x)

def _layernorm(x, axis=-1, eps=1e-05):
    m = jnp.mean(x, axis=axis, keepdims=True)
    v = jnp.var(x, axis=axis, keepdims=True)
    return (x - m) / jnp.sqrt(v + eps)

def _scatter_add(tgt, idx, src, axis=0):
    return tgt.at[idx].add(src)

def _segment_sum(src, seg, n):
    return jax.ops.segment_sum(src, seg, n)
kernel_name = 'mk_flamingo_gated_d1_seqx_r4_e7b2b3'

def setup_inputs(seed: int=0):
    np.random.seed(seed)
    _w = jnp.asarray

    def _rec_inputs():
        import jax
        import jax.numpy as jnp
        _rk = jax.random.key(seed)
        x = -0.0002928 + 1 * jax.random.normal(jax.random.fold_in(_rk, 1), (16, 256, 256), jnp.float32)
        _lenS = 256 - jax.random.randint(jax.random.fold_in(_rk, 7), (16,), 0, max(1, 256 // 4) + 1, jnp.int32)
        _lenS2 = 256 - jax.random.randint(jax.random.fold_in(_rk, 8), (16,), 0, max(1, 256 // 4) + 1, jnp.int32)
        _ctx_1024P = jax.random.normal(jax.random.fold_in(_rk, 11), (16, 16, 256), jnp.float32)
        _ctx_1024c = jax.random.dirichlet(jax.random.fold_in(_rk, 511), 0.3 * jnp.ones((16,), jnp.float32), (16, 256))
        _ctx_1024t = jnp.einsum('bsk,bkd->bsd', _ctx_1024c, _ctx_1024P)
        _ctx_1024t = _ctx_1024t * jax.lax.rsqrt(jnp.mean(jnp.square(_ctx_1024t)) + 1e-12) * 0.953939
        ctx_1024 = -1.39393e-06 + 0.999914 * (_ctx_1024t + 0.3 * jax.random.normal(jax.random.fold_in(_rk, 611), (16, 256, 256), jnp.float32))
        _g = jax.random.normal(jax.random.fold_in(_rk, 9001), (2, 1), jnp.float32)
        _g = jnp.sign(_g) * jnp.maximum(jnp.abs(_g), 1.0) + (_g == 0) * 1.0
        g_xattn = _g[0]
        g_ffn = _g[1]
        return (x, ctx_1024, g_xattn, g_ffn)
    x, ctx_1024, g_xattn, g_ffn = _rec_inputs()

    def _L0_xattn_setup():
        import jax, jax.numpy as jnp
        import numpy as np
        SCALE_BASE = 512.0
        GN_EPS = 1e-05

        def _xpos(x, downscale):
            L, D = (x.shape[-2], x.shape[-1])
            half = D // 2
            base = (jnp.arange(0, D, 2, dtype=jnp.float32) + 0.4 * D) / (1.4 * D)
            min_pos = -(L // 2)
            power = (jnp.arange(min_pos, min_pos + L, dtype=jnp.float32) / SCALE_BASE)[:, None]
            scale = base[None, :] ** power
            inv_freq = 1.0 / 10000.0 ** (jnp.arange(half, dtype=jnp.float32) / half)
            ang = jnp.arange(L, dtype=jnp.float32)[:, None] * inv_freq[None, :]
            sin, cos = (jnp.sin(ang), jnp.cos(ang))
            if downscale:
                scale = 1.0 / scale
            sin_s = jnp.repeat(sin * scale, 2, axis=-1)
            cos_s = jnp.repeat(cos * scale, 2, axis=-1)
            x1, x2 = (x[..., ::2], x[..., 1::2])
            rot = jnp.stack((-x2, x1), axis=-1).reshape(x.shape)
            return x * cos_s + rot * sin_s

        def _decay_mask(L, H):
            gammas = 1.0 - jnp.exp(jnp.linspace(np.log(1.0 / 32.0), np.log(1.0 / 512.0), H)).astype(jnp.float32)
            idx = jnp.arange(L)
            dist = idx[:, None] - idx[None, :]
            causal = dist >= 0
            d = jnp.maximum(dist, 0).astype(jnp.float32)
            return jnp.where(causal[None], gammas[:, None, None] ** d[None], 0.0)
        key = jax.random.key(seed)
        ks = jax.random.split(key, 9)
        B, L, D, H = (2, 512, 256, 16)
        hd = D // H
        return {'query': jax.random.normal(ks[0], (B, L, D), jnp.float32), 'key': jax.random.normal(ks[1], (B, L, D), jnp.float32), 'value': jax.random.normal(ks[2], (B, L, D), jnp.float32), 'W_Q': jax.random.normal(ks[3], (H, D, hd), jnp.float32) / D, 'W_K': jax.random.normal(ks[4], (H, D, hd), jnp.float32) / D, 'W_V': jax.random.normal(ks[5], (H, D, hd), jnp.float32) / D, 'g_w': jax.random.normal(ks[6], (D, D), jnp.float32) * (2.0 / (D + D)) ** 0.5, 'g_b': jnp.zeros((D,), jnp.float32), 'out_w': jax.random.normal(ks[7], (D, D), jnp.float32) * (2.0 / (D + D)) ** 0.5, 'out_b': jnp.zeros((D,), jnp.float32)}
    _L0_xattn_all = _L0_xattn_setup()
    _L0_xattn_in = {k: v for k, v in _L0_xattn_all.items() if k in ('W_Q', 'W_K', 'W_V', 'g_w', 'g_b', 'out_w', 'out_b')}
    del _L0_xattn_all

    def _L0_ffn_setup():
        import jax, jax.numpy as jnp
        import numpy as np
        TOP_K = 2

        def _gelu(x):
            return jax.nn.gelu(x, approximate=False)
        key = jax.random.key(seed)
        ks = jax.random.split(key, 6)
        B, S, D, F, E = (2, 512, 256, 512, 8)
        sc_g = 1.0 / np.sqrt(D)

        def xav(k, shape, fan_in, fan_out):
            lim = np.sqrt(6.0 / (fan_in + fan_out))
            return jax.random.uniform(k, shape, jnp.float32, -lim, lim)
        return {'x': jax.random.normal(ks[0], (B, S, D), jnp.float32), 'Wg': xav(ks[1], (D, E), D, E), 'Wu': xav(ks[2], (E, D, F), D, F), 'Wd': xav(ks[3], (E, F, D), F, D), 'W1': xav(ks[4], (D, F), D, F), 'W2': xav(ks[5], (F, D), F, D)}
    _L0_ffn_all = _L0_ffn_setup()
    _L0_ffn_in = {k: v for k, v in _L0_ffn_all.items() if k in ('Wg', 'Wu', 'Wd', 'W1', 'W2')}
    del _L0_ffn_all
    return {'x': x, 'ctx_1024': ctx_1024, 'g_xattn': g_xattn, 'g_ffn': g_ffn, 'L0_xattn_W_Q': _L0_xattn_in['W_Q'], 'L0_xattn_W_K': _L0_xattn_in['W_K'], 'L0_xattn_W_V': _L0_xattn_in['W_V'], 'L0_xattn_g_w': _L0_xattn_in['g_w'], 'L0_xattn_g_b': _L0_xattn_in['g_b'], 'L0_xattn_out_w': _L0_xattn_in['out_w'], 'L0_xattn_out_b': _L0_xattn_in['out_b'], 'L0_ffn_Wg': _L0_ffn_in['Wg'], 'L0_ffn_Wu': _L0_ffn_in['Wu'], 'L0_ffn_Wd': _L0_ffn_in['Wd'], 'L0_ffn_W1': _L0_ffn_in['W1'], 'L0_ffn_W2': _L0_ffn_in['W2']}

def reference(x, ctx_1024, g_xattn, g_ffn, L0_xattn_W_Q, L0_xattn_W_K, L0_xattn_W_V, L0_xattn_g_w, L0_xattn_g_b, L0_xattn_out_w, L0_xattn_out_b, L0_ffn_Wg, L0_ffn_Wu, L0_ffn_Wd, L0_ffn_W1, L0_ffn_W2):
    import jax
    import jax.numpy as jnp

    def _L0_xattn_ref(query, key, value, W_Q, W_K, W_V, g_w, g_b, out_w, out_b):
        import jax, jax.numpy as jnp
        import numpy as np
        SCALE_BASE = 512.0
        GN_EPS = 1e-05

        def _xpos(x, downscale):
            L, D = (x.shape[-2], x.shape[-1])
            half = D // 2
            base = (jnp.arange(0, D, 2, dtype=jnp.float32) + 0.4 * D) / (1.4 * D)
            min_pos = -(L // 2)
            power = (jnp.arange(min_pos, min_pos + L, dtype=jnp.float32) / SCALE_BASE)[:, None]
            scale = base[None, :] ** power
            inv_freq = 1.0 / 10000.0 ** (jnp.arange(half, dtype=jnp.float32) / half)
            ang = jnp.arange(L, dtype=jnp.float32)[:, None] * inv_freq[None, :]
            sin, cos = (jnp.sin(ang), jnp.cos(ang))
            if downscale:
                scale = 1.0 / scale
            sin_s = jnp.repeat(sin * scale, 2, axis=-1)
            cos_s = jnp.repeat(cos * scale, 2, axis=-1)
            x1, x2 = (x[..., ::2], x[..., 1::2])
            rot = jnp.stack((-x2, x1), axis=-1).reshape(x.shape)
            return x * cos_s + rot * sin_s

        def _decay_mask(L, H):
            gammas = 1.0 - jnp.exp(jnp.linspace(np.log(1.0 / 32.0), np.log(1.0 / 512.0), H)).astype(jnp.float32)
            idx = jnp.arange(L)
            dist = idx[:, None] - idx[None, :]
            causal = dist >= 0
            d = jnp.maximum(dist, 0).astype(jnp.float32)
            return jnp.where(causal[None], gammas[:, None, None] ** d[None], 0.0)
        B, L, D = query.shape
        H = W_Q.shape[0]
        q = jnp.einsum('bld,hde->bhle', query, W_Q)
        k = jnp.einsum('bld,hde->bhle', key, W_K)
        v = jnp.einsum('bld,hde->bhle', value, W_V)
        q = _xpos(q, downscale=False)
        k = _xpos(k, downscale=True)
        sim = jnp.einsum('bhnd,bhsd->bhns', q, k) * _decay_mask(L, H)[None]
        ret = jnp.einsum('bhns,bhsd->bhnd', sim, v)
        mu = ret.mean(axis=-1, keepdims=True)
        var = ret.var(axis=-1, keepdims=True)
        ret = (ret - mu) / jnp.sqrt(var + GN_EPS)
        ret = ret.transpose(0, 2, 1, 3).reshape(B, L, D)
        gate = jax.nn.silu(query @ g_w.T + g_b)
        return ret * gate @ out_w.T + out_b

    def _L0_ffn_ref(x, Wg, Wu, Wd, W1, W2):
        import jax, jax.numpy as jnp
        import numpy as np
        TOP_K = 2

        def _gelu(x):
            return jax.nn.gelu(x, approximate=False)
        B, S, D = x.shape
        E = Wu.shape[0]
        T = B * S
        xt = x.reshape(T, D)
        probs = jax.nn.softmax(xt @ Wg, axis=-1)
        topv, topi = jax.lax.top_k(probs, TOP_K)
        topv = topv / jnp.sum(topv, axis=-1, keepdims=True)
        cw = jnp.zeros((T, E), x.dtype).at[jnp.arange(T)[:, None], topi].set(topv)
        h = _gelu(jnp.einsum('td,edf->tef', xt, Wu))
        y = jnp.einsum('tef,efd->ted', h, Wd)
        moe = jnp.einsum('ted,te->td', y, cw)
        shared = _gelu(xt @ W1) @ W2
        return (shared + moe).reshape(B, S, D)
    x = x + jnp.tanh(g_xattn[0]) * _L0_xattn_ref(_layernorm(x, axis=-1), ctx_1024, ctx_1024, L0_xattn_W_Q, L0_xattn_W_K, L0_xattn_W_V, L0_xattn_g_w, L0_xattn_g_b, L0_xattn_out_w, L0_xattn_out_b)
    x = x + jnp.tanh(g_ffn[0]) * _L0_ffn_ref(_layernorm(x, axis=-1), L0_ffn_Wg, L0_ffn_Wu, L0_ffn_Wd, L0_ffn_W1, L0_ffn_W2)
    return x

_drawn_inputs = setup_inputs


def setup_inputs(seed=0):
    import zlib

    import numpy as np

    out = dict(_drawn_inputs(seed))
    spreads = {'L0_xattn_g_b': (0.0, 0.1), 'L0_xattn_out_b': (0.0, 0.1)}
    factors = {}
    for name, (base, spread) in spreads.items():
        noise = np.random.default_rng([zlib.crc32(name.encode()), seed]).standard_normal(out[name].shape)
        drawn = base * np.exp(spread * noise) if base else spread * noise
        out[name] = jnp.asarray(drawn.astype(out[name].dtype))
    for name, factor in factors.items():
        out[name] = (out[name] * factor).astype(out[name].dtype)
    return out
```

```python
from contextlib import ExitStack

import numpy as np

import concourse.bass as bass
from concourse import mybir

F32, F16 = mybir.dt.float32, mybir.dt.float16
I32, U32 = mybir.dt.int32, mybir.dt.uint32
ALU, ACT, AX = mybir.AluOpType, mybir.ActivationFunctionType, mybir.AxisListType

P = 128
B, L, D, H = 16, 256, 256, 16
HD = D // H
T = B * L // P
KC = D // P
E, F = 8, 512
FC = F // P
CPB = L // P
WS = 256.0
QS = 16.0
LN_EPS = 1e-5
GN_EPS = 1e-5 * (QS * QS) ** 2
CAP = T * P + P
NJ = 2 * T + E
NU = (E + 1) * 4
UP, DOWN = 0, 2 * (E + 1)
UNROLL = 4


class Idx:

    def __init__(self, c, i=None):
        self.c, self.i = c, i

    def at(self, n, k=0):
        v = n * self.c + k
        return v if self.i is None else self.i * (UNROLL * n) + v

    def per(self, m, n, k=0):
        v = n * (self.c // m) + k
        return v if self.i is None else self.i * (UNROLL // m * n) + v

    def slot(self, n):
        return self.c % n

    def __add__(self, k):
        return Idx(self.c + k, self.i)


def tables():
    f = np.float32
    half = HD // 2
    base = ((np.arange(0, HD, 2).astype(f) + f(0.4 * HD)) / f(1.4 * HD)).astype(np.float64)
    power = ((np.arange(L) - L // 2).astype(f) / f(512.0)).astype(np.float64)
    scale = base[None, :] ** power[:, None]
    inv_freq = (f(1.0) / f(10000.0) ** (np.arange(half).astype(f) / f(half))).astype(f)
    ang = (np.arange(L).astype(f)[:, None] * inv_freq[None, :]).astype(np.float64)
    g0 = np.linspace(np.log(1.0 / 32.0), np.log(1.0 / 512.0), H).astype(f)
    gamma = (f(1.0) - np.exp(g0)).astype(np.float64)
    local = np.arange(L) % P - P // 2
    cos, sin = [], []
    for sign in (1, -1):
        s = scale ** sign
        decay = gamma[None, :] ** (sign * local[:, None])
        amp = decay[:, :, None, None] * s[:, None, :, None] * (QS / WS)
        c = amp * np.cos(ang)[:, None, :, None] * np.ones((1, 1, 1, 2))
        n = amp * np.sin(ang)[:, None, :, None] * np.array([-1.0, 1.0])
        cos.append(c.reshape(L, D))
        sin.append(n.reshape(L, D))
    cos = np.concatenate(cos, 1).reshape(CPB, P, 2 * D).transpose(1, 0, 2)
    sin = np.concatenate(sin, 1).reshape(CPB, P, 2 * D).transpose(1, 0, 2)
    row = np.arange(P) // 64
    smask = np.zeros((P, H // 2, 2, HD))
    for g in range(H // 2):
        for a in range(2):
            smask[row == a, g, a, :] = gamma[2 * g + a] ** P
    tri = (np.arange(P)[None, :] >= np.arange(P)[:, None])
    before = (np.arange(P)[:, None] < np.arange(P)[None, :])
    e8 = np.arange(E)
    c32 = [cos.reshape(P, -1), sin.reshape(P, -1), smask.reshape(P, -1), tri, np.eye(P),
           np.tile(e8, (P, 1)), np.tile(e8 * CAP, (P, 1)), np.arange(P)[:, None],
           np.eye(P)[:, :2]]
    c16 = [np.eye(P), before, np.ones((P, P))]
    return (np.ascontiguousarray(np.concatenate(c32, 1).astype(np.float32)),
            np.ascontiguousarray(np.concatenate(c16, 1).astype(np.float16)))


C32 = dict(cos=CPB * 2 * D, sin=CPB * 2 * D, smask=D, tri=P, ident=P, e8=E, ebase=E, part=1, pick=2)
C16 = dict(ident=P, before=P, ones=P)
NQKVG = 4 * D
WA = dict(qkvg=KC * NQKVG, out=KC * D, gate=KC * E)


def cuts(widths):
    at, out = 0, {}
    for name, n in widths.items():
        out[name] = slice(at, at + n)
        at += n
    return out, at


def build(nc, x_d, ctx_d, wa_d, bias_d, gains_d, wf_d, c32_d, c16_d, out_d):
    cut32, n32 = cuts(C32)
    cut16, n16 = cuts(C16)
    cuta, na = cuts(WA)
    x_v = x_d.rearrange("b (c p) d -> (b c) p d", p=P)
    ctx_v = ctx_d.rearrange("b (c p) d -> (b c) p d", p=P)
    out_v = out_d.rearrange("b (c p) d -> (b c) p d", p=P)
    by_expert = nc.dram_tensor("rows_by_expert", [E * CAP, D], F32).ap()
    answers = nc.dram_tensor("answers", [NJ * P, D], F32).ap()

    with ExitStack() as ctx:
        def sb(name, shape, dt=F32, c=ctx):
            return c.enter_context(nc.sbuf_tensor(name, shape, dt))

        def ps(name, shape, dt=F32, c=ctx):
            return c.enter_context(nc.psum_tensor(name, shape, dt))

        def sem(name):
            return ctx.enter_context(nc.semaphore(name))

        def wait(eng, s, value):
            if not isinstance(value, int) or value > 0:
                eng.wait_ge(s, value)

        X = sb("X", [P, T, D])
        XT = sb("XT", [P, T, 2, KC, P], F16)
        WFH = sb("WFH", [P, NU, F], F16)
        WFL = sb("WFL", [P, NU, F], F16)
        c32 = sb("c32", [P, n32 - 2 * CPB * 2 * D])
        c16 = sb("c16", [P, n16], F16)
        gains = sb("gains", [P, 2])
        IDX = sb("IDX", [P, T, 2])
        POS = sb("POS", [P, T, 2])
        GAP = sb("GAP", [P, T])
        seen = sb("seen", [P, 2, E], F16)
        shift = CPB * 4 * D

        def const(name):
            c = cut32[name]
            return c32[:, c.start - shift:c.stop - shift]

        def const16(name):
            return c16[:, cut16[name]]

        with ExitStack() as c1:
            s1 = lambda name, shape, dt=F32: sb(name, shape, dt, c1)
            rot = s1("rot", [P, 2, CPB, 2 * D])
            WAH = s1("WAH", [P, na], F16)
            WAL = s1("WAL", [P, na], F16)
            biasw = s1("biasw", [P, 2 * D], F16)
            ctxb = s1("ctxb", [P, 2, D])
            stage = s1("stage", [P, 2, F])
            xn = s1("xn", [P, 2, D])
            xcs = s1("xcs", [P, 2, 2 * KC, P], F16)
            QKC = s1("QKC", [P, na - KC * NQKVG])
            swp = s1("swp", [P, 2 * D])
            q4 = s1("q4", [P, 2, H, 4, HD], F16)
            QT = s1("QT", [P, 2, H // 2, P], F16)
            KT = s1("KT", [P, H // 2, P], F16)
            sim = s1("sim", [P, H, P])
            V = s1("V", [P, 2, D])
            G = s1("G", [P, 2, D])
            rg = s1("rg", [P, 2, D])
            y = s1("y", [P, 2, D])
            ys = s1("ys", [P, 2, KC, P], F16)
            S4 = s1("S4", [P, 2, D], F16)
            VS = s1("VS", [P, 2, D], F16)
            xn2 = s1("xn2", [P, 4, D])
            st6 = s1("st6", [P, 2, 6])
            mv = s1("mv", [P, 2, 2, 2])
            NPW = H + 2
            pin = s1("pin", [P, 2, NPW])
            pout = s1("pout", [P, 2, NPW])
            pexp = s1("pexp", [P, NPW])
            nm = s1("nm", [P, 2, 2])
            m8 = s1("m8", [P, E])
            i8 = s1("i8", [P, E], U32)
            ix = s1("ix", [P, 2])
            one1 = s1("one1", [P, E])
            gap1 = s1("gap1", [P, 2])
            hot = s1("hot", [P, E], F16)
            rk = s1("rk", [P, E])
            junk = s1("junk", [P, 2, E])
            pos2 = s1("pos2", [P, 2])
            posi = s1("posi", [P, 4, 2], I32)
            vmean = s1("vmean", [P, KC, H])
            bstage = [a[0:2, :, :].rearrange("p a n -> p (a n)") for a in (y, rg)]
            wstage = sim[:, :, :].rearrange("p h n -> p (h n)")
            wstage2 = QKC[:, :]

            bT = ps("bT", [P, 2 * KC, P], F32, c1)
            bQK = ps("bQK", [P, 2 * D], F32, c1)
            bVG = ps("bVG", [P, 2 * D], F32, c1)
            bQT = ps("bQT", [P, H // 2, P], F16, c1)
            bS = [ps(f"bS{a}", [P, 4, P], F32, c1) for a in range(2)]
            bR = ps("bR", [P, 2 * D], F32, c1)
            bY = ps("bY", [P, 2 * D], F32, c1)
            sq = bR[:, D:2 * D]
            Sm = swp[:, 0:D]
            bSt = bQT[:, :, :].rearrange("p h n -> p (h n)").bitcast(F32)[:, 0:D]

            consts_in = sem("consts_in")
            wa_in = sem("wa_in")
            x_in = [sem(f"x_in{k}") for k in range(4)]
            ctx_in = [sem(f"ctx_in{k}") for k in range(2)]
            w_in = [sem(f"w_in{k}") for k in range(2)]
            prep_v, prep_a = sem("prep_v"), sem("prep_a")
            prep_p = sem("prep_p")
            stats_in = sem("stats_in")
            dve_chain = sem("dve_chain")
            aggr = sem("aggr")
            var_ready = sem("var_ready")
            rstd = sem("rstd")
            nm1, nm2 = sem("nm1"), sem("nm2")
            xn_done, xn2_done = sem("xn_done"), sem("xn2_done")
            t1 = sem("t1")
            xc_hi, xc_lo = sem("xc_hi"), sem("xc_lo")
            proj_qk, proj_vg = sem("proj_qk"), sem("proj_vg")
            rotc, rots, rotated = sem("rotc"), sem("rots"), sem("rotated")
            v_done, g_done = sem("v_done"), sem("g_done")
            hi4, lo4, dup4 = sem("hi4"), sem("lo4"), sem("dup4")
            qt, kt = sem("qt"), sem("kt")
            qt_out, kt_out = sem("qt_out"), sem("kt_out")
            scored, masked = sem("scored"), sem("masked")
            vs_hi, vs_done = sem("vs_hi"), sem("vs_done")
            stated, sm_done, s4_hi, s4_done = sem("stated"), sem("sm_done"), sem("s4_hi"), sem("s4_done")
            pv = sem("pv")
            sq_done, rg_done, y_done = sem("sq_done"), sem("rg_done"), sem("y_done")
            ss_done = sem("ss_done")
            yt, x2t = sem("yt"), sem("x2t")
            y_hi, y_lo, x2_hi, x2_lo = sem("y_hi"), sem("y_lo"), sem("x2_hi"), sem("x2_lo")
            outp, x2_done = sem("outp"), sem("x2_done")
            logit, hot_done, ranked, pos_done = sem("logit"), sem("hot_done"), sem("ranked"), sem("pos_done")
            top8, top_ix, ixf, one_done, seen_done = (
                sem("top8"), sem("top_ix"), sem("ixf"), sem("one_done"), sem("seen_done"))
            gap_done = sem("gap_done")
            rk_done, pos_f = sem("rk_done"), sem("pos_f")
            scat = [sem(f"scat{k}") for k in range(4)]
            w_scaled, w_hi, w_lo = sem("w_scaled"), sem("w_hi"), sem("w_lo")

            FIRST, LAST = -4, 37
            LOOP = (8, 28)
            LN1, XN, PROJ, ROT, SCORE, PV, YY, OUT, XN2, ROUTE, SCAT = (
                4, 3, 2, 1, 0, -1, -2, -3, -4, -5, -6)

            def steps(eng, step):
                def straight(s):
                    step(lambda k: Idx(s + k) if 0 <= s + k < T else None, s)
                for s in range(FIRST, LOOP[0]):
                    straight(s)
                with eng.Fori(0, (LOOP[1] - LOOP[0]) // UNROLL) as i:
                    for u in range(UNROLL):
                        step(lambda k, u=u: Idx(LOOP[0] + u + k, i), None)
                for s in range(LOOP[1], LAST + 1):
                    straight(s)

            def so_far(stages, tile_of, s):
                if s is not None:
                    return sum(min(max(s + k + 1, 0), T) for k in stages)
                z = [tile_of(k) for k in stages]
                return z[0].i * (UNROLL * len(z)) + sum(k.c + 1 for k in z)

            def unit_of(tile_of, s):
                if s is None:
                    return tile_of(LN1)
                return Idx(s - FIRST) if 0 <= s - FIRST < NU else None

            def stat_step(tile_of, s):
                if s is None:
                    return tile_of(LN1)
                return Idx(s - FIRST) if s - FIRST < T + 8 else None

            block = c1.enter_context(nc.Block())

            @block.sync
            def _(sp):
                sp.dma_start(wstage[:, 0:KC * NQKVG], wa_d[:, 0:KC * NQKVG]).then_inc(wa_in, 16)
                sp.dma_start(wstage2[:, 0:na - KC * NQKVG], wa_d[:, KC * NQKVG:na]).then_inc(wa_in, 16)
                sp.dma_start(c32[:, :], c32_d[:, shift:]).then_inc(consts_in, 16)
                sp.dma_start(c16[:, :], c16_d).then_inc(consts_in, 16)
                sp.dma_start(bstage[0], bias_d).then_inc(consts_in, 16)
                sp.dma_start(gains[:, :], gains_d).then_inc(consts_in, 16)
                sp.dma_start(rot[:, :, :, :].rearrange("p a c n -> p (a c n)"),
                             c32_d[:, 0:shift]).then_inc(consts_in, 16)

                def step(tile_of, s):
                    t = tile_of(LN1)
                    if t is not None:
                        wait(sp, x_in[t.slot(4)], t.per(4, 16))
                        sp.dma_start(X[:, bass.ds(t.at(1), 1), :], x_v[bass.ds(t.at(1), 1)].rearrange("o p d -> p o d")
                                     ).then_inc(x_in[t.slot(4)], 16)
                    u = unit_of(tile_of, s)
                    if u is not None:
                        wait(sp, w_lo, u.at(1, -1))
                        sp.dma_start(stage[:, u.slot(2), :], wf_d[bass.ds(u.at(1), 1)].rearrange("o p n -> p (o n)")
                                     ).then_inc(w_in[u.slot(2)], 16)
                    if t is not None:
                        wait(sp, t1, t.at(1, -1))
                        sp.dma_start(ctxb[:, t.slot(2), :], ctx_v[bass.ds(t.at(1), 1)].rearrange("o p d -> p (o d)")
                                     ).then_inc(ctx_in[t.slot(2)], 16)
                steps(sp, step)

            @block.gpsimd
            def _(pool):
                nc.gpsimd.memset(pexp[:, :], -0.5).then_inc(prep_p, 1)
                nc.gpsimd.memset(pin[:, :, :], 1.0).then_inc(prep_p, 1)
                pool.wait_ge(prep_p, 2)

                def step(tile_of, s):
                    n = stat_step(tile_of, s)
                    if n is not None and (n.i is not None or n.c >= 1):
                        m = n + -1
                        pool.wait_ge(var_ready, m.at(1, 1))
                        for k, used in ((XN, xn_done), (XN2, xn2_done)):
                            if tile_of(k - 2) is not None:
                                pool.wait_ge(used, tile_of(k - 2).at(1, 1))
                        nc.gpsimd.tensor_tensor(pout[:, m.slot(2), :], pin[:, m.slot(2), :], pexp[:, :],
                                                ALU.pow).then_inc(rstd, 1)
                    c = tile_of(SCAT)
                    if c is not None:
                        pool.wait_ge(pos_done, c.at(1, 1))
                        pool.wait_ge(xn2_done, c.at(1, 1))
                    t = tile_of(YY)
                    if t is not None:
                        pool.wait_ge(rg_done, t.at(1, 1))
                        pool.wait_ge(rstd, n.at(1))
                        wait(pool, yt, t.at(1, -1))
                        nc.gpsimd.tensor_tensor(
                            y[:, t.slot(2), :].rearrange("p (h e) -> p h e", h=H),
                            rg[:, t.slot(2), :].rearrange("p (h e) -> p h e", h=H),
                            pout[:, (n + -1).slot(2), 0:H].unsqueeze(2).to_broadcast([P, H, HD]),
                            ALU.mult).then_inc(y_done, 1)
                    t = c
                    if t is not None:
                        for k in range(2):
                            pool.indirect_dma_start(
                                by_expert[:, :], bass.IndirectOffsetOnAxis(ap=posi[:, t.slot(4), k:k + 1], axis=0),
                                xn2[:, t.slot(4), :], None).then_inc(scat[t.slot(4)], 16)
                    t = tile_of(ROT)
                    if t is not None and t.c % 2 == 0:
                        pool.wait_ge(vs_hi, t.per(2, 1, 1))
                        nc.gpsimd.tensor_tensor(VS[:, 1, :], V[:, t.slot(2), :], VS[:, 0, :], ALU.subtract
                                                ).then_inc(vs_done, 1)
                    u = unit_of(tile_of, s)
                    if u is not None:
                        pool.wait_ge(w_hi, u.at(1, 1))
                        nc.gpsimd.tensor_tensor(WFL[:, bass.ds(u.at(1), 1), :].rearrange("p o n -> p (o n)"),
                                                stage[:, u.slot(2), :],
                                                WFH[:, bass.ds(u.at(1), 1), :].rearrange("p o n -> p (o n)"),
                                                ALU.subtract).then_inc(w_lo, 1)
                steps(pool, step)
                for k in range(4):
                    pool.wait_ge(scat[k], 2 * 16 * (T // 4))

            @block.scalar
            def _(act):
                act.wait_ge(consts_in, 5 * 16)
                act.wait_ge(prep_v, 3)
                nc.scalar.activation(WAH[:, 0:KC * NQKVG], wstage[:, 0:KC * NQKVG], ACT.Copy).then_inc(prep_a, 1)
                nc.scalar.activation(WAH[:, KC * NQKVG:na], wstage2[:, 0:na - KC * NQKVG], ACT.Copy
                                     ).then_inc(prep_a, 1)
                nc.scalar.activation(gains[:, :], gains[:, :], ACT.Tanh).then_inc(prep_a, 1)

                def step(tile_of, s):
                    n = stat_step(tile_of, s)
                    t = tile_of(OUT)
                    r = tile_of(ROUTE)
                    if r is not None:
                        act.wait_ge(x2t, r.at(1, 1))
                    if t is not None:
                        act.wait_ge(yt, t.at(1, 1))
                        wait(act, outp, t.at(1))
                        nc.scalar.activation(ys[:, 0], bY[:, 0:D].rearrange("p (k n) -> p k n", k=KC),
                                             ACT.Copy).then_inc(y_hi, 1)
                    t = r
                    if t is not None:
                        nc.scalar.activation(XT[:, bass.ds(t.at(1), 1), 0].rearrange("p o k n -> p (o k n)"),
                                             bY[:, D:2 * D], ACT.Copy).then_inc(x2_hi, 1)
                    t = tile_of(PROJ)
                    if t is not None:
                        act.wait_ge(t1, t.at(1, 1))
                        wait(act, proj_vg, t.at(1))
                        nc.scalar.activation(xcs[:, 0], bT[:, :, :], ACT.Copy).then_inc(xc_hi, 1)
                    t = tile_of(SCORE)
                    if t is not None:
                        act.wait_ge(qt, t.at(1, 1))
                        wait(act, pv, t.at(1, -1))
                        nc.scalar.activation(QT[:, t.slot(2)], bQT[:, :, :], ACT.Copy).then_inc(qt_out, 1)
                    t = tile_of(PV)
                    if t is not None:
                        act.wait_ge(pv, t.at(1, 1))
                        wait(act, ss_done, t.at(1))
                        nc.scalar.activation(sq, bR[:, 0:D], ACT.Square).then_inc(sq_done, 1)
                    t = tile_of(ROT)
                    if t is not None:
                        act.wait_ge(proj_vg, t.at(1, 1))
                        wait(act, pv, t.at(1, -1))
                        nc.scalar.activation(V[:, t.slot(2), :], bVG[:, 0:D], ACT.Copy, scale=1.0 / WS
                                             ).then_inc(v_done, 1)
                        if t.c % 2 == 0:
                            act.wait_ge(v_done, t.at(1, 1))
                            wait(act, stated, t.per(2, 1))
                            nc.scalar.activation(VS[:, 0, :], V[:, t.slot(2), :], ACT.Copy).then_inc(vs_hi, 1)
                        wait(act, rg_done, t.at(1, -1))
                        nc.scalar.activation(G[:, t.slot(2), :], bVG[:, D:2 * D], ACT.Silu, scale=1.0 / WS
                                             ).then_inc(g_done, 1)
                        act.wait_ge(rotated, t.at(1, 1))
                        wait(act, kt, t.at(1))
                        if t.c % 2:
                            act.wait_ge(stated, t.per(2, 1, 1))
                        r = QKC[:, 0:2 * D].rearrange("p (a h e) -> p a h e", a=2, h=H)
                        for a, at in ((0, q4[:, 0, :, 0::2, :]), (1, q4[:, 1, :, 0:2, :])):
                            nc.scalar.activation(at, r[:, a].unsqueeze(2).to_broadcast([P, H, 2, HD]),
                                                 ACT.Copy).then_inc(hi4, 1)
                    t = tile_of(XN2)
                    if t is not None:
                        act.wait_ge(nm2, t.at(1, 1))
                        wait(act, scat[t.slot(4)], t.per(4, 32))
                        nc.scalar.activation(xn2[:, t.slot(4), :], X[:, bass.ds(t.at(1), 1), :].rearrange("p o d -> p (o d)"),
                                             ACT.Identity, bias=nm[:, 1, t.slot(2):t.slot(2) + 1],
                                             scale=pout[:, (n + -1).slot(2), H:H + 1]).then_inc(xn2_done, 1)
                    t = tile_of(XN)
                    if t is not None:
                        act.wait_ge(nm1, t.at(1, 1))
                        wait(act, t1, t.at(1, -1))
                        nc.scalar.activation(xn[:, t.slot(2), :], X[:, bass.ds(t.at(1), 1), :].rearrange("p o d -> p (o d)"),
                                             ACT.Identity, bias=nm[:, 0, t.slot(2):t.slot(2) + 1],
                                             scale=pout[:, (n + -1).slot(2), H + 1:H + 2]).then_inc(xn_done, 1)
                    u = unit_of(tile_of, s)
                    if u is not None:
                        act.wait_ge(w_in[u.slot(2)], u.per(2, 16, 16))
                        nc.scalar.activation(stage[:, u.slot(2), :], stage[:, u.slot(2), :], ACT.Copy, scale=WS
                                             ).then_inc(w_scaled, 1)
                    if u is not None:
                        act.wait_ge(w_scaled, u.at(1, 1))
                        nc.scalar.activation(WFH[:, bass.ds(u.at(1), 1), :].rearrange("p o n -> p (o n)"),
                                             stage[:, u.slot(2), :], ACT.Copy).then_inc(w_hi, 1)
                steps(act, step)

            @block.vector
            def _(dve):
                vec = nc.vector
                dve.wait_ge(wa_in, 2 * 16)
                wv = wstage[:, 0:KC * NQKVG].rearrange("p (k a h e) -> p k a h e", k=KC, a=4, h=H)
                for k in range(KC):
                    vec.tensor_reduce(vmean[:, k, :], wv[:, k, 2], AX.X, ALU.add).then_inc(prep_v, 1)
                dve.wait_ge(prep_v, 2)
                for k in range(KC):
                    vec.scalar_tensor_tensor(out=wv[:, k, 2], in0=vmean[:, k, :].unsqueeze(2).to_broadcast([P, H, HD]),
                                             scalar=-1.0 / HD, in1=wv[:, k, 2], op0=ALU.mult, op1=ALU.add
                                             ).then_inc(dve_chain, 1)
                dve.wait_ge(dve_chain, 2)
                vec.tensor_scalar(wstage[:, 0:KC * NQKVG], wstage[:, 0:KC * NQKVG], WS, None, ALU.mult
                                  ).then_inc(dve_chain, 1)
                vec.tensor_scalar(wstage2[:, 0:na - KC * NQKVG], wstage2[:, 0:na - KC * NQKVG], WS, None, ALU.mult
                                  ).then_inc(prep_v, 1)
                dve.wait_ge(consts_in, 5 * 16)
                vec.memset(biasw[:, :], 0.0).then_inc(dve_chain, 1)
                vec.memset(seen[:, :, :], 0.0).then_inc(dve_chain, 1)
                b0, b1 = bstage
                vec.tensor_scalar(b0, b0, WS, None, ALU.mult).then_inc(dve_chain, 1)
                dve.wait_ge(dve_chain, 6)
                vec.tensor_copy(biasw[0:2, :], b0).then_inc(dve_chain, 1)
                dve.wait_ge(dve_chain, 7)
                vec.tensor_tensor(b1, b0, biasw[0:2, :], ALU.subtract).then_inc(dve_chain, 1)
                dve.wait_ge(dve_chain, 8)
                vec.tensor_scalar(b1, b1, const("pick")[0:2, 1:2], None, ALU.mult).then_inc(dve_chain, 1)
                dve.wait_ge(dve_chain, 9)
                vec.scalar_tensor_tensor(out=biasw[0:2, :], in0=biasw[0:2, :], scalar=const("pick")[0:2, 0:1],
                                         in1=b1, op0=ALU.mult, op1=ALU.add).then_inc(dve_chain, 1)
                dve.wait_ge(prep_a, 2)
                vec.tensor_tensor(WAL[:, 0:KC * NQKVG], wstage[:, 0:KC * NQKVG], WAH[:, 0:KC * NQKVG], ALU.subtract
                                  ).then_inc(dve_chain, 1)
                vec.tensor_tensor(WAL[:, KC * NQKVG:na], wstage2[:, 0:na - KC * NQKVG], WAH[:, KC * NQKVG:na],
                                  ALU.subtract).then_inc(prep_v, 1)
                dve.wait_ge(prep_a, 3)
                vec.tensor_scalar(gains[:, :], gains[:, :], 1.0 / WS, None, ALU.mult).then_inc(dve_chain, 1)
                dve.wait_ge(dve_chain, 12)
                dve.wait_ge(prep_p, 2)

                def row(a, t):
                    return a[:, bass.ds(t.at(1), 1), :].rearrange("p o d -> p (o d)")

                def mask_round(t, r):
                    dve.wait_ge(scored, t.at(2, r + 1))
                    wait(dve, pv, t.at(1))
                    for a in range(2):
                        vec.tensor_tensor(sim[:, 8 * r + a:8 * r + 8:2, :], bS[a][:, :, :],
                                          const("tri").unsqueeze(1).to_broadcast([P, 4, P]), ALU.mult
                                          ).then_inc(masked, 1)

                def step(tile_of, s):
                    n = stat_step(tile_of, s)
                    if n is not None:
                        wait(dve, rstd, n.at(1, -1))
                    w = tile_of(ROT)
                    if w is not None:
                        wait(dve, hi4, w.at(2))
                        dve.wait_ge(proj_qk, w.at(1, 1))
                        c = w.c % 2
                        o = QKC[:, 0:2 * D]
                        vec.tensor_tensor(o, bQK[:, :], rot[:, 0, c, :], ALU.mult).then_inc(rotc, 1)
                        wait(dve, rotated, w.at(1))
                        z = tile_of(PV)
                        if z is not None:
                            dve.wait_ge(s4_done, z.per(2, 1, 1))
                        pair = bQK[:, :].rearrange("p (a two) -> p a two", two=2)[:, :, ::-1]
                        vec.tensor_tensor(swp[:, :].rearrange("p (a two) -> p a two", two=2), pair,
                                          rot[:, 1, c, :].rearrange("p (a two) -> p a two", two=2), ALU.mult
                                          ).then_inc(rots, 1)
                        dve.wait_ge(rots, w.at(1, 1))
                        vec.tensor_tensor(o, o, swp[:, :], ALU.add).then_inc(rotated, 1)
                    t = tile_of(PV)
                    if t is not None:
                        dve.wait_ge(pv, t.at(1, 1))
                        dve.wait_ge(sq_done, t.at(1, 1))
                        dve.wait_ge(g_done, t.at(1, 1))
                        wait(dve, y_done, t.at(1, -1))
                        vec.tensor_tensor(rg[:, t.slot(2), :], bR[:, 0:D], G[:, t.slot(2), :], ALU.mult
                                          ).then_inc(rg_done, 1)
                        vec.tensor_reduce(pin[:, n.slot(2), 0:H], sq.rearrange("p (h e) -> p h e", h=H),
                                          AX.X, ALU.add).then_inc(ss_done, 1)
                    t = tile_of(OUT)
                    if t is not None:
                        dve.wait_ge(y_hi, t.at(1, 1))
                        if tile_of(ROUTE) is not None:
                            dve.wait_ge(x2_hi, tile_of(ROUTE).at(1, 1))
                        vec.tensor_tensor(ys[:, 1], bY[:, 0:D].rearrange("p (k n) -> p k n", k=KC), ys[:, 0],
                                          ALU.subtract).then_inc(y_lo, 1)
                    t = tile_of(ROUTE)
                    if t is not None:
                        dve.wait_ge(x2_hi, t.at(1, 1))
                        o = XT[:, bass.ds(t.at(1), 1)]
                        vec.tensor_tensor(o[:, :, 1].rearrange("p o k n -> p (o k n)"), bY[:, D:2 * D],
                                          o[:, :, 0].rearrange("p o k n -> p (o k n)"), ALU.subtract
                                          ).then_inc(x2_lo, 1)
                    t = tile_of(PROJ)
                    if t is not None:
                        dve.wait_ge(xc_hi, t.at(1, 1))
                        vec.tensor_tensor(xcs[:, 1], bT[:, :, :], xcs[:, 0], ALU.subtract).then_inc(xc_lo, 1)
                    for k, (off, done, used) in enumerate(((XN, nm1, xn_done), (XN2, nm2, xn2_done))):
                        t = tile_of(off)
                        if t is not None:
                            dve.wait_ge(rstd, n.at(1))
                            wait(dve, used, t.at(1, -1))
                            vec.scalar_tensor_tensor(
                                out=nm[:, k, t.slot(2):t.slot(2) + 1], in0=mv[:, k, t.slot(2), 0:1], scalar=-1.0,
                                in1=pout[:, (n + -1).slot(2), H + 1 - k:H + 2 - k],
                                op0=ALU.mult, op1=ALU.mult).then_inc(done, 1)
                    t = tile_of(SCORE)
                    if t is not None:
                        dve.wait_ge(kt, t.at(1, 1))
                        wait(dve, scored, t.at(2))
                        vec.tensor_copy(KT[:, :, :], bQT[:, :, :]).then_inc(kt_out, 1)
                        mask_round(t, 0)
                        if t.c % 2 == 0:
                            dve.wait_ge(stated, t.per(2, 1, 1))
                            dve.wait_ge(rotated, tile_of(ROT).at(1, 1) if tile_of(ROT) is not None else T)
                            vec.tensor_tensor(Sm, bSt, const("smask"), ALU.mult).then_inc(sm_done, 1)
                            dve.wait_ge(sm_done, t.per(2, 1, 1))
                            wait(dve, pv, t.at(1))
                            vec.tensor_copy(S4[:, 0, :], Sm).then_inc(s4_hi, 1)
                            dve.wait_ge(s4_hi, t.per(2, 1, 1))
                            vec.tensor_tensor(S4[:, 1, :], Sm, S4[:, 0, :], ALU.subtract).then_inc(s4_done, 1)
                    if w is not None:
                        dve.wait_ge(hi4, w.at(2, 2))
                        rr = QKC[:, 0:2 * D].rearrange("p (a h e) -> p a h e", a=2, h=H)
                        for a, slot in ((0, 1), (1, 2)):
                            vec.tensor_tensor(q4[:, a, :, slot, :], rr[:, a], q4[:, a, :, 0, :], ALU.subtract
                                              ).then_inc(lo4, 1)
                        for a, slot in ((0, 1), (1, 2)):
                            dve.wait_ge(lo4, w.at(2, a + 1))
                            vec.tensor_copy(q4[:, a, :, 3, :], q4[:, a, :, slot, :]).then_inc(dup4, 1)
                    t = tile_of(OUT)
                    if t is not None:
                        dve.wait_ge(outp, t.at(1, 1))
                        if tile_of(ROUTE) is not None:
                            dve.wait_ge(logit, tile_of(ROUTE).at(1, 1))
                        vec.scalar_tensor_tensor(out=row(X, t), in0=bY[:, 0:D], scalar=gains[:, 0:1], in1=row(X, t),
                                                 op0=ALU.mult, op1=ALU.add).then_inc(x2_done, 1)
                    r = tile_of(ROUTE)
                    if r is not None:
                        if t is None:
                            dve.wait_ge(logit, r.at(1, 1))
                        vec.max(m8[:, :], bY[:, D:D + E]).then_inc(top8, 1)
                    if t is not None:
                        dve.wait_ge(x2_done, t.at(1, 1))
                    if r is not None:
                        dve.wait_ge(top8, r.at(1, 1))
                        vec.tensor_tensor(gap1[:, r.slot(2):r.slot(2) + 1], m8[:, 1:2], m8[:, 0:1], ALU.subtract
                                          ).then_inc(gap_done, 1)
                        vec.max_index(i8[:, :], m8[:, :], bY[:, D:D + E]).then_inc(top_ix, 1)
                    if t is not None:
                        vec.bn_stats(st6[:, 1, :], row(X, t)).then_inc(stats_in, 1)
                    if r is not None:
                        dve.wait_ge(top_ix, r.at(1, 1))
                        vec.tensor_copy(ix[:, :], i8[:, 0:2]).then_inc(ixf, 1)
                        dve.wait_ge(gap_done, r.at(1, 1))
                        vec.tensor_copy(GAP[:, bass.ds(r.at(1), 1)], gap1[:, r.slot(2):r.slot(2) + 1])
                        dve.wait_ge(ixf, r.at(1, 1))
                        vec.tensor_scalar(one1[:, :], const("e8"), ix[:, 0:1], None, ALU.is_equal
                                          ).then_inc(one_done, 1)
                        vec.tensor_copy(row(IDX, r), ix[:, :])
                    q = tile_of(LN1)
                    if q is not None:
                        dve.wait_ge(x_in[q.slot(4)], q.per(4, 16, 16))
                    if r is not None:
                        dve.wait_ge(one_done, r.at(1, 1))
                        vec.scalar_tensor_tensor(out=hot[:, :], in0=const("e8"), scalar=ix[:, 1:2], in1=one1[:, :],
                                                 op0=ALU.is_equal, op1=ALU.add).then_inc(hot_done, 1)
                    if q is not None:
                        vec.bn_stats(st6[:, 0, :], row(X, q)).then_inc(stats_in, 1)
                    z = tile_of(SCORE)
                    if z is not None:
                        mask_round(z, 1)
                    p = tile_of(PV)
                    if t is not None or q is not None:
                        dve.wait_ge(stats_in, so_far((LN1, OUT), tile_of, s))
                    if p is not None:
                        dve.wait_ge(ss_done, p.at(1, 1))
                        z = vec.tensor_scalar(pin[:, n.slot(2), 0:H], pin[:, n.slot(2), 0:H], 1.0 / HD, GN_EPS,
                                              ALU.mult, ALU.add)
                    if t is not None or q is not None:
                        for k, w_ in ((1, t), (0, q)):
                            if w_ is not None:
                                vec.bn_aggr(mv[:, k, w_.slot(2), :], st6[:, k, :]).then_inc(aggr, 1)
                        dve.wait_ge(aggr, so_far((LN1, OUT), tile_of, s))
                        for k, w_ in ((1, t), (0, q)):
                            if w_ is not None:
                                z = vec.tensor_scalar(pin[:, n.slot(2), H + 1 - k:H + 2 - k],
                                                      mv[:, k, w_.slot(2), 1:2], LN_EPS, None, ALU.add)
                    if not (p is None and t is None and q is None):
                        z.then_inc(var_ready, 1)
                    if r is not None:
                        dve.wait_ge(ranked, r.at(1, 1))
                        vec.tensor_tensor(rk[:, :], bY[:, D + E:D + 2 * E], const("ebase"), ALU.add
                                          ).then_inc(rk_done, 1)
                        wait(dve, seen_done, r.at(1))
                        vec.tensor_tensor(seen[:, (r + 1).slot(2), :], seen[:, r.slot(2), :], hot[:, :], ALU.add
                                          ).then_inc(seen_done, 1)
                        dve.wait_ge(rk_done, r.at(1, 1))
                        for k in range(2):
                            vec.scalar_tensor_tensor(out=junk[:, k, :], in0=const("e8"), scalar=ix[:, k:k + 1],
                                                     in1=rk[:, :], op0=ALU.is_equal, op1=ALU.mult,
                                                     accum_out=pos2[:, k:k + 1]).then_inc(pos_f, 1)
                        dve.wait_ge(pos_f, r.at(2, 2))
                        wait(dve, scat[r.slot(4)], r.per(4, 32))
                        vec.tensor_copy(posi[:, r.slot(4), :], pos2[:, :]).then_inc(pos_done, 1)
                        vec.tensor_copy(row(POS, r), pos2[:, :])

                steps(dve, step)

            @block.tensor
            def _(pe):
                mm = nc.tensor.matmul

                def three(out, parts, first=True, last=True):
                    ops = [(sh, mh) for sh, sl, mh, ml in parts] + \
                          [(sh, ml) for sh, sl, mh, ml in parts] + [(sl, mh) for sh, sl, mh, ml in parts]
                    for k, (st, mo) in enumerate(ops):
                        z = mm(out, st, mo, start=first and k == 0, stop=last and k == len(ops) - 1)
                    return z

                def wa(name, k, a=0, b=None):
                    n = (cuta[name].stop - cuta[name].start) // KC
                    lo = cuta[name].start + k * n
                    b = n if b is None else b
                    return WAH[:, lo + a:lo + b], WAL[:, lo + a:lo + b]

                pe.wait_ge(prep_v, 4)
                pe.wait_ge(dve_chain, 12)

                def slots_transposed(a, done):
                    src = q4[:, a].rearrange("p (g b) j e -> p g (b j e)", b=2)
                    for g in range(H // 2):
                        z = nc.tensor.transpose(bQT[:, g, :], src[:, g, :], const16("ident"))
                    z.then_inc(done, 1)

                def score_round(t, r):
                    wait(pe, masked, t.at(4, 2 * r))
                    for g in range(4):
                        for a in range(2):
                            q = slice(64 * a, 64 * a + 64)
                            z = mm(bS[a][:, g, :], KT[q, 4 * r + g, :], QT[q, t.slot(2), 4 * r + g, :],
                                   start=True, stop=True)
                    z.then_inc(scored, 1)

                def step(tile_of, s):
                    t, r = tile_of(OUT), tile_of(ROUTE)
                    if t is not None or r is not None:
                        a = tile_of(OUT - 1)
                        if a is not None:
                            pe.wait_ge(x2_done, a.at(1, 1))
                        a = tile_of(ROUTE - 1)
                        if a is not None:
                            pe.wait_ge(rk_done, a.at(1, 1))
                    if t is not None:
                        pe.wait_ge(y_done, t.at(1, 1))
                        for k in range(KC):
                            z = nc.tensor.transpose(bY[:, P * k:P * k + P], y[:, t.slot(2), P * k:P * k + P],
                                                    const("ident"))
                        z.then_inc(yt, 1)
                    if r is not None:
                        pe.wait_ge(xn2_done, r.at(1, 1))
                        for k in range(KC):
                            z = nc.tensor.transpose(bY[:, D + P * k:D + P * k + P], xn2[:, r.slot(4), P * k:P * k + P],
                                                    const("ident"))
                        z.then_inc(x2t, 1)
                    t = tile_of(PROJ)
                    if t is not None:
                        pe.wait_ge(xn_done, t.at(1, 1))
                        pe.wait_ge(ctx_in[t.slot(2)], t.per(2, 16, 16))
                        wait(pe, xc_lo, t.at(1))
                        for k in range(KC):
                            nc.tensor.transpose(bT[:, k, :], xn[:, t.slot(2), P * k:P * k + P], const("ident"))
                        for k in range(KC):
                            z = nc.tensor.transpose(bT[:, KC + k, :], ctxb[:, t.slot(2), P * k:P * k + P],
                                                    const("ident"))
                        z.then_inc(t1, 1)
                    w = tile_of(SCORE)
                    if w is not None:
                        pe.wait_ge(dup4, w.at(2, 2))
                        wait(pe, kt_out, w.at(1))
                        wait(pe, sm_done, (w + 1).per(2, 1))
                        slots_transposed(0, qt)
                    t = tile_of(PV)
                    if t is not None:
                        pe.wait_ge(masked, t.at(4, 4))
                        wait(pe, ss_done, t.at(1))
                        ops = []
                        if t.c % 2:
                            pe.wait_ge(s4_done, t.per(2, 1, 1))
                            ops += [(bR[:, 32 * g:32 * g + 32], QT[:, t.slot(2), g, :],
                                     S4[:, a, 32 * g:32 * g + 32]) for g in range(H // 2) for a in range(2)]
                        ops += [(bR[:, HD * h:HD * h + HD], sim[:, h, :], V[:, t.slot(2), HD * h:HD * h + HD])
                                for h in range(H)]
                        for k, (o, st, mo) in enumerate(ops):
                            z = mm(o, st, mo, start=k == 0, stop=k == len(ops) - 1)
                        z.then_inc(pv, 1)
                    if w is not None:
                        pe.wait_ge(qt_out, w.at(1, 1))
                        slots_transposed(1, kt)
                    t = tile_of(PROJ)
                    if t is not None:
                        pe.wait_ge(xc_lo, t.at(1, 1))
                        wait(pe, rots, t.at(1))
                        three(bQK[:, 0:D], [(xcs[:, 0, k], xcs[:, 1, k], *wa("qkvg", k, 0, D)) for k in range(KC)])
                        three(bQK[:, D:2 * D], [(xcs[:, 0, KC + k], xcs[:, 1, KC + k], *wa("qkvg", k, D, 2 * D))
                                                for k in range(KC)]).then_inc(proj_qk, 1)
                    if w is not None:
                        pe.wait_ge(kt_out, w.at(1, 1))
                        if w.c % 2 == 0:
                            pe.wait_ge(vs_done, w.per(2, 1, 1))
                            kk = q4[:, 1].rearrange("p (g b) j e -> p g (b j e)", b=2)
                            for g in range(H // 2):
                                for a in range(2):
                                    z = mm(bSt[:, 32 * g:32 * g + 32], kk[:, g, :],
                                           VS[:, a, 32 * g:32 * g + 32], start=a == 0, stop=a == 1)
                            z.then_inc(stated, 1)
                        score_round(w, 0)
                    t = tile_of(OUT)
                    if t is not None:
                        pe.wait_ge(y_lo, t.at(1, 1))
                        if tile_of(ROUTE) is not None:
                            pe.wait_ge(x2_lo, tile_of(ROUTE).at(1, 1))
                        three(bY[:, 0:D], [(ys[:, 0, k], ys[:, 1, k], *wa("out", k)) for k in range(KC)], last=False)
                        mm(bY[:, 0:D], const16("ones"), biasw[:, D:2 * D], start=False, stop=True).then_inc(outp, 1)
                    t = tile_of(ROUTE)
                    if t is not None:
                        pe.wait_ge(x2_lo, t.at(1, 1))
                        xt = XT[:, bass.ds(t.at(1), 1)]
                        three(bY[:, D:D + E], [(xt[:, :, 0, k].rearrange("p o n -> p (o n)"),
                                                xt[:, :, 1, k].rearrange("p o n -> p (o n)"), *wa("gate", k))
                                               for k in range(KC)]).then_inc(logit, 1)
                    if w is not None:
                        score_round(w, 1)
                    t = tile_of(PROJ)
                    if t is not None:
                        wait(pe, g_done, t.at(1))
                        three(bVG[:, 0:D], [(xcs[:, 0, KC + k], xcs[:, 1, KC + k], *wa("qkvg", k, 2 * D, 3 * D))
                                            for k in range(KC)])
                        three(bVG[:, D:2 * D], [(xcs[:, 0, k], xcs[:, 1, k], *wa("qkvg", k, 3 * D, 4 * D))
                                                for k in range(KC)], last=False)
                        mm(bVG[:, D:2 * D], const16("ones"), biasw[:, 0:D], start=False, stop=True
                           ).then_inc(proj_vg, 1)
                    t = tile_of(ROUTE)
                    if t is not None:
                        pe.wait_ge(hot_done, t.at(1, 1))
                        wait(pe, seen_done, t.at(1))
                        mm(bY[:, D + E:D + 2 * E], const16("before"), hot[:, :], start=True, stop=False)
                        mm(bY[:, D + E:D + 2 * E], const16("ones"), seen[:, t.slot(2), :], start=False, stop=True
                           ).then_inc(ranked, 1)
                steps(pe, step)

        NS = 4
        E0, E1 = NS, NS + NJ
        NP = T + NJ
        with ExitStack() as c2:
            s2 = lambda name, shape, dt=F32: sb(name, shape, dt, c2)
            xg = s2("xg", [P, 4, D])
            xgs = s2("xgs", [P, 2, 2, KC, P], F16)
            g = s2("g", [P, 2, F])
            hs = s2("hs", [P, 2, 2, FC, P], F16)
            yb = s2("yb", [P, 4, D])
            Y12 = s2("Y12", [P, 4, 2, D])
            zero = s2("zero", [P, D])
            nt, cum, cs, delta, oneE, junk2 = (s2(n, [P, E]) for n in ("nt", "cum", "cs", "delta", "oneE", "junk2"))
            nti = s2("nti", [P, E], I32)
            zrow = s2("zrow", [P, E], I32)
            tj = s2("tj", [P, 5])
            which = s2("which", [P, 2 * T, E])
            ints = s2("ints", [P, 2 * NJ], I32)
            posk = s2("posk", [P, T, 2], I32)
            posg = s2("posg", [P, 4, 2], I32)
            ex = s2("ex", [P, T])
            den = s2("den", [P, T])
            offs = s2("offs", [P, 2 * T])
            a12 = s2("a12", [P, T, 2])

            uA = [ps(f"uA{k}", [P, F], F32, c2) for k in range(2)]
            hT = [ps(f"hT{k}", [P, FC, P], F32, c2) for k in range(2)]
            yD = [ps(f"yD{k}", [P, D], F32, c2) for k in range(2)]
            xg_t = ps("xg_t", [P, KC, P], F32, c2)
            cnt = ps("cnt", [P, E], F32, c2)

            counted, tiles_known = sem("counted"), sem("tiles_known")
            ch = sem("ch")
            rows_known, zeroed, zfill = sem("rows_known"), sem("zeroed"), sem("zfill")
            zrows_known, turned = sem("zrows_known"), sem("turned")
            ex_done, mix_done, posk_done = sem("ex_done"), sem("mix_done"), sem("posk_done")
            xg_in = [sem(f"xg_in{k}") for k in range(4)]
            xgt, xg_hi, xg_lo = sem("xgt"), sem("xg_hi"), sem("xg_lo")
            up_done, gelu_done, ht_done = sem("up_done"), sem("gelu_done"), sem("ht_done")
            h_hi, h_lo, down_done = sem("h_hi"), sem("h_lo"), sem("down_done")
            y_out, s_out = sem("y_out"), sem("s_out")
            stored = [sem(f"stored{k}") for k in range(4)]
            posg_done = sem("posg_done")
            y12 = [sem(f"y12_{k}") for k in range(4)]
            mix1, mixed = sem("mix1"), sem("mixed")
            written = sem("written")

            LOAD, XTR, UPS, HTR, DNS = 4, 2, 1, 0, -1
            CF = E1 + 1
            STEPS = (-4, CF + T)
            LOOPS = ((8, 72), (E1 + 4, E1 + 24))

            def steps2(eng, step, between=lambda: None):
                def kind(p):
                    return "routed" if E0 <= p < E1 else "shared"

                def straight(s):
                    step(lambda k: (Idx(s + k), kind(s + k)) if 0 <= s + k < NP else (None, None),
                         Idx(s - CF) if 0 <= s - CF < T else None)
                at = STEPS[0]
                for a, b in LOOPS:
                    for s in range(at, a):
                        straight(s)
                        if s == LOOPS[0][1]:
                            between()
                    with eng.Fori(0, (b - a) // UNROLL) as i:
                        for u in range(UNROLL):
                            step(lambda k, u=u: (Idx(a + u + k, i), kind(a + k)),
                                 Idx(a + u - CF, i) if a > CF else None)
                    at = b
                for s in range(at, STEPS[1]):
                    straight(s)

            def routed(p):
                return p + -E0

            def shared(p, first):
                return p if first else p + -NJ

            def token_tile(p):
                return shared(p, p.i is None and p.c < E0)

            block = c2.enter_context(nc.Block())

            @block.sync
            def _(sp):
                sp.wait_ge(rows_known, 1)
                sp.wait_ge(zfill, E * 16)

                def step(at, m):
                    p, kind = at(LOAD)
                    if kind == "routed":
                        j = routed(p)
                        wait(sp, xgt, j.at(1, -3))
                        r = sp.value_load(ints[0:1, bass.ds(j.at(1), 1)], min_val=0, max_val=E * CAP - P)
                        sp.dma_start(xg[:, j.slot(4), :], by_expert[bass.ds(r, P), :]).then_inc(xg_in[j.slot(4)], 16)
                    p, kind = at(DNS)
                    if kind == "routed":
                        j = routed(p)
                        sp.wait_ge(y_out, j.at(1, 1))
                        sp.dma_start(answers[bass.ds(j.at(P), P), :], yb[:, j.slot(4), :]
                                     ).then_inc(stored[j.slot(4)], 16)
                    if m is not None:
                        sp.wait_ge(mixed, m.at(1, 1))
                        sp.dma_start(out_v[bass.ds(m.at(1), 1)].rearrange("o p d -> p (o d)"),
                                     X[:, bass.ds(m.at(1), 1), :].rearrange("p o d -> p (o d)")
                                     ).then_inc(written, 16)
                steps2(sp, step)
                sp.wait_ge(written, T * 16)

            @block.gpsimd
            def _(pool):
                nc.gpsimd.memset(zero[:, :], 0.0).then_inc(zeroed, 1)
                pool.wait_ge(zrows_known, 1)
                pool.wait_ge(zeroed, 1)
                for e in range(E):
                    pool.indirect_dma_start(by_expert[:, :], bass.IndirectOffsetOnAxis(ap=zrow[:, e:e + 1], axis=0),
                                            zero[:, :], None).then_inc(zfill, 16)
                pool.wait_ge(posk_done, 1)
                for k in range(4):
                    pool.wait_ge(stored[k], NJ // 4 * 16)

                def place(m):
                    wait(pool, mixed, m.at(1, -3))
                    wait(pool, posg_done, m.at(1))
                    nc.gpsimd.tensor_copy(posg[:, m.slot(4), :],
                                          posk[:, bass.ds(m.at(1), 1), :].rearrange("p o d -> p (o d)")
                                          ).then_inc(posg_done, 1)

                def gather(m):
                    for a in range(2):
                        pool.indirect_dma_start(Y12[:, m.slot(4), a, :], None, answers[:, :],
                                                bass.IndirectOffsetOnAxis(ap=posg[:, m.slot(4), a:a + 1], axis=0)
                                                ).then_inc(y12[m.slot(4)], 16)
                for k in range(4):
                    place(Idx(k))
                    if k:
                        gather(Idx(k - 1))
                with pool.Fori(0, T // UNROLL - 1) as i:
                    for k in range(4):
                        place(Idx(4 + k, i))
                        gather(Idx(3 + k, i))
                pool.wait_ge(posg_done, T)
                gather(Idx(T - 1))

            @block.scalar
            def _(act):
                nc.scalar.activation(ex[:, :], GAP[:, :], ACT.Exp, scale=1.0 / WS).then_inc(ex_done, 1)

                def step(at, m):
                    p, kind = at(XTR)
                    if kind == "routed":
                        j = routed(p)
                        act.wait_ge(xgt, j.at(1, 1))
                        wait(act, up_done, p.at(1, -1))
                        nc.scalar.activation(xgs[:, j.slot(2), 0], xg_t[:, :, :], ACT.Copy).then_inc(xg_hi, 1)
                    p, kind = at(UPS)
                    if p is not None:
                        act.wait_ge(up_done, p.at(1, 1))
                        wait(act, ht_done, p.at(1, -1))
                        nc.scalar.activation(g[:, p.slot(2), :], uA[p.slot(2)][:, :], ACT.Gelu, scale=1.0 / WS
                                             ).then_inc(gelu_done, 1)
                    p, kind = at(HTR)
                    if p is not None:
                        act.wait_ge(ht_done, p.at(1, 1))
                        wait(act, down_done, p.at(1, -1))
                        nc.scalar.activation(hs[:, p.slot(2), 0], hT[p.slot(2)][:, :, :], ACT.Copy).then_inc(h_hi, 1)
                    p, kind = at(DNS)
                    if kind == "routed":
                        j = routed(p)
                        act.wait_ge(down_done, p.at(1, 1))
                        wait(act, stored[j.slot(4)], j.per(4, 16))
                        nc.scalar.activation(yb[:, j.slot(4), :], yD[p.slot(2)][:, :], ACT.Copy).then_inc(y_out, 1)
                steps2(act, step)

            @block.vector
            def _(dve):
                vec = nc.vector
                n = [0]

                def link(op):
                    n[0] += 1
                    op.then_inc(ch, 1)
                    dve.wait_ge(ch, n[0])
                part = const("part")
                dve.wait_ge(counted, 1)
                vec.scalar_tensor_tensor(out=zrow[:, :], in0=cnt[:, :], scalar=part, in1=const("ebase"),
                                         op0=ALU.add, op1=ALU.add).then_inc(zrows_known, 1)
                link(vec.tensor_scalar(nti[:, :], cnt[:, :], float(P - 1), None, ALU.add))
                link(vec.tensor_scalar(nti[:, :], nti[:, :], 7, None, ALU.arith_shift_right))
                link(vec.tensor_copy(nt[:, :], nti[:, :]))
                link(vec.memset(oneE[:, :], 1.0))
                link(vec.tensor_tensor_scan(out=cum[:, :], data0=oneE[:, :], data1=nt[:, :], initial=0.0,
                                            op0=ALU.mult, op1=ALU.add))
                link(vec.tensor_tensor(cs[:, :], cum[:, :], nt[:, :], ALU.subtract))
                link(vec.scalar_tensor_tensor(out=delta[:, :], in0=cs[:, :], scalar=float(P), in1=const("ebase"),
                                              op0=ALU.mult, op1=ALU.subtract))
                link(vec.scalar_tensor_tensor(out=junk2[:, :], in0=cum[:, :], scalar=part, in1=oneE[:, :],
                                              op0=ALU.is_le, op1=ALU.mult, accum_out=tj[:, 0:1]))
                link(vec.scalar_tensor_tensor(out=junk2[:, :], in0=const("e8"), scalar=tj[:, 0:1], in1=delta[:, :],
                                              op0=ALU.is_equal, op1=ALU.mult, accum_out=tj[:, 1:2]))
                link(vec.scalar_tensor_tensor(out=tj[:, 2:3], in0=part, scalar=float(P), in1=tj[:, 1:2],
                                              op0=ALU.mult, op1=ALU.subtract))
                link(vec.scalar_tensor_tensor(out=tj[:, 3:4], in0=tj[:, 0:1], scalar=float(E), in1=tj[:, 2:3],
                                              op0=ALU.is_lt, op1=ALU.mult))
                vec.scalar_tensor_tensor(out=tj[:, 4:5], in0=tj[:, 0:1], scalar=float(E), in1=tj[:, 0:1],
                                         op0=ALU.is_lt, op1=ALU.mult).then_inc(tiles_known, 1)
                dve.wait_ge(turned, 1)
                vec.tensor_copy(ints[0:1, :], xg_t[0:1, :, :].rearrange("p k n -> p (k n)")[:, 0:2 * NJ]
                                ).then_inc(rows_known, 1)

                def answers_known():
                    link(vec.tensor_tensor(which[:, :, :], const("e8").unsqueeze(1).to_broadcast([P, 2 * T, E]),
                                           IDX[:, :, :].rearrange("p t k -> p (t k)").unsqueeze(2)
                                           .to_broadcast([P, 2 * T, E]), ALU.is_equal))
                    link(vec.tensor_tensor(which[:, :, :], which[:, :, :],
                                           delta[:, :].unsqueeze(1).to_broadcast([P, 2 * T, E]), ALU.mult))
                    link(vec.tensor_reduce(offs[:, :], which[:, :, :], AX.X, ALU.add))
                    vec.tensor_tensor(posk[:, :, :].rearrange("p t k -> p (t k)"),
                                      POS[:, :, :].rearrange("p t k -> p (t k)"), offs[:, :], ALU.add
                                      ).then_inc(posk_done, 1)
                    dve.wait_ge(ex_done, 1)
                    link(vec.tensor_scalar(den[:, :], ex[:, :], 1.0, None, ALU.add))
                    link(vec.reciprocal(den[:, :], den[:, :]))
                    link(vec.tensor_scalar(a12[:, :, 0], den[:, :], gains[:, 1:2], None, ALU.mult))
                    link(vec.tensor_tensor(a12[:, :, 1], ex[:, :], a12[:, :, 0], ALU.mult))

                def row(a, t):
                    return a[:, bass.ds(t.at(1), 1), :].rearrange("p o d -> p (o d)")

                def step(at, m):
                    p, kind = at(XTR)
                    if kind == "routed":
                        j = routed(p)
                        dve.wait_ge(xg_hi, j.at(1, 1))
                        vec.tensor_tensor(xgs[:, j.slot(2), 1], xg_t[:, :, :], xgs[:, j.slot(2), 0], ALU.subtract
                                          ).then_inc(xg_lo, 1)
                    p, kind = at(HTR)
                    if p is not None:
                        dve.wait_ge(h_hi, p.at(1, 1))
                        vec.tensor_tensor(hs[:, p.slot(2), 1], hT[p.slot(2)][:, :, :], hs[:, p.slot(2), 0],
                                          ALU.subtract).then_inc(h_lo, 1)
                    p, kind = at(DNS)
                    if kind == "shared":
                        t = token_tile(p)
                        dve.wait_ge(down_done, p.at(1, 1))
                        vec.scalar_tensor_tensor(out=row(X, t), in0=yD[p.slot(2)][:, :], scalar=gains[:, 1:2],
                                                 in1=row(X, t), op0=ALU.mult, op1=ALU.add).then_inc(s_out, 1)
                    if m is not None:
                        dve.wait_ge(y12[m.slot(4)], m.per(4, 32, 32))
                        dve.wait_ge(s_out, m.at(1, 1))
                        for k, done in ((0, mix1), (1, mixed)):
                            if k:
                                dve.wait_ge(mix1, m.at(1, 1))
                            vec.scalar_tensor_tensor(
                                out=row(X, m), in0=Y12[:, m.slot(4), k, :],
                                scalar=a12[:, bass.ds(m.at(1), 1), k], in1=row(X, m),
                                op0=ALU.mult, op1=ALU.add).then_inc(done, 1)
                steps2(dve, step, answers_known)

            @block.tensor
            def _(pe):
                mm = nc.tensor.matmul
                mm(cnt[:, :], const16("ones"), seen[:, T % 2, :], start=True, stop=True).then_inc(counted, 1)

                def turn():
                    pe.wait_ge(tiles_known, 1)
                    row = xg_t[0:1, :, :].rearrange("p k n -> p (k n)")
                    for k in range(2):
                        z = mm(row[:, k * NJ:k * NJ + NJ], tj[0:NJ, 3 + k:4 + k], const("ident")[0:NJ, 0:NJ],
                               start=True, stop=True)
                    z.then_inc(turned, 1)
                turn()

                def expert(p, kind):
                    if kind == "shared":
                        return 2 * E
                    j = routed(p)
                    e = pe.value_load(ints[0:1, bass.ds(j.at(1, NJ), 1)], min_val=0, max_val=E - 1)
                    return e * 2

                def unit(a, u):
                    return a[:, bass.ds(u, 1), :].rearrange("p o n -> p (o n)")

                def step(at, m):
                    p, kind = at(XTR)
                    if kind == "routed":
                        j = routed(p)
                        if j.c == 0 and j.i is None:
                            pe.wait_ge(rows_known, 1)
                        pe.wait_ge(xg_in[j.slot(4)], j.per(4, 16, 16))
                        wait(pe, xg_lo, j.at(1))
                        for k in range(KC):
                            z = nc.tensor.transpose(xg_t[:, k, :], xg[:, j.slot(4), P * k:P * k + P], const("ident"))
                        z.then_inc(xgt, 1)
                    p, kind = at(UPS)
                    if p is not None:
                        e = expert(p, kind)
                        wait(pe, gelu_done, p.at(1, -1))
                        if kind == "routed":
                            j = routed(p)
                            pe.wait_ge(xg_lo, j.at(1, 1))
                            xh, xl = ([xgs[:, j.slot(2), a, k, :] for k in range(KC)] for a in range(2))
                        else:
                            t = token_tile(p)
                            xt = XT[:, bass.ds(t.at(1), 1)]
                            xh, xl = ([xt[:, :, a, k].rearrange("p o n -> p (o n)") for k in range(KC)]
                                      for a in range(2))
                        for k in range(KC):
                            wh, wl = unit(WFH, e + (UP + k)), unit(WFL, e + (UP + k))
                            for q, (st, mo) in enumerate(((xh[k], wh), (xh[k], wl), (xl[k], wh))):
                                z = mm(uA[p.slot(2)][:, :], st, mo, start=k == 0 and q == 0,
                                       stop=k == KC - 1 and q == 2)
                        z.then_inc(up_done, 1)
                    p, kind = at(HTR)
                    if p is not None:
                        pe.wait_ge(gelu_done, p.at(1, 1))
                        wait(pe, h_lo, p.at(1, -1))
                        for k in range(FC):
                            z = nc.tensor.transpose(hT[p.slot(2)][:, k, :], g[:, p.slot(2), P * k:P * k + P],
                                                    const("ident"))
                        z.then_inc(ht_done, 1)
                    p, kind = at(DNS)
                    if p is not None:
                        e = expert(p, kind)
                        pe.wait_ge(h_lo, p.at(1, 1))
                        q, was = at(DNS - 2)
                        if was == "routed":
                            pe.wait_ge(y_out, routed(q).at(1, 1))
                        elif was == "shared":
                            pe.wait_ge(s_out, token_tile(q).at(1, 1))
                        for k in range(FC):
                            u, c = e + (DOWN + k // 2), slice(D * (k % 2), D * (k % 2) + D)
                            wh, wl = unit(WFH, u)[:, c], unit(WFL, u)[:, c]
                            hh, hl = (hs[:, p.slot(2), a, k, :] for a in range(2))
                            for q_, (st, mo) in enumerate(((hh, wh), (hh, wl), (hl, wh))):
                                z = mm(yD[p.slot(2)][:, :], st, mo, start=k == 0 and q_ == 0,
                                       stop=k == FC - 1 and q_ == 2)
                        z.then_inc(down_done, 1)
                steps2(pe, step)


def kernel(x, ctx_1024, g_xattn, g_ffn, L0_xattn_W_Q, L0_xattn_W_K, L0_xattn_W_V, L0_xattn_g_w, L0_xattn_g_b,
           L0_xattn_out_w, L0_xattn_out_b, L0_ffn_Wg, L0_ffn_Wu, L0_ffn_Wd, L0_ffn_W1, L0_ffn_W2):
    import concourse.bacc as bacc
    from concourse.bass_utils import run_bass_kernel_spmd

    def heads(w):
        return np.asarray(w).transpose(1, 0, 2).reshape(D, D)

    def rows(w):
        w = np.asarray(w)
        return w.reshape(KC, P, w.shape[1]).transpose(1, 0, 2).reshape(P, -1)

    qkvg = np.concatenate([heads(L0_xattn_W_Q), heads(L0_xattn_W_K), heads(L0_xattn_W_V),
                           np.asarray(L0_xattn_g_w).T], axis=1)
    wa = np.concatenate([rows(qkvg), rows(np.asarray(L0_xattn_out_w).T), rows(L0_ffn_Wg)], axis=1)
    bias = np.concatenate([np.asarray(L0_xattn_g_b), np.asarray(L0_xattn_out_b)])
    bias = np.stack([bias, bias])
    gains = np.stack([np.concatenate([np.asarray(g_xattn), np.asarray(g_ffn)])] * P)
    ups = np.concatenate([np.asarray(L0_ffn_Wu).reshape(2 * E, P, F), np.asarray(L0_ffn_W1).reshape(2, P, F)])
    downs = np.concatenate([np.asarray(L0_ffn_Wd).reshape(2 * E, 2, P, D), np.asarray(L0_ffn_W2).reshape(2, 2, P, D)])
    wf = np.concatenate([ups, downs.transpose(0, 2, 1, 3).reshape(2 * E + 2, P, F)])
    c32, c16 = tables()
    arrays = dict(x=x, ctx=ctx_1024, wa=wa, bias=bias, gains=gains, wf=wf, c32=c32, c16=c16)
    arrays = {f"{k}_in": np.ascontiguousarray(np.asarray(v)) for k, v in arrays.items()}

    nc = bacc.Bacc("TRN2", target_bir_lowering=False, num_devices=1)
    args = [nc.dram_tensor(n, a.shape, mybir.dt.from_np(a.dtype), kind="ExternalInput").ap()
            for n, a in arrays.items()]
    out = nc.dram_tensor("out", (B, L, D), F32, kind="ExternalOutput").ap()
    build(nc, *args, out)
    r = run_bass_kernel_spmd(nc, [arrays], core_ids=[0])
    return r.results[0]["out"]
```

```python
from contextlib import ExitStack

import numpy as np

import concourse.bass as bass
from concourse import mybir

F32, F16 = mybir.dt.float32, mybir.dt.float16
I32, U32 = mybir.dt.int32, mybir.dt.uint32
ALU, ACT, AX = mybir.AluOpType, mybir.ActivationFunctionType, mybir.AxisListType

P = 128
B, L, D, H = 16, 256, 256, 16
HD = D // H
T = B * L // P
KC = D // P
E, F = 8, 512
FC = F // P
CPB = L // P
WS = 256.0
QS = 16.0
LN_EPS = 1e-5
GN_EPS = 1e-5 * (QS * QS) ** 2
CAP = T * P + P
NJ = 2 * T + E
NU = (E + 1) * 4
UP, DOWN = 0, 2 * (E + 1)
UNROLL = 4


class Idx:

    def __init__(self, c, i=None):
        self.c, self.i = c, i

    def at(self, n, k=0):
        v = n * self.c + k
        return v if self.i is None else self.i * (UNROLL * n) + v

    def per(self, m, n, k=0):
        v = n * (self.c // m) + k
        return v if self.i is None else self.i * (UNROLL // m * n) + v

    def slot(self, n):
        return self.c % n

    def __add__(self, k):
        return Idx(self.c + k, self.i)


def tables():
    f = np.float32
    half = HD // 2
    base = ((np.arange(0, HD, 2).astype(f) + f(0.4 * HD)) / f(1.4 * HD)).astype(np.float64)
    power = ((np.arange(L) - L // 2).astype(f) / f(512.0)).astype(np.float64)
    scale = base[None, :] ** power[:, None]
    inv_freq = (f(1.0) / f(10000.0) ** (np.arange(half).astype(f) / f(half))).astype(f)
    ang = (np.arange(L).astype(f)[:, None] * inv_freq[None, :]).astype(np.float64)
    g0 = np.linspace(np.log(1.0 / 32.0), np.log(1.0 / 512.0), H).astype(f)
    gamma = (f(1.0) - np.exp(g0)).astype(np.float64)
    local = np.arange(L) % P - P // 2
    cos, sin = [], []
    for sign in (1, -1):
        s = scale ** sign
        decay = gamma[None, :] ** (sign * local[:, None])
        amp = decay[:, :, None, None] * s[:, None, :, None] * (QS / WS)
        c = amp * np.cos(ang)[:, None, :, None] * np.ones((1, 1, 1, 2))
        n = amp * np.sin(ang)[:, None, :, None] * np.array([-1.0, 1.0])
        cos.append(c.reshape(L, D))
        sin.append(n.reshape(L, D))
    cos = np.concatenate(cos, 1).reshape(CPB, P, 2 * D).transpose(1, 0, 2)
    sin = np.concatenate(sin, 1).reshape(CPB, P, 2 * D).transpose(1, 0, 2)
    row = np.arange(P) // 64
    smask = np.zeros((P, H // 2, 2, HD))
    for g in range(H // 2):
        for a in range(2):
            smask[row == a, g, a, :] = gamma[2 * g + a] ** P
    tri = (np.arange(P)[None, :] >= np.arange(P)[:, None])
    before = (np.arange(P)[:, None] < np.arange(P)[None, :])
    e8 = np.arange(E)
    c32 = [cos.reshape(P, -1), sin.reshape(P, -1), smask.reshape(P, -1), tri, np.eye(P),
           np.tile(e8, (P, 1)), np.tile(e8 * CAP, (P, 1)), np.arange(P)[:, None],
           np.eye(P)[:, :2]]
    c16 = [np.eye(P), before, np.ones((P, P))]
    return (np.ascontiguousarray(np.concatenate(c32, 1).astype(np.float32)),
            np.ascontiguousarray(np.concatenate(c16, 1).astype(np.float16)))


C32 = dict(cos=CPB * 2 * D, sin=CPB * 2 * D, smask=D, tri=P, ident=P, e8=E, ebase=E, part=1, pick=2)
C16 = dict(ident=P, before=P, ones=P)
NQKVG = 4 * D
WA = dict(qkvg=KC * NQKVG, out=KC * D, gate=KC * E)


def cuts(widths):
    at, out = 0, {}
    for name, n in widths.items():
        out[name] = slice(at, at + n)
        at += n
    return out, at


def build(nc, x_d, ctx_d, wa_d, bias_d, gains_d, wf_d, c32_d, c16_d, out_d):
    cut32, n32 = cuts(C32)
    cut16, n16 = cuts(C16)
    cuta, na = cuts(WA)
    x_v = x_d.rearrange("b (c p) d -> (b c) p d", p=P)
    ctx_v = ctx_d.rearrange("b (c p) d -> (b c) p d", p=P)
    out_v = out_d.rearrange("b (c p) d -> (b c) p d", p=P)
    by_expert = nc.dram_tensor("rows_by_expert", [E * CAP, D], F32).ap()
    answers = nc.dram_tensor("answers", [NJ * P, D], F32).ap()

    with ExitStack() as ctx:
        def sb(name, shape, dt=F32, c=ctx):
            return c.enter_context(nc.sbuf_tensor(name, shape, dt))

        def ps(name, shape, dt=F32, c=ctx):
            return c.enter_context(nc.psum_tensor(name, shape, dt))

        def sem(name):
            return ctx.enter_context(nc.semaphore(name))

        def wait(eng, s, value):
            if not isinstance(value, int) or value > 0:
                eng.wait_ge(s, value)

        X = sb("X", [P, T, D])
        XT = sb("XT", [P, T, 2, KC, P], F16)
        WFH = sb("WFH", [P, NU, F], F16)
        WFL = sb("WFL", [P, NU, F], F16)
        c32 = sb("c32", [P, n32 - 2 * CPB * 2 * D])
        c16 = sb("c16", [P, n16], F16)
        gains = sb("gains", [P, 2])
        IDX = sb("IDX", [P, T, 2])
        POS = sb("POS", [P, T, 2])
        GAP = sb("GAP", [P, T])
        seen = sb("seen", [P, 2, E], F16)
        shift = CPB * 4 * D

        def const(name):
            c = cut32[name]
            return c32[:, c.start - shift:c.stop - shift]

        def const16(name):
            return c16[:, cut16[name]]

        with ExitStack() as c1:
            s1 = lambda name, shape, dt=F32: sb(name, shape, dt, c1)
            rot = s1("rot", [P, 2, CPB, 2 * D])
            WAH = s1("WAH", [P, na], F16)
            WAL = s1("WAL", [P, na], F16)
            biasw = s1("biasw", [P, 2 * D], F16)
            ctxb = s1("ctxb", [P, 2, D])
            stage = s1("stage", [P, 2, F])
            xn = s1("xn", [P, 2, D])
            xcs = s1("xcs", [P, 2, 2 * KC, P], F16)
            QKC = s1("QKC", [P, na - KC * NQKVG])
            swp = s1("swp", [P, 2 * D])
            q4 = s1("q4", [P, 2, H, 4, HD], F16)
            QT = s1("QT", [P, H // 2, P], F16)
            KT = s1("KT", [P, H // 2, P], F16)
            sim = s1("sim", [P, H, P])
            V = s1("V", [P, 2, H // 2, 4, HD])
            rT = s1("rT", [P, KC, P])
            sq = s1("sq", [P, D])
            G = s1("G", [P, 2, D])
            y = s1("y", [P, 2, D])
            ys = s1("ys", [P, 2, KC, P], F16)
            S4 = s1("S4", [P, 2, D], F16)
            VS = s1("VS", [P, 2, D], F16)
            xn2 = s1("xn2", [P, 4, D])
            st6 = s1("st6", [P, 2, 6])
            mv = s1("mv", [P, 2, 2, 2])
            NPW = H + 2
            pin = s1("pin", [P, 2, NPW])
            pout = s1("pout", [P, 2, NPW])
            pexp = s1("pexp", [P, NPW])
            nm = s1("nm", [P, 2, 2])
            m8 = s1("m8", [P, E])
            i8 = s1("i8", [P, E], U32)
            ix = s1("ix", [P, 4, 2])
            one1 = s1("one1", [P, E])
            gap1 = s1("gap1", [P, 4])
            hot = s1("hot", [P, E], F16)
            rk = s1("rk", [P, E])
            junk = s1("junk", [P, 2, E])
            pos2 = s1("pos2", [P, 4, 2])
            posi = s1("posi", [P, 4, 2], I32)
            vmean = s1("vmean", [P, KC, H])
            bstage = [a[0:2, :, :].rearrange("p a n -> p (a n)") for a in (y, G)]
            wstage = sim[:, :, :].rearrange("p h n -> p (h n)")
            wstage2 = QKC[:, :]

            bT = ps("bT", [P, 2 * KC, P], F32, c1)
            bQK = ps("bQK", [P, 2 * D], F32, c1)
            bVG = ps("bVG", [P, 2 * D], F32, c1)
            bQT = ps("bQT", [P, H // 2, P], F16, c1)
            bS = [ps(f"bS{a}", [P, 4, P], F32, c1) for a in range(2)]
            bR = ps("bR", [P, 2 * D], F32, c1)
            bY = ps("bY", [P, 2 * D], F32, c1)
            bRT = bR[:, 0:D].rearrange("p (c n) -> p c n", c=KC)
            ret = bR[:, D:2 * D]
            Sm = swp[:, 0:D]
            bSt = bQT[:, :, :].rearrange("p h n -> p (h n)").bitcast(F32)[:, 0:D]

            consts_in = sem("consts_in")
            wa_in = sem("wa_in")
            x_in = [sem(f"x_in{k}") for k in range(4)]
            ctx_in = [sem(f"ctx_in{k}") for k in range(2)]
            w_in = [sem(f"w_in{k}") for k in range(2)]
            prep_v, prep_a = sem("prep_v"), sem("prep_a")
            prep_p = sem("prep_p")
            stats_in = sem("stats_in")
            dve_chain = sem("dve_chain")
            aggr = sem("aggr")
            var_ready = sem("var_ready")
            rstd, rstd_h = sem("rstd"), sem("rstd_h")
            nm1, nm2 = sem("nm1"), sem("nm2")
            xn_done, xn2_done = sem("xn_done"), sem("xn2_done")
            t1 = sem("t1")
            xc_hi, xc_lo = sem("xc_hi"), sem("xc_lo")
            proj_qk, proj_vg = sem("proj_qk"), sem("proj_vg")
            rotc, rots, rotated = sem("rotc"), sem("rots"), sem("rotated")
            v_done, g_done = sem("v_done"), sem("g_done")
            hi4, lo4, dup4 = sem("hi4"), sem("lo4"), sem("dup4")
            qt, kt = sem("qt"), sem("kt")
            qt_out, kt_out = sem("qt_out"), sem("kt_out")
            scored, masked = sem("scored"), sem("masked")
            vs_hi, vs_done = sem("vs_hi"), sem("vs_done")
            qs_done, pvh, pvt, rt_out = sem("qs_done"), sem("pvh"), sem("pvt"), sem("rt_out")
            copied, masked_p = sem("copied"), sem("masked_p")
            stated, sm_done, s4_hi, s4_done = sem("stated"), sem("sm_done"), sem("s4_hi"), sem("s4_done")
            pv = sem("pv")
            sq_done, rg_done, y_done = sem("sq_done"), sem("rg_done"), sem("y_done")
            ss_done = sem("ss_done")
            yt, x2t = sem("yt"), sem("x2t")
            y_hi, y_lo, x2_hi, x2_lo = sem("y_hi"), sem("y_lo"), sem("x2_hi"), sem("x2_lo")
            outp, x2_done = sem("outp"), sem("x2_done")
            logit, hot_done, ranked, pos_done = sem("logit"), sem("hot_done"), sem("ranked"), sem("pos_done")
            top8, top_ix, ixf, one_done, seen_done = (
                sem("top8"), sem("top_ix"), sem("ixf"), sem("one_done"), sem("seen_done"))
            gap_done = sem("gap_done")
            rk_done, pos_f = sem("rk_done"), sem("pos_f")
            scat = [sem(f"scat{k}") for k in range(4)]
            w_scaled, w_hi, w_lo = sem("w_scaled"), sem("w_hi"), sem("w_lo")

            FIRST, LAST = -4, 37
            LOOP = (8, 28)
            LN1, XN, PROJ, ROT, SCORE, PV, YY, YT, OUT, XN2, X2T, ROUTE, SCAT = (
                4, 3, 2, 1, 0, -1, -2, -3, -4, -4, -5, -6, -6)

            def steps(eng, step):
                def straight(s):
                    step(lambda k: Idx(s + k) if 0 <= s + k < T else None, s)
                for s in range(FIRST, LOOP[0]):
                    straight(s)
                with eng.Fori(0, (LOOP[1] - LOOP[0]) // UNROLL) as i:
                    for u in range(UNROLL):
                        step(lambda k, u=u: Idx(LOOP[0] + u + k, i), None)
                for s in range(LOOP[1], LAST + 1):
                    straight(s)

            def so_far(stages, tile_of, s):
                if s is not None:
                    return sum(min(max(s + k + 1, 0), T) for k in stages)
                z = [tile_of(k) for k in stages]
                return z[0].i * (UNROLL * len(z)) + sum(k.c + 1 for k in z)

            def heads_of(a):
                return a.rearrange("p (g a e) -> p g a e", a=2, e=HD)

            def unit_of(tile_of, s, after=0):
                if s is None:
                    return tile_of(LN1) + -after
                s -= after
                return Idx(s - FIRST) if 0 <= s - FIRST < NU else None

            def stat_step(tile_of, s):
                if s is None:
                    return tile_of(LN1)
                return Idx(s - FIRST) if s - FIRST < T + 8 else None

            block = c1.enter_context(nc.Block())

            @block.sync
            def _(sp):
                sp.dma_start(wstage[:, 0:KC * NQKVG], wa_d[:, 0:KC * NQKVG]).then_inc(wa_in, 16)
                sp.dma_start(wstage2[:, 0:na - KC * NQKVG], wa_d[:, KC * NQKVG:na]).then_inc(wa_in, 16)
                sp.dma_start(c32[:, :], c32_d[:, shift:]).then_inc(consts_in, 16)
                sp.dma_start(c16[:, :], c16_d).then_inc(consts_in, 16)
                sp.dma_start(bstage[0], bias_d).then_inc(consts_in, 16)
                sp.dma_start(gains[:, :], gains_d).then_inc(consts_in, 16)
                sp.dma_start(rot[:, :, :, :].rearrange("p a c n -> p (a c n)"),
                             c32_d[:, 0:shift]).then_inc(consts_in, 16)

                def step(tile_of, s):
                    t = tile_of(LN1)
                    if t is not None:
                        wait(sp, x_in[t.slot(4)], t.per(4, 16))
                        sp.dma_start(X[:, bass.ds(t.at(1), 1), :], x_v[bass.ds(t.at(1), 1)].rearrange("o p d -> p o d")
                                     ).then_inc(x_in[t.slot(4)], 16)
                    u = unit_of(tile_of, s)
                    if u is not None:
                        wait(sp, w_lo, u.at(1, -1))
                        sp.dma_start(stage[:, u.slot(2), :], wf_d[bass.ds(u.at(1), 1)].rearrange("o p n -> p (o n)")
                                     ).then_inc(w_in[u.slot(2)], 16)
                    if t is not None:
                        wait(sp, t1, t.at(1, -1))
                        sp.dma_start(ctxb[:, t.slot(2), :], ctx_v[bass.ds(t.at(1), 1)].rearrange("o p d -> p (o d)")
                                     ).then_inc(ctx_in[t.slot(2)], 16)
                steps(sp, step)

            @block.gpsimd
            def _(pool):
                nc.gpsimd.memset(pexp[:, :], -0.5).then_inc(prep_p, 1)
                nc.gpsimd.memset(pin[:, :, :], 1.0).then_inc(prep_p, 1)
                nc.gpsimd.memset(V[:, :, :, :, :], 0.0).then_inc(prep_p, 1)
                pool.wait_ge(prep_p, 2)

                def step(tile_of, s):
                    n = stat_step(tile_of, s)
                    if n is not None and (n.i is not None or n.c >= 1):
                        m = n + -1
                        pool.wait_ge(var_ready, m.at(1, 1))
                        for k, used in ((XN, xn_done), (XN2, xn2_done)):
                            if tile_of(k - 2) is not None:
                                pool.wait_ge(used, tile_of(k - 2).at(1, 1))
                        for a, b, done in ((H, NPW, rstd), (0, H, rstd_h)):
                            nc.gpsimd.tensor_tensor(pout[:, m.slot(2), a:b], pin[:, m.slot(2), a:b], pexp[:, a:b],
                                                    ALU.pow).then_inc(done, 1)
                    t = tile_of(YY)
                    if t is not None:
                        pool.wait_ge(rg_done, t.at(1, 1))
                        pool.wait_ge(rstd_h, n.at(1))
                        nc.gpsimd.tensor_tensor(
                            y[:, t.slot(2), :].rearrange("p (h e) -> p h e", h=H),
                            y[:, t.slot(2), :].rearrange("p (h e) -> p h e", h=H),
                            pout[:, (n + -1).slot(2), 0:H].unsqueeze(2).to_broadcast([P, H, HD]),
                            ALU.mult).then_inc(y_done, 1)
                    t = tile_of(ROT)
                    if t is not None and t.c % 2 == 0:
                        pool.wait_ge(vs_hi, t.per(2, 1, 1))
                        nc.gpsimd.tensor_tensor(heads_of(VS[:, 1, :]), V[:, t.slot(2), :, 0::3, :], heads_of(VS[:, 0, :]), ALU.subtract
                                                ).then_inc(vs_done, 1)
                    t = tile_of(SCORE)
                    if t is not None:
                        pool.wait_ge(copied, t.at(1, 1))
                        nc.gpsimd.tensor_tensor(sim[:, 9:16:2, :], sim[:, 9:16:2, :],
                                                const("tri").unsqueeze(1).to_broadcast([P, 4, P]), ALU.mult
                                                ).then_inc(masked_p, 1)
                    u = unit_of(tile_of, s, 1)
                    if u is not None:
                        pool.wait_ge(w_hi, u.at(1, 1))
                        c = tile_of(SCAT)
                        if c is not None:
                            pool.wait_ge(pos_done, c.at(1, 1))
                            pool.wait_ge(xn2_done, c.at(1, 1))
                        nc.gpsimd.tensor_tensor(WFL[:, bass.ds(u.at(1), 1), :].rearrange("p o n -> p (o n)"),
                                                stage[:, u.slot(2), :],
                                                WFH[:, bass.ds(u.at(1), 1), :].rearrange("p o n -> p (o n)"),
                                                ALU.subtract).then_inc(w_lo, 1)
                    t = tile_of(PROJ)
                    if t is not None:
                        pool.wait_ge(rots, t.at(1, 1))
                        nc.gpsimd.tensor_tensor(QKC[:, 0:2 * D], QKC[:, 0:2 * D], swp[:, :], ALU.add
                                                ).then_inc(rotated, 1)
                    t = tile_of(SCAT)
                    if t is not None:
                        if u is None:
                            pool.wait_ge(pos_done, t.at(1, 1))
                            pool.wait_ge(xn2_done, t.at(1, 1))
                        for k in range(2):
                            pool.indirect_dma_start(
                                by_expert[:, :], bass.IndirectOffsetOnAxis(ap=posi[:, t.slot(4), k:k + 1], axis=0),
                                xn2[:, t.slot(4), :], None).then_inc(scat[t.slot(4)], 16)
                steps(pool, step)
                for k in range(4):
                    pool.wait_ge(scat[k], 2 * 16 * (T // 4))

            @block.scalar
            def _(act):
                act.wait_ge(consts_in, 5 * 16)
                act.wait_ge(prep_p, 3)
                act.wait_ge(prep_v, 3)
                nc.scalar.activation(WAH[:, 0:KC * NQKVG], wstage[:, 0:KC * NQKVG], ACT.Copy).then_inc(prep_a, 1)
                nc.scalar.activation(WAH[:, KC * NQKVG:na], wstage2[:, 0:na - KC * NQKVG], ACT.Copy
                                     ).then_inc(prep_a, 1)
                nc.scalar.activation(gains[:, :], gains[:, :], ACT.Tanh).then_inc(prep_a, 1)

                def step(tile_of, s):
                    n = stat_step(tile_of, s)
                    t = tile_of(PROJ)
                    if t is not None:
                        act.wait_ge(t1, t.at(1, 1))
                        wait(act, proj_vg, t.at(1))
                        nc.scalar.activation(xcs[:, 0], bT[:, :, :], ACT.Copy).then_inc(xc_hi, 1)
                    t = tile_of(SCORE)
                    if t is not None:
                        act.wait_ge(qt, t.at(1, 1))
                        wait(act, scored, t.at(2))
                        if t.c % 2 == 0:
                            wait(act, qs_done, t.per(2, 1))
                        nc.scalar.activation(QT[:, :, :], bQT[:, :, :], ACT.Copy).then_inc(qt_out, 1)
                    u = unit_of(tile_of, s, 1)
                    if u is not None:
                        act.wait_ge(w_in[u.slot(2)], u.per(2, 16, 16))
                        nc.scalar.activation(stage[:, u.slot(2), :], stage[:, u.slot(2), :], ACT.Copy, scale=WS
                                             ).then_inc(w_scaled, 1)
                    if t is not None:
                        act.wait_ge(kt, t.at(1, 1))
                        nc.scalar.activation(KT[:, :, :], bQT[:, :, :], ACT.Copy).then_inc(kt_out, 1)
                    w = tile_of(ROT)
                    if w is not None:
                        act.wait_ge(rotated, w.at(1, 1))
                        wait(act, kt, w.at(1))
                        if w.c % 2:
                            act.wait_ge(stated, w.per(2, 1, 1))
                        r = QKC[:, 0:2 * D].rearrange("p (a h e) -> p a h e", a=2, h=H)
                        for a, at in ((0, q4[:, 0, :, 0::2, :]), (1, q4[:, 1, :, 0:2, :])):
                            nc.scalar.activation(at, r[:, a].unsqueeze(2).to_broadcast([P, H, 2, HD]),
                                                 ACT.Copy).then_inc(hi4, 1)
                    t = tile_of(PV)
                    if t is not None:
                        act.wait_ge(pvt, t.at(1, 1))
                        wait(act, pv, t.at(1))
                        nc.scalar.activation(rT[:, :, :], bRT, ACT.Copy).then_inc(rt_out, 1)
                    if w is not None:
                        act.wait_ge(proj_vg, w.at(1, 1))
                        wait(act, pvt, w.at(1, -1))
                        nc.scalar.activation(V[:, w.slot(2), :, 0::3, :], heads_of(bVG[:, 0:D]), ACT.Copy,
                                             scale=1.0 / WS).then_inc(v_done, 1)
                        if w.c % 2 == 0:
                            act.wait_ge(v_done, w.at(1, 1))
                            wait(act, stated, w.per(2, 1))
                            nc.scalar.activation(heads_of(VS[:, 0, :]), V[:, w.slot(2), :, 0::3, :], ACT.Copy
                                                 ).then_inc(vs_hi, 1)
                    if u is not None:
                        act.wait_ge(w_scaled, u.at(1, 1))
                        nc.scalar.activation(WFH[:, bass.ds(u.at(1), 1), :].rearrange("p o n -> p (o n)"),
                                             stage[:, u.slot(2), :], ACT.Copy).then_inc(w_hi, 1)
                    if w is not None:
                        wait(act, rg_done, w.at(1, -1))
                        nc.scalar.activation(G[:, w.slot(2), :], bVG[:, D:2 * D], ACT.Silu, scale=1.0 / WS
                                             ).then_inc(g_done, 1)
                    t = tile_of(PV)
                    if t is not None:
                        act.wait_ge(rg_done, t.at(1, 1))
                        wait(act, ss_done, t.at(1))
                        nc.scalar.activation(sq[:, :], ret, ACT.Square).then_inc(sq_done, 1)
                    t = tile_of(XN)
                    if t is not None:
                        act.wait_ge(nm1, t.at(1, 1))
                        wait(act, t1, t.at(1, -1))
                        nc.scalar.activation(xn[:, t.slot(2), :], X[:, bass.ds(t.at(1), 1), :].rearrange("p o d -> p (o d)"),
                                             ACT.Identity, bias=nm[:, 0, t.slot(2):t.slot(2) + 1],
                                             scale=pout[:, (n + -1).slot(2), H + 1:H + 2]).then_inc(xn_done, 1)
                    r, t = tile_of(X2T), tile_of(YT)
                    if r is not None:
                        act.wait_ge(x2t, r.at(1, 1))
                    if t is not None:
                        act.wait_ge(yt, t.at(1, 1))
                        wait(act, outp, t.at(1))
                        nc.scalar.activation(ys[:, 0], bY[:, 0:D].rearrange("p (k n) -> p k n", k=KC),
                                             ACT.Copy).then_inc(y_hi, 1)
                    if r is not None:
                        nc.scalar.activation(XT[:, bass.ds(r.at(1), 1), 0].rearrange("p o k n -> p (o k n)"),
                                             bY[:, D:2 * D], ACT.Copy).then_inc(x2_hi, 1)
                    t = tile_of(SCORE)
                    if t is not None:
                        act.wait_ge(scored, t.at(2, 2))
                        wait(act, pvt, t.at(1))
                        nc.scalar.activation(sim[:, 9:16:2, :], bS[1][:, :, :], ACT.Copy).then_inc(copied, 1)
                    t = tile_of(XN2)
                    if t is not None:
                        act.wait_ge(nm2, t.at(1, 1))
                        wait(act, scat[t.slot(4)], t.per(4, 32))
                        nc.scalar.activation(xn2[:, t.slot(4), :], X[:, bass.ds(t.at(1), 1), :].rearrange("p o d -> p (o d)"),
                                             ACT.Identity, bias=nm[:, 1, t.slot(2):t.slot(2) + 1],
                                             scale=pout[:, (n + -1).slot(2), H:H + 1]).then_inc(xn2_done, 1)
                steps(act, step)

            @block.vector
            def _(dve):
                vec = nc.vector
                dve.wait_ge(wa_in, 2 * 16)
                wv = wstage[:, 0:KC * NQKVG].rearrange("p (k a h e) -> p k a h e", k=KC, a=4, h=H)
                for k in range(KC):
                    vec.tensor_reduce(vmean[:, k, :], wv[:, k, 2], AX.X, ALU.add).then_inc(prep_v, 1)
                dve.wait_ge(prep_v, 2)
                for k in range(KC):
                    vec.scalar_tensor_tensor(out=wv[:, k, 2], in0=vmean[:, k, :].unsqueeze(2).to_broadcast([P, H, HD]),
                                             scalar=-1.0 / HD, in1=wv[:, k, 2], op0=ALU.mult, op1=ALU.add
                                             ).then_inc(dve_chain, 1)
                dve.wait_ge(dve_chain, 2)
                vec.tensor_scalar(wstage[:, 0:KC * NQKVG], wstage[:, 0:KC * NQKVG], WS, None, ALU.mult
                                  ).then_inc(dve_chain, 1)
                vec.tensor_scalar(wstage2[:, 0:na - KC * NQKVG], wstage2[:, 0:na - KC * NQKVG], WS, None, ALU.mult
                                  ).then_inc(prep_v, 1)
                dve.wait_ge(consts_in, 5 * 16)
                vec.memset(biasw[:, :], 0.0).then_inc(dve_chain, 1)
                vec.memset(seen[:, :, :], 0.0).then_inc(dve_chain, 1)
                b0, b1 = bstage
                vec.tensor_scalar(b0, b0, WS, None, ALU.mult).then_inc(dve_chain, 1)
                dve.wait_ge(dve_chain, 6)
                vec.tensor_copy(biasw[0:2, :], b0).then_inc(dve_chain, 1)
                dve.wait_ge(dve_chain, 7)
                vec.tensor_tensor(b1, b0, biasw[0:2, :], ALU.subtract).then_inc(dve_chain, 1)
                dve.wait_ge(dve_chain, 8)
                vec.tensor_scalar(b1, b1, const("pick")[0:2, 1:2], None, ALU.mult).then_inc(dve_chain, 1)
                dve.wait_ge(dve_chain, 9)
                vec.scalar_tensor_tensor(out=biasw[0:2, :], in0=biasw[0:2, :], scalar=const("pick")[0:2, 0:1],
                                         in1=b1, op0=ALU.mult, op1=ALU.add).then_inc(dve_chain, 1)
                dve.wait_ge(prep_a, 2)
                vec.tensor_tensor(WAL[:, 0:KC * NQKVG], wstage[:, 0:KC * NQKVG], WAH[:, 0:KC * NQKVG], ALU.subtract
                                  ).then_inc(dve_chain, 1)
                vec.tensor_tensor(WAL[:, KC * NQKVG:na], wstage2[:, 0:na - KC * NQKVG], WAH[:, KC * NQKVG:na],
                                  ALU.subtract).then_inc(prep_v, 1)
                dve.wait_ge(prep_a, 3)
                vec.tensor_scalar(gains[:, :], gains[:, :], 1.0 / WS, None, ALU.mult).then_inc(dve_chain, 1)
                dve.wait_ge(dve_chain, 12)
                dve.wait_ge(prep_p, 2)

                def row(a, t):
                    return a[:, bass.ds(t.at(1), 1), :].rearrange("p o d -> p (o d)")

                def group(a, t):
                    return a[:, bass.ds(t.at(1, -3), 4), :]

                def mask_round(t, r):
                    dve.wait_ge(scored, t.at(2, r + 1))
                    wait(dve, pvt if r else pvh, t.at(1))
                    for a in range(2 - r):
                        vec.tensor_tensor(sim[:, 8 * r + a:8 * r + 8:2, :], bS[a][:, :, :],
                                          const("tri").unsqueeze(1).to_broadcast([P, 4, P]), ALU.mult
                                          ).then_inc(masked, 1)

                def step(tile_of, s):
                    n = stat_step(tile_of, s)
                    if n is not None:
                        wait(dve, rstd_h, n.at(1, -1))
                    w = tile_of(ROT)
                    t = tile_of(PROJ)
                    if t is not None:
                        dve.wait_ge(xc_hi, t.at(1, 1))
                        vec.tensor_tensor(xcs[:, 1], bT[:, :, :], xcs[:, 0], ALU.subtract).then_inc(xc_lo, 1)
                    t, r, q, p = tile_of(OUT), tile_of(ROUTE), tile_of(LN1 - 1), tile_of(PV - 1)
                    m = n + -1 if n is not None and (n.i is not None or n.c >= 1) else None
                    if m is not None and q is not None:
                        dve.wait_ge(x_in[q.slot(4)], q.per(4, 16, 16))
                    if t is not None:
                        dve.wait_ge(outp, t.at(1, 1))
                        if r is not None:
                            dve.wait_ge(logit, r.at(1, 1))
                        vec.scalar_tensor_tensor(out=row(X, t), in0=bY[:, 0:D], scalar=gains[:, 0:1], in1=row(X, t),
                                                 op0=ALU.mult, op1=ALU.add).then_inc(x2_done, 1)
                    if r is not None:
                        if t is None:
                            dve.wait_ge(logit, r.at(1, 1))
                        vec.max(m8[:, :], bY[:, D:D + E]).then_inc(top8, 1)
                    if m is not None and q is not None:
                        vec.bn_stats(st6[:, 0, :], row(X, q)).then_inc(stats_in, 1)
                    if t is not None:
                        dve.wait_ge(x2_done, t.at(1, 1))
                    if r is not None:
                        dve.wait_ge(top8, r.at(1, 1))
                        vec.tensor_tensor(gap1[:, r.slot(4):r.slot(4) + 1], m8[:, 1:2], m8[:, 0:1], ALU.subtract
                                          ).then_inc(gap_done, 1)
                        vec.max_index(i8[:, :], m8[:, :], bY[:, D:D + E]).then_inc(top_ix, 1)
                    if m is not None and t is not None:
                        vec.bn_stats(st6[:, 1, :], row(X, t)).then_inc(stats_in, 1)
                    if r is not None:
                        dve.wait_ge(top_ix, r.at(1, 1))
                        vec.tensor_copy(ix[:, r.slot(4), :], i8[:, 0:2]).then_inc(ixf, 1)
                    if m is not None and p is not None:
                        dve.wait_ge(ss_done, p.at(1, 1))
                        z = vec.tensor_scalar(pin[:, m.slot(2), 0:H], pin[:, m.slot(2), 0:H], 1.0 / HD, GN_EPS,
                                              ALU.mult, ALU.add)
                    if r is not None:
                        dve.wait_ge(ixf, r.at(1, 1))
                        vec.tensor_scalar(one1[:, :], const("e8"), ix[:, r.slot(4), 0:1], None, ALU.is_equal
                                          ).then_inc(one_done, 1)
                        if r.c % 4 == 3:
                            vec.tensor_copy(group(IDX, r), ix[:, :, :])
                            dve.wait_ge(gap_done, r.at(1, 1))
                            vec.tensor_copy(GAP[:, bass.ds(r.at(1, -3), 4)], gap1[:, :])
                    if m is not None and (t is not None or q is not None):
                        dve.wait_ge(stats_in, so_far((LN1 - 1, OUT), tile_of, s))
                        if p is None:
                            vec.tensor_copy(junk[:, 0, 0:1], st6[:, 0, 0:1])
                    if r is not None:
                        dve.wait_ge(one_done, r.at(1, 1))
                        vec.scalar_tensor_tensor(out=hot[:, :], in0=const("e8"), scalar=ix[:, r.slot(4), 1:2],
                                                 in1=one1[:, :], op0=ALU.is_equal, op1=ALU.add).then_inc(hot_done, 1)
                    if m is not None:
                        if t is not None or q is not None:
                            for k, w_ in ((1, t), (0, q)):
                                if w_ is not None:
                                    vec.bn_aggr(mv[:, k, w_.slot(2), :], st6[:, k, :]).then_inc(aggr, 1)
                            dve.wait_ge(aggr, so_far((LN1 - 1, OUT), tile_of, s))
                            for k, w_ in ((1, t), (0, q)):
                                if w_ is not None:
                                    z = vec.tensor_scalar(pin[:, m.slot(2), H + 1 - k:H + 2 - k],
                                                          mv[:, k, w_.slot(2), 1:2], LN_EPS, None, ALU.add)
                        z.then_inc(var_ready, 1)
                    if r is not None:
                        dve.wait_ge(ranked, r.at(1, 1))
                        vec.tensor_tensor(rk[:, :], bY[:, D + E:D + 2 * E], const("ebase"), ALU.add
                                          ).then_inc(rk_done, 1)
                        wait(dve, seen_done, r.at(1))
                        vec.tensor_tensor(seen[:, (r + 1).slot(2), :], seen[:, r.slot(2), :], hot[:, :], ALU.add
                                          ).then_inc(seen_done, 1)
                    c = tile_of(SCORE)
                    if c is not None and c.c % 2 == 0:
                        dve.wait_ge(stated, c.per(2, 1, 1))
                        dve.wait_ge(rotated, w.at(1, 1) if w is not None else T)
                        vec.tensor_tensor(Sm, bSt, const("smask"), ALU.mult).then_inc(sm_done, 1)
                        dve.wait_ge(sm_done, c.per(2, 1, 1))
                        wait(dve, qs_done, c.per(2, 1))
                        vec.tensor_copy(S4[:, 0, :], Sm).then_inc(s4_hi, 1)
                        dve.wait_ge(s4_hi, c.per(2, 1, 1))
                        vec.tensor_tensor(S4[:, 1, :], Sm, S4[:, 0, :], ALU.subtract).then_inc(s4_done, 1)
                    if c is not None:
                        mask_round(c, 0)
                    t = tile_of(PV)
                    if t is not None:
                        dve.wait_ge(pv, t.at(1, 1))
                        dve.wait_ge(g_done, t.at(1, 1))
                        wait(dve, yt, t.at(1, -1))
                        vec.tensor_tensor(y[:, t.slot(2), :], ret, G[:, t.slot(2), :], ALU.mult
                                          ).then_inc(rg_done, 1)
                    if r is not None:
                        dve.wait_ge(rk_done, r.at(1, 1))
                        for k in range(2):
                            vec.scalar_tensor_tensor(out=junk[:, k, :], in0=const("e8"),
                                                     scalar=ix[:, r.slot(4), k:k + 1], in1=rk[:, :],
                                                     op0=ALU.is_equal, op1=ALU.mult,
                                                     accum_out=pos2[:, r.slot(4), k:k + 1]).then_inc(pos_f, 1)
                    for k, (off, done, used) in enumerate(((XN, nm1, xn_done), (XN2, nm2, xn2_done))):
                        t = tile_of(off)
                        if t is not None:
                            dve.wait_ge(rstd, n.at(1))
                            wait(dve, used, t.at(1, -1))
                            vec.scalar_tensor_tensor(
                                out=nm[:, k, t.slot(2):t.slot(2) + 1], in0=mv[:, k, t.slot(2), 0:1], scalar=-1.0,
                                in1=pout[:, (n + -1).slot(2), H + 1 - k:H + 2 - k],
                                op0=ALU.mult, op1=ALU.mult).then_inc(done, 1)
                    t = tile_of(PV)
                    if t is not None:
                        dve.wait_ge(sq_done, t.at(1, 1))
                        vec.tensor_reduce(pin[:, n.slot(2), 0:H], sq[:, :].rearrange("p (h e) -> p h e", h=H),
                                          AX.X, ALU.add).then_inc(ss_done, 1)
                    if r is not None:
                        dve.wait_ge(pos_f, r.at(2, 2))
                        wait(dve, scat[r.slot(4)], r.per(4, 32))
                        vec.tensor_copy(posi[:, r.slot(4), :], pos2[:, r.slot(4), :]).then_inc(pos_done, 1)
                        if r.c % 4 == 3:
                            vec.tensor_copy(group(POS, r), pos2[:, :, :])
                    if c is not None:
                        mask_round(c, 1)
                    if w is not None:
                        dve.wait_ge(hi4, w.at(2, 2))
                        rr = QKC[:, 0:2 * D].rearrange("p (a h e) -> p a h e", a=2, h=H)
                        for a, slot in ((0, 1), (1, 2)):
                            vec.tensor_tensor(q4[:, a, :, slot, :], rr[:, a], q4[:, a, :, 0, :], ALU.subtract
                                              ).then_inc(lo4, 1)
                        for a, slot in ((0, 1), (1, 2)):
                            dve.wait_ge(lo4, w.at(2, a + 1))
                            vec.tensor_copy(q4[:, a, :, 3, :], q4[:, a, :, slot, :]).then_inc(dup4, 1)
                    t = tile_of(YT)
                    if t is not None:
                        dve.wait_ge(y_hi, t.at(1, 1))
                        if tile_of(X2T) is not None:
                            dve.wait_ge(x2_hi, tile_of(X2T).at(1, 1))
                        vec.tensor_tensor(ys[:, 1], bY[:, 0:D].rearrange("p (k n) -> p k n", k=KC), ys[:, 0],
                                          ALU.subtract).then_inc(y_lo, 1)
                    t = tile_of(X2T)
                    if t is not None:
                        dve.wait_ge(x2_hi, t.at(1, 1))
                        o = XT[:, bass.ds(t.at(1), 1)]
                        vec.tensor_tensor(o[:, :, 1].rearrange("p o k n -> p (o k n)"), bY[:, D:2 * D],
                                          o[:, :, 0].rearrange("p o k n -> p (o k n)"), ALU.subtract
                                          ).then_inc(x2_lo, 1)
                    t = tile_of(PROJ)
                    if t is not None:
                        dve.wait_ge(proj_qk, t.at(1, 1))
                        wait(dve, hi4, t.at(2))
                        k = t.c % 2
                        vec.tensor_tensor(QKC[:, 0:2 * D], bQK[:, :], rot[:, 0, k, :], ALU.mult
                                          ).then_inc(rotc, 1)
                        wait(dve, rotated, t.at(1))
                        if c is not None:
                            dve.wait_ge(s4_done, c.per(2, 1, 1))
                        pair = bQK[:, :].rearrange("p (a two) -> p a two", two=2)[:, :, ::-1]
                        vec.tensor_tensor(swp[:, :].rearrange("p (a two) -> p a two", two=2), pair,
                                          rot[:, 1, k, :].rearrange("p (a two) -> p a two", two=2), ALU.mult
                                          ).then_inc(rots, 1)

                steps(dve, step)

            @block.tensor
            def _(pe):
                mm = nc.tensor.matmul

                def three(out, parts, first=True, last=True):
                    ops = [(sh, mh) for sh, sl, mh, ml in parts] + \
                          [(sh, ml) for sh, sl, mh, ml in parts] + [(sl, mh) for sh, sl, mh, ml in parts]
                    for k, (st, mo) in enumerate(ops):
                        z = mm(out, st, mo, start=first and k == 0, stop=last and k == len(ops) - 1)
                    return z

                def wa(name, k, a=0, b=None):
                    n = (cuta[name].stop - cuta[name].start) // KC
                    lo = cuta[name].start + k * n
                    b = n if b is None else b
                    return WAH[:, lo + a:lo + b], WAL[:, lo + a:lo + b]

                pe.wait_ge(prep_v, 4)
                pe.wait_ge(dve_chain, 12)
                pe.wait_ge(prep_p, 3)

                def slots_transposed(a, done):
                    src = q4[:, a].rearrange("p (g b) j e -> p g (b j e)", b=2)
                    for g in range(H // 2):
                        z = nc.tensor.transpose(bQT[:, g, :], src[:, g, :], const16("ident"))
                    z.then_inc(done, 1)

                def score_round(t, r):
                    wait(pe, masked, t.at(3, 2 * r))
                    wait(pe, copied, t.at(1))
                    for g in range(4):
                        for a in range(2):
                            q = slice(64 * a, 64 * a + 64)
                            z = mm(bS[a][:, g, :], KT[q, 4 * r + g, :], QT[q, 4 * r + g, :],
                                   start=True, stop=True)
                    z.then_inc(scored, 1)

                def step(tile_of, s):
                    t = tile_of(PROJ)
                    if t is not None:
                        pe.wait_ge(xn_done, t.at(1, 1))
                        pe.wait_ge(ctx_in[t.slot(2)], t.per(2, 16, 16))
                        wait(pe, xc_lo, t.at(1))
                        for k in range(KC):
                            nc.tensor.transpose(bT[:, k, :], xn[:, t.slot(2), P * k:P * k + P], const("ident"))
                        for k in range(KC):
                            z = nc.tensor.transpose(bT[:, KC + k, :], ctxb[:, t.slot(2), P * k:P * k + P],
                                                    const("ident"))
                        z.then_inc(t1, 1)
                    p = tile_of(PV)
                    if p is not None:
                        wait(pe, ss_done, p.at(1))
                        if p.c % 2:
                            pe.wait_ge(s4_done, p.per(2, 1, 1))
                            for a in range(2):
                                for g in range(H // 2):
                                    z = mm(bRT[32 * (g % 4):32 * (g % 4) + 32, g // 4, :],
                                           S4[:, a, 32 * g:32 * g + 32], QT[:, g, :],
                                           start=a == 0 and g < 4, stop=False)
                            z.then_inc(qs_done, 1)
                    w = tile_of(SCORE)
                    if w is not None:
                        pe.wait_ge(dup4, w.at(2, 2))
                        wait(pe, kt_out, w.at(1))
                        wait(pe, sm_done, (w + 1).per(2, 1))
                        slots_transposed(0, qt)
                    t = tile_of(OUT)
                    if t is not None:
                        pe.wait_ge(y_lo, t.at(1, 1))
                        if tile_of(ROUTE) is not None:
                            pe.wait_ge(x2_lo, tile_of(ROUTE).at(1, 1))
                        three(bY[:, 0:D], [(ys[:, 0, k], ys[:, 1, k], *wa("out", k)) for k in range(KC)], last=False)
                        mm(bY[:, 0:D], const16("ones"), biasw[:, D:2 * D], start=False, stop=True).then_inc(outp, 1)
                    t = tile_of(ROUTE)
                    if t is not None:
                        pe.wait_ge(x2_lo, t.at(1, 1))
                        xt = XT[:, bass.ds(t.at(1), 1)]
                        three(bY[:, D:D + E], [(xt[:, :, 0, k].rearrange("p o n -> p (o n)"),
                                                xt[:, :, 1, k].rearrange("p o n -> p (o n)"), *wa("gate", k))
                                               for k in range(KC)]).then_inc(logit, 1)
                    if w is not None:
                        pe.wait_ge(qt_out, w.at(1, 1))
                        slots_transposed(1, kt)
                    t = tile_of(PROJ)
                    if t is not None:
                        pe.wait_ge(xc_lo, t.at(1, 1))
                        wait(pe, rots, t.at(1))
                        three(bQK[:, 0:D], [(xcs[:, 0, k], xcs[:, 1, k], *wa("qkvg", k, 0, D)) for k in range(KC)])
                        three(bQK[:, D:2 * D], [(xcs[:, 0, KC + k], xcs[:, 1, KC + k], *wa("qkvg", k, D, 2 * D))
                                                for k in range(KC)]).then_inc(proj_qk, 1)
                    if w is not None:
                        pe.wait_ge(kt_out, w.at(1, 1))
                        if w.c % 2 == 0:
                            pe.wait_ge(vs_done, w.per(2, 1, 1))
                            kk = q4[:, 1].rearrange("p (g b) j e -> p g (b j e)", b=2)
                            for g in range(H // 2):
                                for a in range(2):
                                    z = mm(bSt[:, 32 * g:32 * g + 32], kk[:, g, :],
                                           VS[:, a, 32 * g:32 * g + 32], start=a == 0, stop=a == 1)
                            z.then_inc(stated, 1)
                        score_round(w, 0)
                    t = tile_of(ROUTE)
                    if t is not None:
                        pe.wait_ge(hot_done, t.at(1, 1))
                        wait(pe, seen_done, t.at(1))
                        mm(bY[:, D + E:D + 2 * E], const16("before"), hot[:, :], start=True, stop=False)
                        mm(bY[:, D + E:D + 2 * E], const16("ones"), seen[:, t.slot(2), :], start=False, stop=True
                           ).then_inc(ranked, 1)
                    if p is not None:
                        for c in range(KC):
                            pe.wait_ge(masked, p.at(3, 2 + c))
                            if c:
                                pe.wait_ge(masked_p, p.at(1, 1))
                            for a in range(2):
                                for k in range(4):
                                    g = 4 * c + k
                                    z = mm(bRT[32 * k:32 * k + 32, c, :],
                                           V[:, p.slot(2), g, 2 * a:2 * a + 2, :].rearrange("p a e -> p (a e)"),
                                           sim[:, 2 * g + a, :], start=p.c % 2 == 0 and c == 0 and a == 0,
                                           stop=c == 1 and a == 1)
                            z.then_inc(pvt if c else pvh, 1)
                    t, r = tile_of(YT), tile_of(X2T)
                    if t is not None or r is not None:
                        a = tile_of(OUT)
                        if a is not None:
                            pe.wait_ge(x2_done, a.at(1, 1))
                        a = tile_of(ROUTE)
                        if a is not None:
                            pe.wait_ge(rk_done, a.at(1, 1))
                    if r is not None:
                        pe.wait_ge(xn2_done, r.at(1, 1))
                        for k in range(KC):
                            z = nc.tensor.transpose(bY[:, D + P * k:D + P * k + P], xn2[:, r.slot(4), P * k:P * k + P],
                                                    const("ident"))
                        z.then_inc(x2t, 1)
                    if p is not None:
                        pe.wait_ge(rt_out, p.at(1, 1))
                        for c in range(KC):
                            z = nc.tensor.transpose(ret[:, P * c:P * c + P], rT[:, c, :], const("ident"))
                        z.then_inc(pv, 1)
                    if t is not None:
                        pe.wait_ge(y_done, t.at(1, 1))
                        for k in range(KC):
                            z = nc.tensor.transpose(bY[:, P * k:P * k + P], y[:, t.slot(2), P * k:P * k + P],
                                                    const("ident"))
                        z.then_inc(yt, 1)
                    if w is not None:
                        score_round(w, 1)
                    t = tile_of(PROJ)
                    if t is not None:
                        wait(pe, g_done, t.at(1))
                        three(bVG[:, 0:D], [(xcs[:, 0, KC + k], xcs[:, 1, KC + k], *wa("qkvg", k, 2 * D, 3 * D))
                                            for k in range(KC)])
                        three(bVG[:, D:2 * D], [(xcs[:, 0, k], xcs[:, 1, k], *wa("qkvg", k, 3 * D, 4 * D))
                                                for k in range(KC)], last=False)
                        mm(bVG[:, D:2 * D], const16("ones"), biasw[:, 0:D], start=False, stop=True
                           ).then_inc(proj_vg, 1)
                steps(pe, step)

        NS = 4
        E0, E1 = NS, NS + NJ
        NP = T + NJ
        with ExitStack() as c2:
            s2 = lambda name, shape, dt=F32: sb(name, shape, dt, c2)
            xg = s2("xg", [P, 4, D])
            xgs = s2("xgs", [P, 2, 2, KC, P], F16)
            g = s2("g", [P, 2, F])
            hs = s2("hs", [P, 2, 2, FC, P], F16)
            yb = s2("yb", [P, 4, D])
            Y12 = s2("Y12", [P, 4, 2, D])
            zero = s2("zero", [P, D])
            nt, cum, cs, delta, oneE, junk2 = (s2(n, [P, E]) for n in ("nt", "cum", "cs", "delta", "oneE", "junk2"))
            nti = s2("nti", [P, E], I32)
            zrow = s2("zrow", [P, E], I32)
            tj = s2("tj", [P, 5])
            which = s2("which", [P, 2 * T, E])
            ints = s2("ints", [P, 2 * NJ], I32)
            posk = s2("posk", [P, T, 2], I32)
            posg = s2("posg", [P, 4, 2], I32)
            ex = s2("ex", [P, T])
            den = s2("den", [P, T])
            offs = s2("offs", [P, 2 * T])
            a12 = s2("a12", [P, T, 2])

            uA = [ps(f"uA{k}", [P, F], F32, c2) for k in range(2)]
            hT = [ps(f"hT{k}", [P, FC, P], F32, c2) for k in range(2)]
            yD = [ps(f"yD{k}", [P, D], F32, c2) for k in range(2)]
            xg_t = ps("xg_t", [P, KC, P], F32, c2)
            cnt = ps("cnt", [P, E], F32, c2)

            counted, tiles_known = sem("counted"), sem("tiles_known")
            ch = sem("ch")
            rows_known, zeroed, zfill = sem("rows_known"), sem("zeroed"), sem("zfill")
            zrows_known, turned = sem("zrows_known"), sem("turned")
            ex_done, mix_done, posk_done = sem("ex_done"), sem("mix_done"), sem("posk_done")
            xg_in = [sem(f"xg_in{k}") for k in range(4)]
            xgt, xg_hi, xg_lo = sem("xgt"), sem("xg_hi"), sem("xg_lo")
            up_done, gelu_done, ht_done = sem("up_done"), sem("gelu_done"), sem("ht_done")
            h_hi, h_lo, down_done = sem("h_hi"), sem("h_lo"), sem("down_done")
            y_out, s_out = sem("y_out"), sem("s_out")
            stored = [sem(f"stored{k}") for k in range(4)]
            posg_done = sem("posg_done")
            y12 = [sem(f"y12_{k}") for k in range(4)]
            mix1, mixed = sem("mix1"), sem("mixed")
            written = sem("written")

            LOAD, XTR, UPS, HTR, DNS = 4, 2, 1, 0, -1
            CF = E1 + 1
            STEPS = (-4, CF + T)
            LOOPS = ((9, 69), (E1 + 4, E1 + 24))

            def steps2(eng, step, between=lambda: None):
                def kind(p):
                    return "routed" if E0 <= p < E1 else "shared"

                def straight(s):
                    step(lambda k: (Idx(s + k), kind(s + k)) if 0 <= s + k < NP else (None, None),
                         Idx(s - CF) if 0 <= s - CF < T else None)
                at = STEPS[0]
                for a, b in LOOPS:
                    for s in range(at, a):
                        straight(s)
                        if s == LOOPS[0][1]:
                            between()
                    with eng.Fori(0, (b - a) // UNROLL) as i:
                        for u in range(UNROLL):
                            step(lambda k, u=u: (Idx(a + u + k, i), kind(a + k)),
                                 Idx(a + u - CF, i) if a > CF else None)
                    at = b
                for s in range(at, STEPS[1]):
                    straight(s)

            def routed(p):
                return p + -E0

            def shared(p, first):
                return p if first else p + -NJ

            def flat(a):
                return a[:, :, :].rearrange("p k n -> p (k n)")

            def hidden(p, kind):
                return flat(hT[p.slot(2)]) if kind == "routed" else g[:, p.slot(2), :]

            def token_tile(p):
                return shared(p, p.i is None and p.c < E0)

            block = c2.enter_context(nc.Block())

            @block.sync
            def _(sp):
                sp.wait_ge(rows_known, 1)
                sp.wait_ge(zfill, E * 16)

                def step(at, m):
                    p, kind = at(LOAD)
                    if kind == "routed":
                        j = routed(p)
                        wait(sp, xgt, j.at(1, -3))
                        r = sp.value_load(ints[0:1, bass.ds(j.at(1), 1)], min_val=0, max_val=E * CAP - P)
                        sp.dma_start(xg[:, j.slot(4), :], by_expert[bass.ds(r, P), :]).then_inc(xg_in[j.slot(4)], 16)
                    p, kind = at(DNS)
                    if kind == "routed":
                        j = routed(p)
                        sp.wait_ge(y_out, j.at(1, 1))
                        sp.dma_start(answers[bass.ds(j.at(P), P), :], yb[:, j.slot(4), :]
                                     ).then_inc(stored[j.slot(4)], 16)
                    if m is not None:
                        sp.wait_ge(mixed, m.at(1, 1))
                        sp.dma_start(out_v[bass.ds(m.at(1), 1)].rearrange("o p d -> p (o d)"),
                                     X[:, bass.ds(m.at(1), 1), :].rearrange("p o d -> p (o d)")
                                     ).then_inc(written, 16)
                steps2(sp, step)
                sp.wait_ge(written, T * 16)

            @block.gpsimd
            def _(pool):
                nc.gpsimd.memset(zero[:, :], 0.0).then_inc(zeroed, 1)
                pool.wait_ge(zrows_known, 1)
                pool.wait_ge(zeroed, 1)
                for e in range(E):
                    pool.indirect_dma_start(by_expert[:, :], bass.IndirectOffsetOnAxis(ap=zrow[:, e:e + 1], axis=0),
                                            zero[:, :], None).then_inc(zfill, 16)
                pool.wait_ge(posk_done, 1)
                for k in range(4):
                    pool.wait_ge(stored[k], NJ // 4 * 16)

                def place(m):
                    wait(pool, mixed, m.at(1, -3))
                    wait(pool, posg_done, m.at(1))
                    nc.gpsimd.tensor_copy(posg[:, m.slot(4), :],
                                          posk[:, bass.ds(m.at(1), 1), :].rearrange("p o d -> p (o d)")
                                          ).then_inc(posg_done, 1)

                def gather(m):
                    for a in range(2):
                        pool.indirect_dma_start(Y12[:, m.slot(4), a, :], None, answers[:, :],
                                                bass.IndirectOffsetOnAxis(ap=posg[:, m.slot(4), a:a + 1], axis=0)
                                                ).then_inc(y12[m.slot(4)], 16)
                for k in range(4):
                    place(Idx(k))
                    if k:
                        gather(Idx(k - 1))
                with pool.Fori(0, T // UNROLL - 1) as i:
                    for k in range(4):
                        place(Idx(4 + k, i))
                        gather(Idx(3 + k, i))
                pool.wait_ge(posg_done, T)
                gather(Idx(T - 1))

            @block.scalar
            def _(act):
                nc.scalar.activation(ex[:, :], GAP[:, :], ACT.Exp, scale=1.0 / WS).then_inc(ex_done, 1)

                def step(at, m):
                    p, kind = at(XTR)
                    if kind == "routed":
                        j = routed(p)
                        act.wait_ge(xgt, j.at(1, 1))
                        wait(act, up_done, p.at(1, -1))
                        nc.scalar.activation(xgs[:, j.slot(2), 0], xg_t[:, :, :], ACT.Copy).then_inc(xg_hi, 1)
                    def up():
                        p, kind = at(UPS)
                        if p is None:
                            return
                        act.wait_ge(up_done, p.at(1, 1))
                        wait(act, h_lo, p.at(1, -1))
                        u = uA[p.slot(2)][:, :] if kind == "routed" else flat(hT[p.slot(2)])
                        nc.scalar.activation(g[:, p.slot(2), :], u, ACT.Gelu, scale=1.0 / WS
                                             ).then_inc(gelu_done, 1)
                    def high():
                        p, kind = at(HTR)
                        if p is None:
                            return
                        if kind == "routed":
                            act.wait_ge(ht_done, routed(p).at(1, 1))
                        else:
                            act.wait_ge(gelu_done, p.at(1, 1))
                        wait(act, down_done, p.at(1, -1))
                        nc.scalar.activation(flat(hs[:, p.slot(2), 0]), hidden(p, kind), ACT.Copy).then_inc(h_hi, 1)
                    for stage in ((up, high) if at(HTR)[1] == "routed" else (high, up)):
                        stage()
                    p, kind = at(DNS)
                    if kind == "routed":
                        j = routed(p)
                        act.wait_ge(down_done, p.at(1, 1))
                        wait(act, stored[j.slot(4)], j.per(4, 16))
                        nc.scalar.activation(yb[:, j.slot(4), :], yD[p.slot(2)][:, :], ACT.Copy).then_inc(y_out, 1)
                steps2(act, step)

            @block.vector
            def _(dve):
                vec = nc.vector
                n = [0]

                def link(op):
                    n[0] += 1
                    op.then_inc(ch, 1)
                    dve.wait_ge(ch, n[0])
                part = const("part")
                dve.wait_ge(counted, 1)
                vec.scalar_tensor_tensor(out=zrow[:, :], in0=cnt[:, :], scalar=part, in1=const("ebase"),
                                         op0=ALU.add, op1=ALU.add).then_inc(zrows_known, 1)
                link(vec.tensor_scalar(nti[:, :], cnt[:, :], float(P - 1), None, ALU.add))
                link(vec.tensor_scalar(nti[:, :], nti[:, :], 7, None, ALU.arith_shift_right))
                link(vec.tensor_copy(nt[:, :], nti[:, :]))
                link(vec.memset(oneE[:, :], 1.0))
                link(vec.tensor_tensor_scan(out=cum[:, :], data0=oneE[:, :], data1=nt[:, :], initial=0.0,
                                            op0=ALU.mult, op1=ALU.add))
                link(vec.tensor_tensor(cs[:, :], cum[:, :], nt[:, :], ALU.subtract))
                link(vec.scalar_tensor_tensor(out=delta[:, :], in0=cs[:, :], scalar=float(P), in1=const("ebase"),
                                              op0=ALU.mult, op1=ALU.subtract))
                link(vec.scalar_tensor_tensor(out=junk2[:, :], in0=cum[:, :], scalar=part, in1=oneE[:, :],
                                              op0=ALU.is_le, op1=ALU.mult, accum_out=tj[:, 0:1]))
                link(vec.scalar_tensor_tensor(out=junk2[:, :], in0=const("e8"), scalar=tj[:, 0:1], in1=delta[:, :],
                                              op0=ALU.is_equal, op1=ALU.mult, accum_out=tj[:, 1:2]))
                link(vec.scalar_tensor_tensor(out=tj[:, 2:3], in0=part, scalar=float(P), in1=tj[:, 1:2],
                                              op0=ALU.mult, op1=ALU.subtract))
                link(vec.scalar_tensor_tensor(out=tj[:, 3:4], in0=tj[:, 0:1], scalar=float(E), in1=tj[:, 2:3],
                                              op0=ALU.is_lt, op1=ALU.mult))
                vec.scalar_tensor_tensor(out=tj[:, 4:5], in0=tj[:, 0:1], scalar=float(E), in1=tj[:, 0:1],
                                         op0=ALU.is_lt, op1=ALU.mult).then_inc(tiles_known, 1)
                dve.wait_ge(turned, 1)
                vec.tensor_copy(ints[0:1, :], xg_t[0:1, :, :].rearrange("p k n -> p (k n)")[:, 0:2 * NJ]
                                ).then_inc(rows_known, 1)

                def answers_known():
                    link(vec.tensor_tensor(which[:, :, :], const("e8").unsqueeze(1).to_broadcast([P, 2 * T, E]),
                                           IDX[:, :, :].rearrange("p t k -> p (t k)").unsqueeze(2)
                                           .to_broadcast([P, 2 * T, E]), ALU.is_equal))
                    link(vec.tensor_tensor(which[:, :, :], which[:, :, :],
                                           delta[:, :].unsqueeze(1).to_broadcast([P, 2 * T, E]), ALU.mult))
                    link(vec.tensor_reduce(offs[:, :], which[:, :, :], AX.X, ALU.add))
                    vec.tensor_tensor(posk[:, :, :].rearrange("p t k -> p (t k)"),
                                      POS[:, :, :].rearrange("p t k -> p (t k)"), offs[:, :], ALU.add
                                      ).then_inc(posk_done, 1)
                    dve.wait_ge(ex_done, 1)
                    link(vec.tensor_scalar(den[:, :], ex[:, :], 1.0, None, ALU.add))
                    link(vec.reciprocal(den[:, :], den[:, :]))
                    link(vec.tensor_scalar(a12[:, :, 0], den[:, :], gains[:, 1:2], None, ALU.mult))
                    link(vec.tensor_tensor(a12[:, :, 1], ex[:, :], a12[:, :, 0], ALU.mult))

                def row(a, t):
                    return a[:, bass.ds(t.at(1), 1), :].rearrange("p o d -> p (o d)")

                def step(at, m):
                    p, kind = at(XTR)
                    if kind == "routed":
                        j = routed(p)
                        dve.wait_ge(xg_hi, j.at(1, 1))
                        vec.tensor_tensor(xgs[:, j.slot(2), 1], xg_t[:, :, :], xgs[:, j.slot(2), 0], ALU.subtract
                                          ).then_inc(xg_lo, 1)
                    p, kind = at(HTR)
                    if p is not None:
                        dve.wait_ge(h_hi, p.at(1, 1))
                        vec.tensor_tensor(flat(hs[:, p.slot(2), 1]), hidden(p, kind), flat(hs[:, p.slot(2), 0]),
                                          ALU.subtract).then_inc(h_lo, 1)
                    p, kind = at(DNS)
                    if kind == "shared":
                        t = token_tile(p)
                        dve.wait_ge(down_done, p.at(1, 1))
                        vec.scalar_tensor_tensor(out=row(X, t), in0=yD[p.slot(2)][:, :], scalar=gains[:, 1:2],
                                                 in1=row(X, t), op0=ALU.mult, op1=ALU.add).then_inc(s_out, 1)
                    if m is not None:
                        dve.wait_ge(y12[m.slot(4)], m.per(4, 32, 32))
                        dve.wait_ge(s_out, m.at(1, 1))
                        for k, done in ((0, mix1), (1, mixed)):
                            if k:
                                dve.wait_ge(mix1, m.at(1, 1))
                            vec.scalar_tensor_tensor(
                                out=row(X, m), in0=Y12[:, m.slot(4), k, :],
                                scalar=a12[:, bass.ds(m.at(1), 1), k], in1=row(X, m),
                                op0=ALU.mult, op1=ALU.add).then_inc(done, 1)
                steps2(dve, step, answers_known)

            @block.tensor
            def _(pe):
                mm = nc.tensor.matmul
                mm(cnt[:, :], const16("ones"), seen[:, T % 2, :], start=True, stop=True).then_inc(counted, 1)

                def turn():
                    pe.wait_ge(tiles_known, 1)
                    row = xg_t[0:1, :, :].rearrange("p k n -> p (k n)")
                    for k in range(2):
                        z = mm(row[:, k * NJ:k * NJ + NJ], tj[0:NJ, 3 + k:4 + k], const("ident")[0:NJ, 0:NJ],
                               start=True, stop=True)
                    z.then_inc(turned, 1)
                turn()

                regs = [pe.alloc_register(f"expert{k}") for k in range(4)]
                known = {}

                def expert(p, kind):
                    if kind == "shared":
                        return 2 * E
                    j = routed(p)
                    key = (j.c, j.i is None)
                    if key not in known:
                        c = j.c // 4 * 4
                        pe.load(regs, ints[0:1, bass.ds(Idx(c, j.i).at(1, NJ), 4)])
                        for k in range(4):
                            known[c + k, j.i is None] = pe.snap(regs[k], min_val=0, max_val=E - 1)
                    return known[key] * 2

                def unit(a, u):
                    return a[:, bass.ds(u, 1), :].rearrange("p o n -> p (o n)")

                def step(at, m):
                    p, kind = at(XTR)
                    if kind == "routed":
                        j = routed(p)
                        if j.c == 0 and j.i is None:
                            pe.wait_ge(rows_known, 1)
                        pe.wait_ge(xg_in[j.slot(4)], j.per(4, 16, 16))
                        wait(pe, xg_lo, j.at(1))
                        for k in range(KC):
                            z = nc.tensor.transpose(xg_t[:, k, :], xg[:, j.slot(4), P * k:P * k + P], const("ident"))
                        z.then_inc(xgt, 1)
                    p, kind = at(UPS)
                    if p is not None:
                        e = expert(p, kind)
                        if kind == "routed":
                            wait(pe, gelu_done, p.at(1, -1))
                            j = routed(p)
                            pe.wait_ge(xg_lo, j.at(1, 1))
                            xh, xl = ([xgs[:, j.slot(2), a, k, :] for k in range(KC)] for a in range(2))
                        else:
                            wait(pe, h_lo, p.at(1, -1))
                            wait(pe, gelu_done, p.at(1, -1))
                            t = token_tile(p)
                            xt = XT[:, bass.ds(t.at(1), 1)]
                            xh, xl = ([xt[:, :, a, k].rearrange("p o n -> p (o n)") for k in range(KC)]
                                      for a in range(2))
                        if kind == "shared":
                            for f in range(FC):
                                for k in range(KC):
                                    wh, wl = (unit(a, e + (UP + k))[:, P * f:P * f + P] for a in (WFH, WFL))
                                    for q, (st, mo) in enumerate(((wh, xh[k]), (wl, xh[k]), (wh, xl[k]))):
                                        z = mm(hT[p.slot(2)][:, f, :], st, mo, start=k == 0 and q == 0,
                                               stop=k == KC - 1 and q == 2)
                        else:
                            for k in range(KC):
                                wh, wl = unit(WFH, e + (UP + k)), unit(WFL, e + (UP + k))
                                for q, (st, mo) in enumerate(((xh[k], wh), (xh[k], wl), (xl[k], wh))):
                                    z = mm(uA[p.slot(2)][:, :], st, mo, start=k == 0 and q == 0,
                                           stop=k == KC - 1 and q == 2)
                        z.then_inc(up_done, 1)
                    p, kind = at(HTR)
                    if kind == "routed":
                        pe.wait_ge(gelu_done, p.at(1, 1))
                        wait(pe, h_lo, p.at(1, -1))
                        for k in range(FC):
                            z = nc.tensor.transpose(hT[p.slot(2)][:, k, :], g[:, p.slot(2), P * k:P * k + P],
                                                    const("ident"))
                        z.then_inc(ht_done, 1)
                    p, kind = at(DNS)
                    if p is not None:
                        e = expert(p, kind)
                        pe.wait_ge(h_lo, p.at(1, 1))
                        q, was = at(DNS - 2)
                        if was == "routed":
                            pe.wait_ge(y_out, routed(q).at(1, 1))
                        elif was == "shared":
                            pe.wait_ge(s_out, token_tile(q).at(1, 1))
                        for k in range(FC):
                            u, c = e + (DOWN + k // 2), slice(D * (k % 2), D * (k % 2) + D)
                            wh, wl = unit(WFH, u)[:, c], unit(WFL, u)[:, c]
                            hh, hl = (hs[:, p.slot(2), a, k, :] for a in range(2))
                            for q_, (st, mo) in enumerate(((hh, wh), (hh, wl), (hl, wh))):
                                z = mm(yD[p.slot(2)][:, :], st, mo, start=k == 0 and q_ == 0,
                                       stop=k == FC - 1 and q_ == 2)
                        z.then_inc(down_done, 1)
                steps2(pe, step)


def kernel(x, ctx_1024, g_xattn, g_ffn, L0_xattn_W_Q, L0_xattn_W_K, L0_xattn_W_V, L0_xattn_g_w, L0_xattn_g_b,
           L0_xattn_out_w, L0_xattn_out_b, L0_ffn_Wg, L0_ffn_Wu, L0_ffn_Wd, L0_ffn_W1, L0_ffn_W2):
    import concourse.bacc as bacc
    from concourse.bass_utils import run_bass_kernel_spmd

    def heads(w):
        return np.asarray(w).transpose(1, 0, 2).reshape(D, D)

    def rows(w):
        w = np.asarray(w)
        return w.reshape(KC, P, w.shape[1]).transpose(1, 0, 2).reshape(P, -1)

    qkvg = np.concatenate([heads(L0_xattn_W_Q), heads(L0_xattn_W_K), heads(L0_xattn_W_V),
                           np.asarray(L0_xattn_g_w).T], axis=1)
    wa = np.concatenate([rows(qkvg), rows(np.asarray(L0_xattn_out_w).T), rows(L0_ffn_Wg)], axis=1)
    bias = np.concatenate([np.asarray(L0_xattn_g_b), np.asarray(L0_xattn_out_b)])
    bias = np.stack([bias, bias])
    gains = np.stack([np.concatenate([np.asarray(g_xattn), np.asarray(g_ffn)])] * P)
    ups = np.concatenate([np.asarray(L0_ffn_Wu).reshape(2 * E, P, F), np.asarray(L0_ffn_W1).reshape(2, P, F)])
    downs = np.concatenate([np.asarray(L0_ffn_Wd).reshape(2 * E, 2, P, D), np.asarray(L0_ffn_W2).reshape(2, 2, P, D)])
    wf = np.concatenate([ups, downs.transpose(0, 2, 1, 3).reshape(2 * E + 2, P, F)])
    c32, c16 = tables()
    arrays = dict(x=x, ctx=ctx_1024, wa=wa, bias=bias, gains=gains, wf=wf, c32=c32, c16=c16)
    arrays = {f"{k}_in": np.ascontiguousarray(np.asarray(v)) for k, v in arrays.items()}

    nc = bacc.Bacc("TRN2", target_bir_lowering=False, num_devices=1)
    args = [nc.dram_tensor(n, a.shape, mybir.dt.from_np(a.dtype), kind="ExternalInput").ap()
            for n, a in arrays.items()]
    out = nc.dram_tensor("out", (B, L, D), F32, kind="ExternalOutput").ap()
    build(nc, *args, out)
    r = run_bass_kernel_spmd(nc, [arrays], core_ids=[0])
    return r.results[0]["out"]
```

```python
from contextlib import ExitStack

import numpy as np

import concourse.bass as bass
from concourse import mybir

F32, F16 = mybir.dt.float32, mybir.dt.float16
I32, U32 = mybir.dt.int32, mybir.dt.uint32
ALU, ACT, AX = mybir.AluOpType, mybir.ActivationFunctionType, mybir.AxisListType

P = 128
B, L, D, H = 16, 256, 256, 16
HD = D // H
T = B * L // P
KC = D // P
E, F = 8, 512
FC = F // P
CPB = L // P
WS = 256.0
QS = 16.0
LN_EPS = 1e-5
GN_EPS = 1e-5 * (QS * QS) ** 2
CAP = T * P + P
NJ = 2 * T + E
NU = (E + 1) * 4
UP, DOWN = 0, 2 * (E + 1)
ND = 6
UNROLL = 4


class Idx:

    def __init__(self, c, i=None, n=UNROLL):
        self.c, self.i, self.n = c, i, n

    def at(self, m, k=0):
        v = m * self.c + k
        return v if self.i is None else self.i * (self.n * m) + v

    def per(self, d, m, k=0):
        v = m * (self.c // d) + k
        return v if self.i is None else self.i * (self.n // d * m) + v

    def slot(self, d):
        return self.c % d

    def __add__(self, k):
        return Idx(self.c + k, self.i, self.n)


def tables():
    f = np.float32
    half = HD // 2
    base = ((np.arange(0, HD, 2).astype(f) + f(0.4 * HD)) / f(1.4 * HD)).astype(np.float64)
    power = ((np.arange(L) - L // 2).astype(f) / f(512.0)).astype(np.float64)
    scale = base[None, :] ** power[:, None]
    inv_freq = (f(1.0) / f(10000.0) ** (np.arange(half).astype(f) / f(half))).astype(f)
    ang = (np.arange(L).astype(f)[:, None] * inv_freq[None, :]).astype(np.float64)
    g0 = np.linspace(np.log(1.0 / 32.0), np.log(1.0 / 512.0), H).astype(f)
    gamma = (f(1.0) - np.exp(g0)).astype(np.float64)
    local = np.arange(L) % P - P // 2
    cos, sin = [], []
    for sign in (1, -1):
        s = scale ** sign
        decay = gamma[None, :] ** (sign * local[:, None])
        amp = decay[:, :, None, None] * s[:, None, :, None] * (QS / WS)
        c = amp * np.cos(ang)[:, None, :, None] * np.ones((1, 1, 1, 2))
        n = amp * np.sin(ang)[:, None, :, None] * np.array([-1.0, 1.0])
        cos.append(c.reshape(L, D))
        sin.append(n.reshape(L, D))
    cos = np.concatenate(cos, 1).reshape(CPB, P, 2 * D).transpose(1, 0, 2)
    sin = np.concatenate(sin, 1).reshape(CPB, P, 2 * D).transpose(1, 0, 2)
    row = np.arange(P) // 64
    smask = np.zeros((P, H // 2, 2, HD))
    for g in range(H // 2):
        for a in range(2):
            smask[row == a, g, a, :] = gamma[2 * g + a] ** P
    tri = (np.arange(P)[None, :] >= np.arange(P)[:, None])
    before = (np.arange(P)[:, None] < np.arange(P)[None, :])
    e8 = np.arange(E)
    c32 = [cos.reshape(P, -1), sin.reshape(P, -1), smask.reshape(P, -1), tri, np.eye(P),
           np.tile(e8, (P, 1)), np.tile(e8 * CAP, (P, 1)), np.arange(P)[:, None],
           np.eye(P)[:, :2]]
    c16 = [np.eye(P), before, np.ones((P, P))]
    return (np.ascontiguousarray(np.concatenate(c32, 1).astype(np.float32)),
            np.ascontiguousarray(np.concatenate(c16, 1).astype(np.float16)))


C32 = dict(cos=CPB * 2 * D, sin=CPB * 2 * D, smask=D, tri=P, ident=P, e8=E, ebase=E, part=1, pick=2)
C16 = dict(ident=P, before=P, ones=P)
NQKVG = 4 * D
WA = dict(qkvg=KC * NQKVG, out=KC * D, gate=KC * E)


def cuts(widths):
    at, out = 0, {}
    for name, n in widths.items():
        out[name] = slice(at, at + n)
        at += n
    return out, at


def build(nc, x_d, ctx_d, wa_d, bias_d, gains_d, wf_d, c32_d, c16_d, out_d):
    cut32, n32 = cuts(C32)
    cut16, n16 = cuts(C16)
    cuta, na = cuts(WA)
    x_v = x_d.rearrange("b (c p) d -> (b c) p d", p=P)
    ctx_v = ctx_d.rearrange("b (c p) d -> (b c) p d", p=P)
    out_v = out_d.rearrange("b (c p) d -> (b c) p d", p=P)
    by_expert = nc.dram_tensor("rows_by_expert", [E * CAP, D], F32).ap()
    answers = nc.dram_tensor("answers", [NJ * P, D], F32).ap()

    with ExitStack() as ctx:
        def sb(name, shape, dt=F32, c=ctx):
            return c.enter_context(nc.sbuf_tensor(name, shape, dt))

        def ps(name, shape, dt=F32, c=ctx):
            return c.enter_context(nc.psum_tensor(name, shape, dt))

        def sem(name):
            return ctx.enter_context(nc.semaphore(name))

        def wait(eng, s, value):
            if not isinstance(value, int) or value > 0:
                eng.wait_ge(s, value)

        X = sb("X", [P, T, D])
        XT = sb("XT", [P, T, 2, KC, P], F16)
        WFH = sb("WFH", [P, NU, F], F16)
        WFL = sb("WFL", [P, NU, F], F16)
        c32 = sb("c32", [P, n32 - 2 * CPB * 2 * D])
        c16 = sb("c16", [P, n16], F16)
        gains = sb("gains", [P, 2])
        IDX = sb("IDX", [P, T, 2])
        POS = sb("POS", [P, T, 2])
        GAP = sb("GAP", [P, T])
        seen = sb("seen", [P, 2, E], F16)
        shift = CPB * 4 * D

        def const(name):
            c = cut32[name]
            return c32[:, c.start - shift:c.stop - shift]

        def const16(name):
            return c16[:, cut16[name]]

        with ExitStack() as c1:
            s1 = lambda name, shape, dt=F32: sb(name, shape, dt, c1)
            rot = s1("rot", [P, 2, CPB, 2 * D])
            WAH = s1("WAH", [P, na], F16)
            WAL = s1("WAL", [P, na], F16)
            biasw = s1("biasw", [P, 2 * D], F16)
            ctxb = s1("ctxb", [P, 2, D])
            stage = s1("stage", [P, 2, F])
            xn = s1("xn", [P, 2, D])
            xcs = s1("xcs", [P, 2, 2 * KC, P], F16)
            QKC = s1("QKC", [P, na - KC * NQKVG])
            swp = s1("swp", [P, 2 * D])
            q4 = s1("q4", [P, 2, H, 4, HD], F16)
            QT = s1("QT", [P, H // 2, P], F16)
            KT = s1("KT", [P, H // 2, P], F16)
            sim = s1("sim", [P, H, P])
            V = s1("V", [P, 2, H // 2, 4, HD])
            rT = s1("rT", [P, KC, P])
            sq = s1("sq", [P, D])
            G = s1("G", [P, 2, D])
            y = s1("y", [P, 2, D])
            ys = s1("ys", [P, 2, KC, P], F16)
            S4 = s1("S4", [P, 2, D], F16)
            VS = s1("VS", [P, 2, D], F16)
            xn2 = s1("xn2", [P, 4, D])
            st6 = s1("st6", [P, 2, 6])
            mv = s1("mv", [P, 2, 2, 2])
            NPW = H + 2
            pin = s1("pin", [P, 2, NPW])
            pout = s1("pout", [P, 2, NPW])
            pexp = s1("pexp", [P, NPW])
            nm = s1("nm", [P, 2, 2])
            m8 = s1("m8", [P, E])
            i8 = s1("i8", [P, E], U32)
            ix = s1("ix", [P, 4, 2])
            one1 = s1("one1", [P, E])
            gap1 = s1("gap1", [P, 4])
            hot = s1("hot", [P, E], F16)
            rk = s1("rk", [P, E])
            junk = s1("junk", [P, 2, E])
            pos2 = s1("pos2", [P, 4, 2])
            posi = s1("posi", [P, 4, 2], I32)
            vmean = s1("vmean", [P, KC, H])
            bstage = [a[0:2, :, :].rearrange("p a n -> p (a n)") for a in (y, G)]
            wstage = sim[:, :, :].rearrange("p h n -> p (h n)")
            wstage2 = QKC[:, :]

            bT = ps("bT", [P, 2 * KC, P], F32, c1)
            bQK = ps("bQK", [P, 2 * D], F32, c1)
            bVG = ps("bVG", [P, 2 * D], F32, c1)
            bQT = ps("bQT", [P, H // 2, P], F16, c1)
            bS = [ps(f"bS{a}", [P, 4, P], F32, c1) for a in range(2)]
            bR = ps("bR", [P, 2 * D], F32, c1)
            bY = ps("bY", [P, 2 * D], F32, c1)
            bRT = bR[:, 0:D].rearrange("p (c n) -> p c n", c=KC)
            ret = bR[:, D:2 * D]
            Sm = swp[:, 0:D]
            f_hT = [a[:, :] for a in (bQK, bVG)]
            f_g = [rot[:, 0, k, :] for k in range(2)]
            f_hs = [rot[:, 1, k, :].bitcast(F16).rearrange("p (a n) -> p a n", a=2) for k in range(2)]
            f_y = [bT[:, 0:KC, :].rearrange("p k n -> p (k n)"), bS[0][:, 0:KC, :].rearrange("p k n -> p (k n)")]
            bSt = bQT[:, :, :].rearrange("p h n -> p (h n)").bitcast(F32)[:, 0:D]

            consts_in, c16_in, gains_in, rot_in = sem("consts_in"), sem("c16_in"), sem("gains_in"), sem("rot_in")
            wa_in, wo_in = sem("wa_in"), sem("wo_in")
            x_in = [sem(f"x_in{k}") for k in range(4)]
            ctx_in = [sem(f"ctx_in{k}") for k in range(2)]
            w_in = [sem(f"w_in{k}") for k in range(2)]
            prep_v, prep_a = sem("prep_v"), sem("prep_a")
            prep_p, gained = sem("prep_p"), sem("gained")
            stats_in = sem("stats_in")
            dve_chain = sem("dve_chain")
            aggr = sem("aggr")
            var_ready = sem("var_ready")
            rstd, rstd_h = sem("rstd"), sem("rstd_h")
            nm1, nm2 = sem("nm1"), sem("nm2")
            xn_done, xn2_done = sem("xn_done"), sem("xn2_done")
            t1 = sem("t1")
            xc_hi, xc_lo = sem("xc_hi"), sem("xc_lo")
            proj_qk, proj_vg = sem("proj_qk"), sem("proj_vg")
            rotc, rots, rotated = sem("rotc"), sem("rots"), sem("rotated")
            v_done, g_done = sem("v_done"), sem("g_done")
            hi4, lo4, dup4 = sem("hi4"), sem("lo4"), sem("dup4")
            qt, kt = sem("qt"), sem("kt")
            qt_out, kt_out = sem("qt_out"), sem("kt_out")
            scored, masked = sem("scored"), sem("masked")
            vs_hi, vs_done = sem("vs_hi"), sem("vs_done")
            qs_done, pvh, pvt, rt_out = sem("qs_done"), sem("pvh"), sem("pvt"), sem("rt_out")
            copied, masked_p = sem("copied"), sem("masked_p")
            stated, sm_done, s4_hi, s4_done = sem("stated"), sem("sm_done"), sem("s4_hi"), sem("s4_done")
            pv = sem("pv")
            sq_done, rg_done, y_done = sem("sq_done"), sem("rg_done"), sem("y_done")
            ss_done = sem("ss_done")
            yt, x2t = sem("yt"), sem("x2t")
            y_hi, y_lo, x2_hi, x2_lo = sem("y_hi"), sem("y_lo"), sem("x2_hi"), sem("x2_lo")
            outp, x2_done = sem("outp"), sem("x2_done")
            logit, hot_done, ranked, pos_done = sem("logit"), sem("hot_done"), sem("ranked"), sem("pos_done")
            top8, top_ix, ixf, one_done, seen_done = (
                sem("top8"), sem("top_ix"), sem("ixf"), sem("one_done"), sem("seen_done"))
            gap_done = sem("gap_done")
            rk_done, pos_f = sem("rk_done"), sem("pos_f")
            scat = [sem(f"scat{k}") for k in range(4)]
            f_up, f_gelu, f_hi, f_lo, f_down, f_out = (
                sem("f_up"), sem("f_gelu"), sem("f_hi"), sem("f_lo"), sem("f_down"), sem("f_out"))
            w_scaled, w_hi, w_lo = sem("w_scaled"), sem("w_hi"), sem("w_lo")

            FIRST, LAST = -4, 37
            LOOP = (8, 28)
            LN1, XN, PROJ, ROT, SCORE, PV, YY, YT, OUT, XN2, X2T, ROUTE, SCAT = (
                4, 3, 2, 1, 0, -1, -2, -3, -4, -4, -5, -6, -6)

            def steps(eng, step, before={}):
                def straight(s):
                    step(lambda k: Idx(s + k) if 0 <= s + k < T else None, s)
                for s in range(FIRST, LOOP[0]):
                    if s in before:
                        before[s]()
                    straight(s)
                with eng.Fori(0, (LOOP[1] - LOOP[0]) // UNROLL) as i:
                    for u in range(UNROLL):
                        step(lambda k, u=u: Idx(LOOP[0] + u + k, i), None)
                for s in range(LOOP[1], LAST + 1):
                    straight(s)

            def so_far(stages, tile_of, s):
                if s is not None:
                    return sum(min(max(s + k + 1, 0), T) for k in stages)
                z = [tile_of(k) for k in stages]
                return z[0].i * (UNROLL * len(z)) + sum(k.c + 1 for k in z)

            def heads_of(a):
                return a.rearrange("p (g a e) -> p g a e", a=2, e=HD)

            def drain(s, half):
                k = 2 * (s - T) + half if s is not None else -1
                return k if 0 <= k < ND else None, k - 1 if 1 <= k <= ND else None

            def unit_of(tile_of, s, after=0):
                if s is None:
                    return tile_of(LN1) + -after
                s -= after
                return Idx(s - FIRST) if 0 <= s - FIRST < NU else None

            def stat_step(tile_of, s):
                if s is None:
                    return tile_of(LN1)
                return Idx(s - FIRST) if s - FIRST < T + 8 else None

            CENTRED = 8 + 2 * KC

            def qkvg(a, half):
                return a[:, 0:KC * NQKVG].rearrange("p (k a n) -> p k a n", k=KC, a=2)[:, :, half]

            block = c1.enter_context(nc.Block())

            @block.sync
            def _(sp):
                def constants():
                    sp.dma_start(gains[:, :], gains_d).then_inc(gains_in, 16)
                    sp.dma_start(bstage[0], bias_d).then_inc(consts_in, 16)
                    sp.dma_start(c32[:, :], c32_d[:, shift:]).then_inc(consts_in, 16)
                    sp.dma_start(wstage[:, 0:KC * NQKVG], wa_d[:, 0:KC * NQKVG]).then_inc(wa_in, 16)
                    sp.dma_start(wstage2[:, 0:na - KC * NQKVG], wa_d[:, KC * NQKVG:na]).then_inc(wo_in, 16)
                    sp.dma_start(c16[:, :], c16_d).then_inc(c16_in, 16)

                def rotations():
                    sp.dma_start(rot[:, :, :, :].rearrange("p a c n -> p (a c n)"), c32_d[:, 0:shift]
                                 ).then_inc(rot_in, 16)

                def step(tile_of, s):
                    t = tile_of(LN1)
                    if t is not None:
                        wait(sp, x_in[t.slot(4)], t.per(4, 16))
                        sp.dma_start(X[:, bass.ds(t.at(1), 1), :], x_v[bass.ds(t.at(1), 1)].rearrange("o p d -> p o d")
                                     ).then_inc(x_in[t.slot(4)], 16)
                    u = unit_of(tile_of, s)
                    if u is not None:
                        wait(sp, w_lo, u.at(1, -1))
                        sp.dma_start(stage[:, u.slot(2), :], wf_d[bass.ds(u.at(1), 1)].rearrange("o p n -> p (o n)")
                                     ).then_inc(w_in[u.slot(2)], 16)
                    if t is not None:
                        wait(sp, t1, t.at(1, -1))
                        sp.dma_start(ctxb[:, t.slot(2), :], ctx_v[bass.ds(t.at(1), 1)].rearrange("o p d -> p (o d)")
                                     ).then_inc(ctx_in[t.slot(2)], 16)
                steps(sp, step, {FIRST + 1: constants, FIRST + 2: rotations})

            @block.gpsimd
            def _(pool):
                nc.gpsimd.memset(pexp[:, :], -0.5).then_inc(prep_p, 1)
                nc.gpsimd.memset(pin[:, :, :], 1.0).then_inc(prep_p, 1)
                nc.gpsimd.memset(V[:, :, :, :, :], 0.0).then_inc(prep_p, 1)
                pool.wait_ge(prep_p, 2)

                def step(tile_of, s):
                    n = stat_step(tile_of, s)
                    if n is not None and (n.i is not None or n.c >= 1):
                        m = n + -1
                        pool.wait_ge(var_ready, m.at(1, 1))
                        for k, used in ((XN, xn_done), (XN2, xn2_done)):
                            if tile_of(k - 2) is not None:
                                pool.wait_ge(used, tile_of(k - 2).at(1, 1))
                        heads = H if tile_of(PV - 1) is not None else 1
                        for a, b, done in ((H, NPW, rstd), (0, heads, rstd_h)):
                            nc.gpsimd.tensor_tensor(pout[:, m.slot(2), a:b], pin[:, m.slot(2), a:b], pexp[:, a:b],
                                                    ALU.pow).then_inc(done, 1)
                    t = tile_of(YY)
                    if t is not None:
                        pool.wait_ge(rg_done, t.at(1, 1))
                        pool.wait_ge(rstd_h, n.at(1))
                        nc.gpsimd.tensor_tensor(
                            y[:, t.slot(2), :].rearrange("p (h e) -> p h e", h=H),
                            y[:, t.slot(2), :].rearrange("p (h e) -> p h e", h=H),
                            pout[:, (n + -1).slot(2), 0:H].unsqueeze(2).to_broadcast([P, H, HD]),
                            ALU.mult).then_inc(y_done, 1)
                    t = tile_of(ROT)
                    if t is not None and t.c % 2 == 0:
                        pool.wait_ge(vs_hi, t.per(2, 1, 1))
                        nc.gpsimd.tensor_tensor(heads_of(VS[:, 1, :]), V[:, t.slot(2), :, 0::3, :], heads_of(VS[:, 0, :]), ALU.subtract
                                                ).then_inc(vs_done, 1)
                    t = tile_of(SCORE)
                    if t is not None:
                        pool.wait_ge(copied, t.at(1, 1))
                        nc.gpsimd.tensor_tensor(sim[:, 9:16:2, :], sim[:, 9:16:2, :],
                                                const("tri").unsqueeze(1).to_broadcast([P, 4, P]), ALU.mult
                                                ).then_inc(masked_p, 1)
                    u = unit_of(tile_of, s, 1)
                    if u is not None:
                        pool.wait_ge(w_hi, u.at(1, 1))
                        c = tile_of(SCAT)
                        if c is not None:
                            pool.wait_ge(pos_done, c.at(1, 1))
                            pool.wait_ge(xn2_done, c.at(1, 1))
                        nc.gpsimd.tensor_tensor(WFL[:, bass.ds(u.at(1), 1), :].rearrange("p o n -> p (o n)"),
                                                stage[:, u.slot(2), :],
                                                WFH[:, bass.ds(u.at(1), 1), :].rearrange("p o n -> p (o n)"),
                                                ALU.subtract).then_inc(w_lo, 1)
                    t = tile_of(PROJ)
                    if t is not None:
                        pool.wait_ge(rots, t.at(1, 1))
                        nc.gpsimd.tensor_tensor(QKC[:, 0:2 * D], QKC[:, 0:2 * D], swp[:, :], ALU.add
                                                ).then_inc(rotated, 1)
                    t = tile_of(SCAT)
                    if t is not None:
                        if u is None:
                            pool.wait_ge(pos_done, t.at(1, 1))
                            pool.wait_ge(xn2_done, t.at(1, 1))
                        for k in range(2):
                            pool.indirect_dma_start(
                                by_expert[:, :], bass.IndirectOffsetOnAxis(ap=posi[:, t.slot(4), k:k + 1], axis=0),
                                xn2[:, t.slot(4), :], None).then_inc(scat[t.slot(4)], 16)
                steps(pool, step)
                for k in range(4):
                    pool.wait_ge(scat[k], 2 * 16 * (T // 4))

            @block.scalar
            def _(act):
                act.wait_ge(gains_in, 16)
                nc.scalar.activation(gains[:, :], gains[:, :], ACT.Tanh).then_inc(gained, 1)

                def weights():
                    act.wait_ge(prep_p, 3)
                    act.wait_ge(wa_in, 16)
                    nc.scalar.activation(qkvg(WAH, 0), qkvg(wstage, 0), ACT.Copy, scale=WS).then_inc(prep_a, 1)
                    act.wait_ge(dve_chain, CENTRED)
                    nc.scalar.activation(qkvg(WAH, 1), qkvg(wstage, 1), ACT.Copy, scale=WS).then_inc(prep_a, 1)
                    act.wait_ge(wo_in, 16)
                    nc.scalar.activation(WAH[:, KC * NQKVG:na], wstage2[:, 0:na - KC * NQKVG], ACT.Copy, scale=WS
                                         ).then_inc(prep_a, 1)

                def shared_hidden(s, half):
                    d, _ = drain(s, half)
                    if d is not None:
                        act.wait_ge(f_up, d + 1)
                        act.wait_ge(rots, T)
                        wait(act, f_lo, d - 1)
                        nc.scalar.activation(f_g[d % 2], f_hT[d % 2], ACT.Gelu, scale=1.0 / WS).then_inc(f_gelu, 1)
                        act.wait_ge(f_gelu, d + 1)
                        wait(act, f_down, d - 1)
                        nc.scalar.activation(f_hs[d % 2][:, 0, :], f_g[d % 2], ACT.Copy).then_inc(f_hi, 1)

                def step(tile_of, s):
                    n = stat_step(tile_of, s)
                    t = tile_of(PROJ)
                    if t is not None:
                        act.wait_ge(t1, t.at(1, 1))
                        wait(act, proj_vg, t.at(1))
                        nc.scalar.activation(xcs[:, 0], bT[:, :, :], ACT.Copy).then_inc(xc_hi, 1)
                    t = tile_of(SCORE)
                    if t is not None:
                        act.wait_ge(qt, t.at(1, 1))
                        wait(act, scored, t.at(2))
                        if t.c % 2 == 0:
                            wait(act, qs_done, t.per(2, 1))
                        nc.scalar.activation(QT[:, :, :], bQT[:, :, :], ACT.Copy).then_inc(qt_out, 1)
                    u = unit_of(tile_of, s, 1)
                    if u is not None:
                        act.wait_ge(w_in[u.slot(2)], u.per(2, 16, 16))
                        nc.scalar.activation(stage[:, u.slot(2), :], stage[:, u.slot(2), :], ACT.Copy, scale=WS
                                             ).then_inc(w_scaled, 1)
                    if t is not None:
                        act.wait_ge(kt, t.at(1, 1))
                        nc.scalar.activation(KT[:, :, :], bQT[:, :, :], ACT.Copy).then_inc(kt_out, 1)
                    w = tile_of(ROT)
                    if w is not None:
                        act.wait_ge(rotated, w.at(1, 1))
                        wait(act, kt, w.at(1))
                        if w.c % 2:
                            act.wait_ge(stated, w.per(2, 1, 1))
                        r = QKC[:, 0:2 * D].rearrange("p (a h e) -> p a h e", a=2, h=H)
                        for a, at in ((0, q4[:, 0, :, 0::2, :]), (1, q4[:, 1, :, 0:2, :])):
                            nc.scalar.activation(at, r[:, a].unsqueeze(2).to_broadcast([P, H, 2, HD]),
                                                 ACT.Copy).then_inc(hi4, 1)
                    shared_hidden(s, 0)
                    t = tile_of(PV)
                    if t is not None:
                        act.wait_ge(pvt, t.at(1, 1))
                        wait(act, pv, t.at(1))
                        nc.scalar.activation(rT[:, :, :], bRT, ACT.Copy).then_inc(rt_out, 1)
                    if w is not None:
                        act.wait_ge(proj_vg, w.at(1, 1))
                        wait(act, pvt, w.at(1, -1))
                        nc.scalar.activation(V[:, w.slot(2), :, 0::3, :], heads_of(bVG[:, 0:D]), ACT.Copy,
                                             scale=1.0 / WS).then_inc(v_done, 1)
                        if w.c % 2 == 0:
                            act.wait_ge(v_done, w.at(1, 1))
                            wait(act, stated, w.per(2, 1))
                            nc.scalar.activation(heads_of(VS[:, 0, :]), V[:, w.slot(2), :, 0::3, :], ACT.Copy
                                                 ).then_inc(vs_hi, 1)
                    if u is not None:
                        act.wait_ge(w_scaled, u.at(1, 1))
                        nc.scalar.activation(WFH[:, bass.ds(u.at(1), 1), :].rearrange("p o n -> p (o n)"),
                                             stage[:, u.slot(2), :], ACT.Copy).then_inc(w_hi, 1)
                    if w is not None:
                        wait(act, rg_done, w.at(1, -1))
                        nc.scalar.activation(G[:, w.slot(2), :], bVG[:, D:2 * D], ACT.Silu, scale=1.0 / WS
                                             ).then_inc(g_done, 1)
                    t = tile_of(PV)
                    if t is not None:
                        act.wait_ge(rg_done, t.at(1, 1))
                        wait(act, ss_done, t.at(1))
                        nc.scalar.activation(sq[:, :], ret, ACT.Square).then_inc(sq_done, 1)
                    t = tile_of(XN)
                    if t is not None:
                        act.wait_ge(nm1, t.at(1, 1))
                        wait(act, t1, t.at(1, -1))
                        nc.scalar.activation(xn[:, t.slot(2), :], X[:, bass.ds(t.at(1), 1), :].rearrange("p o d -> p (o d)"),
                                             ACT.Identity, bias=nm[:, 0, t.slot(2):t.slot(2) + 1],
                                             scale=pout[:, (n + -1).slot(2), H + 1:H + 2]).then_inc(xn_done, 1)
                    r, t = tile_of(X2T), tile_of(YT)
                    if r is not None:
                        act.wait_ge(x2t, r.at(1, 1))
                    if t is not None:
                        act.wait_ge(yt, t.at(1, 1))
                        wait(act, outp, t.at(1))
                        nc.scalar.activation(ys[:, 0], bY[:, 0:D].rearrange("p (k n) -> p k n", k=KC),
                                             ACT.Copy).then_inc(y_hi, 1)
                    if r is not None:
                        nc.scalar.activation(XT[:, bass.ds(r.at(1), 1), 0].rearrange("p o k n -> p (o k n)"),
                                             bY[:, D:2 * D], ACT.Copy).then_inc(x2_hi, 1)
                    t = tile_of(SCORE)
                    if t is not None:
                        act.wait_ge(scored, t.at(2, 2))
                        wait(act, pvt, t.at(1))
                        nc.scalar.activation(sim[:, 9:16:2, :], bS[1][:, :, :], ACT.Copy).then_inc(copied, 1)
                    t = tile_of(XN2)
                    if t is not None:
                        act.wait_ge(nm2, t.at(1, 1))
                        wait(act, scat[t.slot(4)], t.per(4, 32))
                        nc.scalar.activation(xn2[:, t.slot(4), :], X[:, bass.ds(t.at(1), 1), :].rearrange("p o d -> p (o d)"),
                                             ACT.Identity, bias=nm[:, 1, t.slot(2):t.slot(2) + 1],
                                             scale=pout[:, (n + -1).slot(2), H:H + 1]).then_inc(xn2_done, 1)
                    shared_hidden(s, 1)
                steps(act, step, {FIRST + 2: weights})

            @block.vector
            def _(dve):
                vec = nc.vector
                def biases():
                    dve.wait_ge(consts_in, 2 * 16)
                    vec.memset(biasw[:, :], 0.0).then_inc(dve_chain, 1)
                    vec.memset(seen[:, :, :], 0.0).then_inc(dve_chain, 1)
                    b0, b1 = bstage
                    vec.tensor_scalar(b0, b0, WS, None, ALU.mult).then_inc(dve_chain, 1)
                    dve.wait_ge(dve_chain, 3)
                    vec.tensor_copy(biasw[0:2, :], b0).then_inc(dve_chain, 1)
                    dve.wait_ge(dve_chain, 4)
                    vec.tensor_tensor(b1, b0, biasw[0:2, :], ALU.subtract).then_inc(dve_chain, 1)
                    dve.wait_ge(dve_chain, 5)
                    vec.tensor_scalar(b1, b1, const("pick")[0:2, 1:2], None, ALU.mult).then_inc(dve_chain, 1)
                    dve.wait_ge(dve_chain, 6)
                    vec.scalar_tensor_tensor(out=biasw[0:2, :], in0=biasw[0:2, :], scalar=const("pick")[0:2, 0:1],
                                             in1=b1, op0=ALU.mult, op1=ALU.add).then_inc(dve_chain, 1)
                    dve.wait_ge(gained, 1)
                    vec.tensor_scalar(gains[:, :], gains[:, :], 1.0 / WS, None, ALU.mult).then_inc(dve_chain, 1)

                def weights():
                    biases()
                    dve.wait_ge(wa_in, 16)
                    wv = wstage[:, 0:KC * NQKVG].rearrange("p (k a h e) -> p k a h e", k=KC, a=4, h=H)
                    for k in range(KC):
                        vec.tensor_reduce(vmean[:, k, :], wv[:, k, 2], AX.X, ALU.add).then_inc(dve_chain, 1)
                    dve.wait_ge(dve_chain, CENTRED - KC)
                    for k in range(KC):
                        vec.scalar_tensor_tensor(out=wv[:, k, 2],
                                                 in0=vmean[:, k, :].unsqueeze(2).to_broadcast([P, H, HD]),
                                                 scalar=-1.0 / HD, in1=wv[:, k, 2], op0=ALU.mult, op1=ALU.add
                                                 ).then_inc(dve_chain, 1)
                    for k in range(2):
                        dve.wait_ge(prep_a, k + 1)
                        vec.scalar_tensor_tensor(out=qkvg(WAL, k), in0=qkvg(wstage, k), scalar=WS, in1=qkvg(WAH, k),
                                                 op0=ALU.mult, op1=ALU.subtract).then_inc(prep_v, 1)
                    dve.wait_ge(prep_a, 3)
                    dve.wait_ge(wo_in, 16)
                    vec.scalar_tensor_tensor(out=WAL[:, KC * NQKVG:na], in0=wstage2[:, 0:na - KC * NQKVG], scalar=WS,
                                             in1=WAH[:, KC * NQKVG:na], op0=ALU.mult, op1=ALU.subtract
                                             ).then_inc(prep_v, 1)
                dve.wait_ge(prep_p, 2)

                def row(a, t):
                    return a[:, bass.ds(t.at(1), 1), :].rearrange("p o d -> p (o d)")

                def group(a, t):
                    return a[:, bass.ds(t.at(1, -3), 4), :]

                def mask_round(t, r):
                    dve.wait_ge(scored, t.at(2, r + 1))
                    wait(dve, pvt if r else pvh, t.at(1))
                    for a in range(2 - r):
                        vec.tensor_tensor(sim[:, 8 * r + a:8 * r + 8:2, :], bS[a][:, :, :],
                                          const("tri").unsqueeze(1).to_broadcast([P, 4, P]), ALU.mult
                                          ).then_inc(masked, 1)

                def shared_hidden(s, half):
                    d, e = drain(s, half)
                    if d is not None:
                        dve.wait_ge(f_hi, d + 1)
                        vec.tensor_tensor(f_hs[d % 2][:, 1, :], f_g[d % 2], f_hs[d % 2][:, 0, :], ALU.subtract
                                          ).then_inc(f_lo, 1)
                    if e is not None:
                        dve.wait_ge(f_down, e + 1)
                        dve.wait_ge(xn2_done, e + 1)
                        vec.scalar_tensor_tensor(out=X[:, e, :], in0=f_y[e % 2], scalar=gains[:, 1:2],
                                                 in1=X[:, e, :], op0=ALU.mult, op1=ALU.add).then_inc(f_out, 1)

                def step(tile_of, s):
                    n = stat_step(tile_of, s)
                    if n is not None:
                        wait(dve, rstd_h, n.at(1, -1))
                    w = tile_of(ROT)
                    t = tile_of(PROJ)
                    if t is not None:
                        dve.wait_ge(xc_hi, t.at(1, 1))
                        vec.tensor_tensor(xcs[:, 1], bT[:, :, :], xcs[:, 0], ALU.subtract).then_inc(xc_lo, 1)
                    t, r, q, p = tile_of(OUT), tile_of(ROUTE), tile_of(LN1 - 1), tile_of(PV - 1)
                    m = n + -1 if n is not None and (n.i is not None or n.c >= 1) else None
                    if m is not None and q is not None:
                        dve.wait_ge(x_in[q.slot(4)], q.per(4, 16, 16))
                    if t is not None:
                        dve.wait_ge(outp, t.at(1, 1))
                        if r is not None:
                            dve.wait_ge(logit, r.at(1, 1))
                        vec.scalar_tensor_tensor(out=row(X, t), in0=bY[:, 0:D], scalar=gains[:, 0:1], in1=row(X, t),
                                                 op0=ALU.mult, op1=ALU.add).then_inc(x2_done, 1)
                    if r is not None:
                        if t is None:
                            dve.wait_ge(logit, r.at(1, 1))
                        vec.max(m8[:, :], bY[:, D:D + E]).then_inc(top8, 1)
                    if m is not None and q is not None:
                        vec.bn_stats(st6[:, 0, :], row(X, q)).then_inc(stats_in, 1)
                    if t is not None:
                        dve.wait_ge(x2_done, t.at(1, 1))
                    if r is not None:
                        dve.wait_ge(top8, r.at(1, 1))
                        vec.tensor_tensor(gap1[:, r.slot(4):r.slot(4) + 1], m8[:, 1:2], m8[:, 0:1], ALU.subtract
                                          ).then_inc(gap_done, 1)
                        vec.max_index(i8[:, :], m8[:, :], bY[:, D:D + E]).then_inc(top_ix, 1)
                    if m is not None and t is not None:
                        vec.bn_stats(st6[:, 1, :], row(X, t)).then_inc(stats_in, 1)
                    if r is not None:
                        dve.wait_ge(top_ix, r.at(1, 1))
                        vec.tensor_copy(ix[:, r.slot(4), :], i8[:, 0:2]).then_inc(ixf, 1)
                    if m is not None and p is not None:
                        dve.wait_ge(ss_done, p.at(1, 1))
                        z = vec.tensor_scalar(pin[:, m.slot(2), 0:H], pin[:, m.slot(2), 0:H], 1.0 / HD, GN_EPS,
                                              ALU.mult, ALU.add)
                    if r is not None:
                        dve.wait_ge(ixf, r.at(1, 1))
                        vec.tensor_scalar(one1[:, :], const("e8"), ix[:, r.slot(4), 0:1], None, ALU.is_equal
                                          ).then_inc(one_done, 1)
                        if r.c % 4 == 3:
                            vec.tensor_copy(group(IDX, r), ix[:, :, :])
                            dve.wait_ge(gap_done, r.at(1, 1))
                            vec.tensor_copy(GAP[:, bass.ds(r.at(1, -3), 4)], gap1[:, :])
                    if m is not None and (t is not None or q is not None):
                        dve.wait_ge(stats_in, so_far((LN1 - 1, OUT), tile_of, s))
                        if p is None:
                            vec.tensor_copy(junk[:, 0, 0:1], st6[:, 0, 0:1])
                    if r is not None:
                        dve.wait_ge(one_done, r.at(1, 1))
                        vec.scalar_tensor_tensor(out=hot[:, :], in0=const("e8"), scalar=ix[:, r.slot(4), 1:2],
                                                 in1=one1[:, :], op0=ALU.is_equal, op1=ALU.add).then_inc(hot_done, 1)
                    if m is not None:
                        if t is not None or q is not None:
                            for k, w_ in ((1, t), (0, q)):
                                if w_ is not None:
                                    vec.bn_aggr(mv[:, k, w_.slot(2), :], st6[:, k, :]).then_inc(aggr, 1)
                            dve.wait_ge(aggr, so_far((LN1 - 1, OUT), tile_of, s))
                            for k, w_ in ((1, t), (0, q)):
                                if w_ is not None:
                                    z = vec.tensor_scalar(pin[:, m.slot(2), H + 1 - k:H + 2 - k],
                                                          mv[:, k, w_.slot(2), 1:2], LN_EPS, None, ALU.add)
                        z.then_inc(var_ready, 1)
                    if r is not None:
                        dve.wait_ge(ranked, r.at(1, 1))
                        vec.tensor_tensor(rk[:, :], bY[:, D + E:D + 2 * E], const("ebase"), ALU.add
                                          ).then_inc(rk_done, 1)
                        wait(dve, seen_done, r.at(1))
                        vec.tensor_tensor(seen[:, (r + 1).slot(2), :], seen[:, r.slot(2), :], hot[:, :], ALU.add
                                          ).then_inc(seen_done, 1)
                    c = tile_of(SCORE)
                    if c is not None and c.c % 2 == 0:
                        dve.wait_ge(stated, c.per(2, 1, 1))
                        dve.wait_ge(rotated, w.at(1, 1) if w is not None else T)
                        vec.tensor_tensor(Sm, bSt, const("smask"), ALU.mult).then_inc(sm_done, 1)
                        dve.wait_ge(sm_done, c.per(2, 1, 1))
                        wait(dve, qs_done, c.per(2, 1))
                        vec.tensor_copy(S4[:, 0, :], Sm).then_inc(s4_hi, 1)
                        dve.wait_ge(s4_hi, c.per(2, 1, 1))
                        vec.tensor_tensor(S4[:, 1, :], Sm, S4[:, 0, :], ALU.subtract).then_inc(s4_done, 1)
                    if c is not None:
                        mask_round(c, 0)
                    t = tile_of(PV)
                    if t is not None:
                        dve.wait_ge(pv, t.at(1, 1))
                        dve.wait_ge(g_done, t.at(1, 1))
                        wait(dve, yt, t.at(1, -1))
                        vec.tensor_tensor(y[:, t.slot(2), :], ret, G[:, t.slot(2), :], ALU.mult
                                          ).then_inc(rg_done, 1)
                    if r is not None:
                        dve.wait_ge(rk_done, r.at(1, 1))
                        for k in range(2):
                            vec.scalar_tensor_tensor(out=junk[:, k, :], in0=const("e8"),
                                                     scalar=ix[:, r.slot(4), k:k + 1], in1=rk[:, :],
                                                     op0=ALU.is_equal, op1=ALU.mult,
                                                     accum_out=pos2[:, r.slot(4), k:k + 1]).then_inc(pos_f, 1)
                    for k, (off, done, used) in enumerate(((XN, nm1, xn_done), (XN2, nm2, xn2_done))):
                        t = tile_of(off)
                        if t is not None:
                            dve.wait_ge(rstd, n.at(1))
                            wait(dve, used, t.at(1, -1))
                            vec.scalar_tensor_tensor(
                                out=nm[:, k, t.slot(2):t.slot(2) + 1], in0=mv[:, k, t.slot(2), 0:1], scalar=-1.0,
                                in1=pout[:, (n + -1).slot(2), H + 1 - k:H + 2 - k],
                                op0=ALU.mult, op1=ALU.mult).then_inc(done, 1)
                    if r is not None:
                        dve.wait_ge(pos_f, r.at(2, 2))
                        wait(dve, scat[r.slot(4)], r.per(4, 32))
                        vec.tensor_copy(posi[:, r.slot(4), :], pos2[:, r.slot(4), :]).then_inc(pos_done, 1)
                        if r.c % 4 == 3:
                            vec.tensor_copy(group(POS, r), pos2[:, :, :])
                    if c is not None:
                        mask_round(c, 1)
                    t = tile_of(PV)
                    if t is not None:
                        dve.wait_ge(sq_done, t.at(1, 1))
                        vec.tensor_reduce(pin[:, n.slot(2), 0:H], sq[:, :].rearrange("p (h e) -> p h e", h=H),
                                          AX.X, ALU.add).then_inc(ss_done, 1)
                    if w is not None:
                        dve.wait_ge(hi4, w.at(2, 2))
                        rr = QKC[:, 0:2 * D].rearrange("p (a h e) -> p a h e", a=2, h=H)
                        for a, slot in ((0, 1), (1, 2)):
                            vec.tensor_tensor(q4[:, a, :, slot, :], rr[:, a], q4[:, a, :, 0, :], ALU.subtract
                                              ).then_inc(lo4, 1)
                        for a, slot in ((0, 1), (1, 2)):
                            dve.wait_ge(lo4, w.at(2, a + 1))
                            vec.tensor_copy(q4[:, a, :, 3, :], q4[:, a, :, slot, :]).then_inc(dup4, 1)
                    shared_hidden(s, 0)
                    t = tile_of(YT)
                    if t is not None:
                        dve.wait_ge(y_hi, t.at(1, 1))
                        if tile_of(X2T) is not None:
                            dve.wait_ge(x2_hi, tile_of(X2T).at(1, 1))
                        vec.tensor_tensor(ys[:, 1], bY[:, 0:D].rearrange("p (k n) -> p k n", k=KC), ys[:, 0],
                                          ALU.subtract).then_inc(y_lo, 1)
                    t = tile_of(X2T)
                    if t is not None:
                        dve.wait_ge(x2_hi, t.at(1, 1))
                        o = XT[:, bass.ds(t.at(1), 1)]
                        vec.tensor_tensor(o[:, :, 1].rearrange("p o k n -> p (o k n)"), bY[:, D:2 * D],
                                          o[:, :, 0].rearrange("p o k n -> p (o k n)"), ALU.subtract
                                          ).then_inc(x2_lo, 1)
                    t = tile_of(PROJ)
                    if t is not None:
                        if s == FIRST + 2:
                            dve.wait_ge(rot_in, 16)
                        dve.wait_ge(proj_qk, t.at(1, 1))
                        wait(dve, hi4, t.at(2))
                        k = t.c % 2
                        vec.tensor_tensor(QKC[:, 0:2 * D], bQK[:, :], rot[:, 0, k, :], ALU.mult
                                          ).then_inc(rotc, 1)
                        wait(dve, rotated, t.at(1))
                        if c is not None:
                            dve.wait_ge(s4_done, c.per(2, 1, 1))
                        pair = bQK[:, :].rearrange("p (a two) -> p a two", two=2)[:, :, ::-1]
                        vec.tensor_tensor(swp[:, :].rearrange("p (a two) -> p a two", two=2), pair,
                                          rot[:, 1, k, :].rearrange("p (a two) -> p a two", two=2), ALU.mult
                                          ).then_inc(rots, 1)
                    shared_hidden(s, 1)

                steps(dve, step, {FIRST + 2: weights})

            @block.tensor
            def _(pe):
                mm = nc.tensor.matmul

                def three(out, parts, first=True, last=True):
                    ops = [(sh, mh) for sh, sl, mh, ml in parts] + \
                          [(sh, ml) for sh, sl, mh, ml in parts] + [(sl, mh) for sh, sl, mh, ml in parts]
                    for k, (st, mo) in enumerate(ops):
                        z = mm(out, st, mo, start=first and k == 0, stop=last and k == len(ops) - 1)
                    return z

                def wa(name, k, a=0, b=None):
                    n = (cuta[name].stop - cuta[name].start) // KC
                    lo = cuta[name].start + k * n
                    b = n if b is None else b
                    return WAH[:, lo + a:lo + b], WAL[:, lo + a:lo + b]

                pe.wait_ge(consts_in, 2 * 16)
                pe.wait_ge(prep_p, 3)

                def slots_transposed(a, done):
                    src = q4[:, a].rearrange("p (g b) j e -> p g (b j e)", b=2)
                    for g in range(H // 2):
                        z = nc.tensor.transpose(bQT[:, g, :], src[:, g, :], const16("ident"))
                    z.then_inc(done, 1)

                def score_round(t, r):
                    wait(pe, masked, t.at(3, 2 * r))
                    wait(pe, copied, t.at(1))
                    for g in range(4):
                        for a in range(2):
                            q = slice(64 * a, 64 * a + 64)
                            z = mm(bS[a][:, g, :], KT[q, 4 * r + g, :], QT[q, 4 * r + g, :],
                                   start=True, stop=True)
                    z.then_inc(scored, 1)

                def shared_expert(s, half):
                    d, e = drain(s, half)
                    if d is not None:
                        wait(pe, f_gelu, d - 1)
                        pe.wait_ge(rots if d % 2 == 0 else g_done, T)
                        pe.wait_ge(w_lo, DOWN + 2)
                        pe.wait_ge(x2_lo, d + 1)
                        h = f_hT[d % 2].rearrange("p (f n) -> p f n", f=FC)
                        for f in range(FC):
                            c = slice(P * f, P * f + P)
                            z = three(h[:, f, :], [(WFH[:, UP + k, c], WFL[:, UP + k, c], XT[:, d, 0, k], XT[:, d, 1, k])
                                                   for k in range(KC)])
                        z.then_inc(f_up, 1)
                    if e is not None:
                        pe.wait_ge(f_lo, e + 1)
                        wait(pe, f_out, e - 1)
                        hh, hl = (f_hs[e % 2][:, a, :].rearrange("p (f n) -> p f n", f=FC) for a in range(2))
                        three(f_y[e % 2], [(hh[:, k], hl[:, k],
                                            *(a[:, DOWN + k // 2, D * (k % 2):D * (k % 2) + D] for a in (WFH, WFL)))
                                           for k in range(FC)]).then_inc(f_down, 1)

                def step(tile_of, s):
                    t = tile_of(PROJ)
                    if t is not None:
                        pe.wait_ge(xn_done, t.at(1, 1))
                        pe.wait_ge(ctx_in[t.slot(2)], t.per(2, 16, 16))
                        wait(pe, xc_lo, t.at(1))
                        for k in range(KC):
                            nc.tensor.transpose(bT[:, k, :], xn[:, t.slot(2), P * k:P * k + P], const("ident"))
                        for k in range(KC):
                            z = nc.tensor.transpose(bT[:, KC + k, :], ctxb[:, t.slot(2), P * k:P * k + P],
                                                    const("ident"))
                        z.then_inc(t1, 1)
                    p = tile_of(PV)
                    if p is not None:
                        wait(pe, ss_done, p.at(1))
                        if p.c % 2:
                            pe.wait_ge(s4_done, p.per(2, 1, 1))
                            for a in range(2):
                                for g in range(H // 2):
                                    z = mm(bRT[32 * (g % 4):32 * (g % 4) + 32, g // 4, :],
                                           S4[:, a, 32 * g:32 * g + 32], QT[:, g, :],
                                           start=a == 0 and g < 4, stop=False)
                            z.then_inc(qs_done, 1)
                    w = tile_of(SCORE)
                    if w is not None:
                        pe.wait_ge(dup4, w.at(2, 2))
                        wait(pe, kt_out, w.at(1))
                        wait(pe, sm_done, (w + 1).per(2, 1))
                        slots_transposed(0, qt)
                    t = tile_of(OUT)
                    if t is not None:
                        pe.wait_ge(y_lo, t.at(1, 1))
                        if tile_of(ROUTE) is not None:
                            pe.wait_ge(x2_lo, tile_of(ROUTE).at(1, 1))
                        three(bY[:, 0:D], [(ys[:, 0, k], ys[:, 1, k], *wa("out", k)) for k in range(KC)], last=False)
                        mm(bY[:, 0:D], const16("ones"), biasw[:, D:2 * D], start=False, stop=True).then_inc(outp, 1)
                    t = tile_of(ROUTE)
                    if t is not None:
                        pe.wait_ge(x2_lo, t.at(1, 1))
                        xt = XT[:, bass.ds(t.at(1), 1)]
                        three(bY[:, D:D + E], [(xt[:, :, 0, k].rearrange("p o n -> p (o n)"),
                                                xt[:, :, 1, k].rearrange("p o n -> p (o n)"), *wa("gate", k))
                                               for k in range(KC)]).then_inc(logit, 1)
                    shared_expert(s, 0)
                    if w is not None:
                        pe.wait_ge(qt_out, w.at(1, 1))
                        slots_transposed(1, kt)
                    t = tile_of(PROJ)
                    if t is not None:
                        pe.wait_ge(xc_lo, t.at(1, 1))
                        wait(pe, rots, t.at(1))
                        if s == FIRST + 2:
                            pe.wait_ge(prep_v, 1)
                        three(bQK[:, 0:D], [(xcs[:, 0, k], xcs[:, 1, k], *wa("qkvg", k, 0, D)) for k in range(KC)])
                        three(bQK[:, D:2 * D], [(xcs[:, 0, KC + k], xcs[:, 1, KC + k], *wa("qkvg", k, D, 2 * D))
                                                for k in range(KC)]).then_inc(proj_qk, 1)
                    if w is not None:
                        pe.wait_ge(kt_out, w.at(1, 1))
                        if w.c % 2 == 0:
                            pe.wait_ge(vs_done, w.per(2, 1, 1))
                            kk = q4[:, 1].rearrange("p (g b) j e -> p g (b j e)", b=2)
                            for g in range(H // 2):
                                for a in range(2):
                                    z = mm(bSt[:, 32 * g:32 * g + 32], kk[:, g, :],
                                           VS[:, a, 32 * g:32 * g + 32], start=a == 0, stop=a == 1)
                            z.then_inc(stated, 1)
                        score_round(w, 0)
                    t = tile_of(ROUTE)
                    if t is not None:
                        pe.wait_ge(hot_done, t.at(1, 1))
                        wait(pe, seen_done, t.at(1))
                        mm(bY[:, D + E:D + 2 * E], const16("before"), hot[:, :], start=True, stop=False)
                        mm(bY[:, D + E:D + 2 * E], const16("ones"), seen[:, t.slot(2), :], start=False, stop=True
                           ).then_inc(ranked, 1)
                    if p is not None:
                        for c in range(KC):
                            pe.wait_ge(masked, p.at(3, 2 + c))
                            if c:
                                pe.wait_ge(masked_p, p.at(1, 1))
                            for a in range(2):
                                for k in range(4):
                                    g = 4 * c + k
                                    z = mm(bRT[32 * k:32 * k + 32, c, :],
                                           V[:, p.slot(2), g, 2 * a:2 * a + 2, :].rearrange("p a e -> p (a e)"),
                                           sim[:, 2 * g + a, :], start=p.c % 2 == 0 and c == 0 and a == 0,
                                           stop=c == 1 and a == 1)
                            z.then_inc(pvt if c else pvh, 1)
                    t, r = tile_of(YT), tile_of(X2T)
                    if t is not None or r is not None:
                        a = tile_of(OUT)
                        if a is not None:
                            pe.wait_ge(x2_done, a.at(1, 1))
                        a = tile_of(ROUTE)
                        if a is not None:
                            pe.wait_ge(rk_done, a.at(1, 1))
                    if r is not None:
                        pe.wait_ge(xn2_done, r.at(1, 1))
                        for k in range(KC):
                            z = nc.tensor.transpose(bY[:, D + P * k:D + P * k + P], xn2[:, r.slot(4), P * k:P * k + P],
                                                    const("ident"))
                        z.then_inc(x2t, 1)
                    if p is not None:
                        pe.wait_ge(rt_out, p.at(1, 1))
                        for c in range(KC):
                            z = nc.tensor.transpose(ret[:, P * c:P * c + P], rT[:, c, :], const("ident"))
                        z.then_inc(pv, 1)
                    if t is not None:
                        pe.wait_ge(y_done, t.at(1, 1))
                        for k in range(KC):
                            z = nc.tensor.transpose(bY[:, P * k:P * k + P], y[:, t.slot(2), P * k:P * k + P],
                                                    const("ident"))
                        z.then_inc(yt, 1)
                    if w is not None:
                        score_round(w, 1)
                    t = tile_of(PROJ)
                    if t is not None:
                        wait(pe, g_done, t.at(1))
                        if s == FIRST + 2:
                            pe.wait_ge(prep_v, 3)
                            pe.wait_ge(dve_chain, CENTRED)
                            pe.wait_ge(c16_in, 16)
                        three(bVG[:, 0:D], [(xcs[:, 0, KC + k], xcs[:, 1, KC + k], *wa("qkvg", k, 2 * D, 3 * D))
                                            for k in range(KC)])
                        three(bVG[:, D:2 * D], [(xcs[:, 0, k], xcs[:, 1, k], *wa("qkvg", k, 3 * D, 4 * D))
                                                for k in range(KC)], last=False)
                        mm(bVG[:, D:2 * D], const16("ones"), biasw[:, 0:D], start=False, stop=True
                           ).then_inc(proj_vg, 1)
                    shared_expert(s, 1)
                steps(pe, step)

        NS = 4
        E0, E1 = NS, NS + NJ
        RING = 5
        NP = T - ND + NJ
        with ExitStack() as c2:
            s2 = lambda name, shape, dt=F32: sb(name, shape, dt, c2)
            xg = s2("xg", [P, 4, D])
            xgs = s2("xgs", [P, 2, 2, KC, P], F16)
            g = s2("g", [P, 2, F])
            hs = s2("hs", [P, 2, 2, FC, P], F16)
            yb = s2("yb", [P, 4, D])
            Y12 = s2("Y12", [P, RING, 2, D])
            zero = s2("zero", [P, D])
            nt, cum, cs, delta, oneE, junk2 = (s2(n, [P, E]) for n in ("nt", "cum", "cs", "delta", "oneE", "junk2"))
            nti = s2("nti", [P, E], I32)
            zrow = s2("zrow", [1, E], I32)
            tj = s2("tj", [P, 5])
            which = s2("which", [P, 2 * T, E])
            ints = s2("ints", [P, 2 * NJ], I32)
            posk = s2("posk", [P, T, 2], I32)
            posg = s2("posg", [P, RING, 2], I32)
            ex = s2("ex", [P, T])
            den = s2("den", [P, T])
            offs = s2("offs", [P, 2 * T])
            a12 = s2("a12", [P, T, 2])

            uA = [ps(f"uA{k}", [P, F], F32, c2) for k in range(2)]
            hT = [ps(f"hT{k}", [P, FC, P], F32, c2) for k in range(2)]
            yD = [ps(f"yD{k}", [P, D], F32, c2) for k in range(2)]
            xg_t = ps("xg_t", [P, KC, P], F32, c2)
            cnt = ps("cnt", [P, E], F32, c2)

            counted, tiles_known = sem("counted"), sem("tiles_known")
            ch = sem("ch")
            rows_known, zeroed, zfill = sem("rows_known"), sem("zeroed"), sem("zfill")
            zrows_known, turned = sem("zrows_known"), sem("turned")
            ex_done, mix_done, posk_done = sem("ex_done"), sem("mix_done"), sem("posk_done")
            xg_in = [sem(f"xg_in{k}") for k in range(4)]
            xgt, xg_hi, xg_lo = sem("xgt"), sem("xg_hi"), sem("xg_lo")
            up_done, gelu_done, ht_done = sem("up_done"), sem("gelu_done"), sem("ht_done")
            h_hi, h_lo, down_done = sem("h_hi"), sem("h_lo"), sem("down_done")
            y_out, s_out = sem("y_out"), sem("s_out")
            stored = [sem(f"stored{k}") for k in range(4)]
            posg_done = sem("posg_done")
            y12 = [sem(f"y12_{k}") for k in range(RING)]
            mix1, mixed = sem("mix1"), sem("mixed")
            written = sem("written")

            LOAD, XTR, UPS, HTR, DNS = 4, 2, 1, 0, -1
            CF = E1 + 1
            PACE = ((0,), (1,), (2,), (3, 4))
            LOOPS = ((9, 69), (E1 + 4, E1 + 20))
            LATE = LOOPS[1][0] - CF + (LOOPS[1][1] - LOOPS[1][0]) // UNROLL * RING
            STEPS = (-4, LOOPS[1][1] + (T - LATE + 1) // 2)

            def sums(s):
                k = 2 * (s - LOOPS[1][1]) + LATE
                return [Idx(m) for m in ([s - CF] if s < LOOPS[1][1] else [k, k + 1]) if 0 <= m < T]

            def steps2(eng, step, between=lambda: None):
                def kind(p):
                    return "routed" if E0 <= p < E1 else "shared"

                def straight(s):
                    step(lambda k: (Idx(s + k), kind(s + k)) if 0 <= s + k < NP else (None, None),
                         sums(s))
                at = STEPS[0]
                for a, b in LOOPS:
                    for s in range(at, a):
                        straight(s)
                        if s == LOOPS[0][1]:
                            between()
                    with eng.Fori(0, (b - a) // UNROLL) as i:
                        for u in range(UNROLL):
                            step(lambda k, u=u: (Idx(a + u + k, i), kind(a + k)),
                                 [Idx(a - CF + k, i, RING) for k in PACE[u]] if a > CF else [])
                    at = b
                for s in range(at, STEPS[1]):
                    straight(s)

            def routed(p):
                return p + -E0

            def shared(p, first):
                return p if first else p + -NJ

            def flat(a):
                return a[:, :, :].rearrange("p k n -> p (k n)")

            def hidden(p, kind):
                return flat(hT[p.slot(2)]) if kind == "routed" else g[:, p.slot(2), :]

            def ordinal(p):
                return shared(p, p.i is None and p.c < E0)

            def token_tile(p):
                return ordinal(p) + ND

            block = c2.enter_context(nc.Block())

            @block.sync
            def _(sp):
                sp.wait_ge(zrows_known, 1)
                sp.wait_ge(zeroed, 1)
                regs = [sp.alloc_register(f"zeros{e}") for e in range(E)]
                sp.load(regs, zrow[0:1, :])
                for e in range(E):
                    r = sp.snap(regs[e], min_val=0, max_val=E * CAP - P)
                    sp.dma_start(by_expert[bass.ds(r, P), :], zero[:, :]).then_inc(zfill, 16)
                sp.wait_ge(rows_known, 1)
                sp.wait_ge(zfill, E * 16)

                def step(at, ms):
                    p, kind = at(LOAD)
                    if kind == "routed":
                        j = routed(p)
                        wait(sp, xgt, j.at(1, -3))
                        r = sp.value_load(ints[0:1, bass.ds(j.at(1), 1)], min_val=0, max_val=E * CAP - P)
                        sp.dma_start(xg[:, j.slot(4), :], by_expert[bass.ds(r, P), :]).then_inc(xg_in[j.slot(4)], 16)
                    p, kind = at(DNS)
                    if kind == "routed":
                        j = routed(p)
                        sp.wait_ge(y_out, j.at(1, 1))
                        sp.dma_start(answers[bass.ds(j.at(P), P), :], yb[:, j.slot(4), :]
                                     ).then_inc(stored[j.slot(4)], 16)
                    for m in ms:
                        sp.wait_ge(mixed, m.at(1, 1))
                        sp.dma_start(out_v[bass.ds(m.at(1), 1)].rearrange("o p d -> p (o d)"),
                                     X[:, bass.ds(m.at(1), 1), :].rearrange("p o d -> p (o d)")
                                     ).then_inc(written, 16)
                steps2(sp, step)
                sp.wait_ge(written, T * 16)

            @block.gpsimd
            def _(pool):
                nc.gpsimd.memset(zero[:, :], 0.0).then_inc(zeroed, 1)
                pool.wait_ge(posk_done, 1)
                for k in range(4):
                    pool.wait_ge(stored[k], NJ // 4 * 16)

                def place(m):
                    wait(pool, mixed, m.at(1, 1 - RING))
                    wait(pool, posg_done, m.at(1))
                    nc.gpsimd.tensor_copy(posg[:, m.slot(RING), :],
                                          posk[:, bass.ds(m.at(1), 1), :].rearrange("p o d -> p (o d)")
                                          ).then_inc(posg_done, 1)

                def gather(m):
                    for a in range(2):
                        pool.indirect_dma_start(Y12[:, m.slot(RING), a, :], None, answers[:, :],
                                                bass.IndirectOffsetOnAxis(ap=posg[:, m.slot(RING), a:a + 1], axis=0)
                                                ).then_inc(y12[m.slot(RING)], 16)
                for k in range(RING):
                    place(Idx(k))
                    if k:
                        gather(Idx(k - 1))
                with pool.Fori(0, T // RING - 1) as i:
                    for k in range(RING):
                        place(Idx(RING + k, i, RING))
                        gather(Idx(RING + k - 1, i, RING))
                for k in range(T // RING * RING, T):
                    place(Idx(k))
                    gather(Idx(k - 1))
                pool.wait_ge(posg_done, T)
                gather(Idx(T - 1))

            @block.scalar
            def _(act):
                nc.scalar.activation(ex[:, :], GAP[:, :], ACT.Exp, scale=1.0 / WS).then_inc(ex_done, 1)

                def step(at, ms):
                    p, kind = at(XTR)
                    if kind == "routed":
                        j = routed(p)
                        act.wait_ge(xgt, j.at(1, 1))
                        wait(act, up_done, p.at(1, -1))
                        nc.scalar.activation(xgs[:, j.slot(2), 0], xg_t[:, :, :], ACT.Copy).then_inc(xg_hi, 1)
                    def up():
                        p, kind = at(UPS)
                        if p is None:
                            return
                        act.wait_ge(up_done, p.at(1, 1))
                        wait(act, h_lo, p.at(1, -1))
                        u = uA[p.slot(2)][:, :] if kind == "routed" else flat(hT[p.slot(2)])
                        nc.scalar.activation(g[:, p.slot(2), :], u, ACT.Gelu, scale=1.0 / WS
                                             ).then_inc(gelu_done, 1)
                    def high():
                        p, kind = at(HTR)
                        if p is None:
                            return
                        if kind == "routed":
                            act.wait_ge(ht_done, routed(p).at(1, 1))
                        else:
                            act.wait_ge(gelu_done, p.at(1, 1))
                        wait(act, down_done, p.at(1, -1))
                        nc.scalar.activation(flat(hs[:, p.slot(2), 0]), hidden(p, kind), ACT.Copy).then_inc(h_hi, 1)
                    for stage in ((up, high) if at(HTR)[1] == "routed" else (high, up)):
                        stage()
                    p, kind = at(DNS)
                    if kind == "routed":
                        j = routed(p)
                        act.wait_ge(down_done, p.at(1, 1))
                        wait(act, stored[j.slot(4)], j.per(4, 16))
                        nc.scalar.activation(yb[:, j.slot(4), :], yD[p.slot(2)][:, :], ACT.Copy).then_inc(y_out, 1)
                steps2(act, step)

            @block.vector
            def _(dve):
                vec = nc.vector
                n = [0]

                def link(op):
                    n[0] += 1
                    op.then_inc(ch, 1)
                    dve.wait_ge(ch, n[0])
                part = const("part")
                dve.wait_ge(counted, 1)
                vec.tensor_tensor(zrow[:, :], cnt[0:1, :], const("ebase")[0:1, :], ALU.add).then_inc(zrows_known, 1)
                link(vec.tensor_scalar(nti[:, :], cnt[:, :], float(P - 1), None, ALU.add))
                link(vec.tensor_scalar(nti[:, :], nti[:, :], 7, None, ALU.arith_shift_right))
                link(vec.tensor_copy(nt[:, :], nti[:, :]))
                link(vec.memset(oneE[:, :], 1.0))
                link(vec.tensor_tensor_scan(out=cum[:, :], data0=oneE[:, :], data1=nt[:, :], initial=0.0,
                                            op0=ALU.mult, op1=ALU.add))
                link(vec.tensor_tensor(cs[:, :], cum[:, :], nt[:, :], ALU.subtract))
                link(vec.scalar_tensor_tensor(out=delta[:, :], in0=cs[:, :], scalar=float(P), in1=const("ebase"),
                                              op0=ALU.mult, op1=ALU.subtract))
                link(vec.scalar_tensor_tensor(out=junk2[:, :], in0=cum[:, :], scalar=part, in1=oneE[:, :],
                                              op0=ALU.is_le, op1=ALU.mult, accum_out=tj[:, 0:1]))
                link(vec.scalar_tensor_tensor(out=junk2[:, :], in0=const("e8"), scalar=tj[:, 0:1], in1=delta[:, :],
                                              op0=ALU.is_equal, op1=ALU.mult, accum_out=tj[:, 1:2]))
                link(vec.scalar_tensor_tensor(out=tj[:, 2:3], in0=part, scalar=float(P), in1=tj[:, 1:2],
                                              op0=ALU.mult, op1=ALU.subtract))
                link(vec.scalar_tensor_tensor(out=tj[:, 3:4], in0=tj[:, 0:1], scalar=float(E), in1=tj[:, 2:3],
                                              op0=ALU.is_lt, op1=ALU.mult))
                vec.scalar_tensor_tensor(out=tj[:, 4:5], in0=tj[:, 0:1], scalar=float(E), in1=tj[:, 0:1],
                                         op0=ALU.is_lt, op1=ALU.mult).then_inc(tiles_known, 1)
                dve.wait_ge(turned, 1)
                vec.tensor_copy(ints[0:1, :], xg_t[0:1, :, :].rearrange("p k n -> p (k n)")[:, 0:2 * NJ]
                                ).then_inc(rows_known, 1)

                def answers_known():
                    link(vec.tensor_tensor(which[:, :, :], const("e8").unsqueeze(1).to_broadcast([P, 2 * T, E]),
                                           IDX[:, :, :].rearrange("p t k -> p (t k)").unsqueeze(2)
                                           .to_broadcast([P, 2 * T, E]), ALU.is_equal))
                    link(vec.tensor_tensor(which[:, :, :], which[:, :, :],
                                           delta[:, :].unsqueeze(1).to_broadcast([P, 2 * T, E]), ALU.mult))
                    link(vec.tensor_reduce(offs[:, :], which[:, :, :], AX.X, ALU.add))
                    vec.tensor_tensor(posk[:, :, :].rearrange("p t k -> p (t k)"),
                                      POS[:, :, :].rearrange("p t k -> p (t k)"), offs[:, :], ALU.add
                                      ).then_inc(posk_done, 1)
                    dve.wait_ge(ex_done, 1)
                    link(vec.tensor_scalar(den[:, :], ex[:, :], 1.0, None, ALU.add))
                    link(vec.reciprocal(den[:, :], den[:, :]))
                    link(vec.tensor_scalar(a12[:, :, 0], den[:, :], gains[:, 1:2], None, ALU.mult))
                    link(vec.tensor_tensor(a12[:, :, 1], ex[:, :], a12[:, :, 0], ALU.mult))

                def row(a, t):
                    return a[:, bass.ds(t.at(1), 1), :].rearrange("p o d -> p (o d)")

                def step(at, ms):
                    p, kind = at(XTR)
                    if kind == "routed":
                        j = routed(p)
                        dve.wait_ge(xg_hi, j.at(1, 1))
                        vec.tensor_tensor(xgs[:, j.slot(2), 1], xg_t[:, :, :], xgs[:, j.slot(2), 0], ALU.subtract
                                          ).then_inc(xg_lo, 1)
                    p, kind = at(HTR)
                    if p is not None:
                        dve.wait_ge(h_hi, p.at(1, 1))
                        vec.tensor_tensor(flat(hs[:, p.slot(2), 1]), hidden(p, kind), flat(hs[:, p.slot(2), 0]),
                                          ALU.subtract).then_inc(h_lo, 1)
                    p, kind = at(DNS)
                    if kind == "shared":
                        t = token_tile(p)
                        dve.wait_ge(down_done, p.at(1, 1))
                        vec.scalar_tensor_tensor(out=row(X, t), in0=yD[p.slot(2)][:, :], scalar=gains[:, 1:2],
                                                 in1=row(X, t), op0=ALU.mult, op1=ALU.add).then_inc(s_out, 1)
                    for m in ms:
                        dve.wait_ge(y12[m.slot(RING)], m.per(RING, 32, 32))
                        wait(dve, mixed, m.at(1))
                        for k, done in ((0, mix1), (1, mixed)):
                            if k:
                                dve.wait_ge(mix1, m.at(1, 1))
                            vec.scalar_tensor_tensor(
                                out=row(X, m), in0=Y12[:, m.slot(RING), k, :],
                                scalar=a12[:, bass.ds(m.at(1), 1), k], in1=row(X, m),
                                op0=ALU.mult, op1=ALU.add).then_inc(done, 1)
                steps2(dve, step, answers_known)

            @block.tensor
            def _(pe):
                mm = nc.tensor.matmul
                mm(cnt[:, :], const16("ones"), seen[:, T % 2, :], start=True, stop=True).then_inc(counted, 1)

                def turn():
                    pe.wait_ge(tiles_known, 1)
                    row = xg_t[0:1, :, :].rearrange("p k n -> p (k n)")
                    for k in range(2):
                        z = mm(row[:, k * NJ:k * NJ + NJ], tj[0:NJ, 3 + k:4 + k], const("ident")[0:NJ, 0:NJ],
                               start=True, stop=True)
                    z.then_inc(turned, 1)
                turn()

                regs = [pe.alloc_register(f"expert{k}") for k in range(4)]
                known = {}

                def expert(p, kind):
                    if kind == "shared":
                        return 0
                    j = routed(p)
                    key = (j.c, j.i is None)
                    if key not in known:
                        c = j.c // 4 * 4
                        pe.load(regs, ints[0:1, bass.ds(Idx(c, j.i).at(1, NJ), 4)])
                        for k in range(4):
                            known[c + k, j.i is None] = pe.snap(regs[k], min_val=0, max_val=E - 1)
                    return known[key] * 2 + 2

                def unit(a, u):
                    return a[:, bass.ds(u, 1), :].rearrange("p o n -> p (o n)")

                def step(at, ms):
                    p, kind = at(XTR)
                    if kind == "routed":
                        j = routed(p)
                        if j.c == 0 and j.i is None:
                            pe.wait_ge(rows_known, 1)
                        pe.wait_ge(xg_in[j.slot(4)], j.per(4, 16, 16))
                        wait(pe, xg_lo, j.at(1))
                        for k in range(KC):
                            z = nc.tensor.transpose(xg_t[:, k, :], xg[:, j.slot(4), P * k:P * k + P], const("ident"))
                        z.then_inc(xgt, 1)
                    p, kind = at(UPS)
                    if p is not None:
                        e = expert(p, kind)
                        if kind == "routed":
                            wait(pe, gelu_done, p.at(1, -1))
                            j = routed(p)
                            pe.wait_ge(xg_lo, j.at(1, 1))
                            xh, xl = ([xgs[:, j.slot(2), a, k, :] for k in range(KC)] for a in range(2))
                        else:
                            wait(pe, h_lo, p.at(1, -1))
                            wait(pe, gelu_done, p.at(1, -1))
                            t = token_tile(p)
                            xt = XT[:, bass.ds(t.at(1), 1)]
                            xh, xl = ([xt[:, :, a, k].rearrange("p o n -> p (o n)") for k in range(KC)]
                                      for a in range(2))
                        if kind == "shared":
                            for f in range(FC):
                                for k in range(KC):
                                    wh, wl = (unit(a, e + (UP + k))[:, P * f:P * f + P] for a in (WFH, WFL))
                                    for q, (st, mo) in enumerate(((wh, xh[k]), (wl, xh[k]), (wh, xl[k]))):
                                        z = mm(hT[p.slot(2)][:, f, :], st, mo, start=k == 0 and q == 0,
                                               stop=k == KC - 1 and q == 2)
                        else:
                            for k in range(KC):
                                wh, wl = unit(WFH, e + (UP + k)), unit(WFL, e + (UP + k))
                                for q, (st, mo) in enumerate(((xh[k], wh), (xh[k], wl), (xl[k], wh))):
                                    z = mm(uA[p.slot(2)][:, :], st, mo, start=k == 0 and q == 0,
                                           stop=k == KC - 1 and q == 2)
                        z.then_inc(up_done, 1)
                    p, kind = at(HTR)
                    if kind == "routed":
                        pe.wait_ge(gelu_done, p.at(1, 1))
                        wait(pe, h_lo, p.at(1, -1))
                        for k in range(FC):
                            z = nc.tensor.transpose(hT[p.slot(2)][:, k, :], g[:, p.slot(2), P * k:P * k + P],
                                                    const("ident"))
                        z.then_inc(ht_done, 1)
                    p, kind = at(DNS)
                    if p is not None:
                        e = expert(p, kind)
                        pe.wait_ge(h_lo, p.at(1, 1))
                        q, was = at(DNS - 2)
                        if was == "routed":
                            pe.wait_ge(y_out, routed(q).at(1, 1))
                        elif was == "shared":
                            pe.wait_ge(s_out, ordinal(q).at(1, 1))
                        for k in range(FC):
                            u, c = e + (DOWN + k // 2), slice(D * (k % 2), D * (k % 2) + D)
                            wh, wl = unit(WFH, u)[:, c], unit(WFL, u)[:, c]
                            hh, hl = (hs[:, p.slot(2), a, k, :] for a in range(2))
                            for q_, (st, mo) in enumerate(((hh, wh), (hh, wl), (hl, wh))):
                                z = mm(yD[p.slot(2)][:, :], st, mo, start=k == 0 and q_ == 0,
                                       stop=k == FC - 1 and q_ == 2)
                        z.then_inc(down_done, 1)
                steps2(pe, step)


def kernel(x, ctx_1024, g_xattn, g_ffn, L0_xattn_W_Q, L0_xattn_W_K, L0_xattn_W_V, L0_xattn_g_w, L0_xattn_g_b,
           L0_xattn_out_w, L0_xattn_out_b, L0_ffn_Wg, L0_ffn_Wu, L0_ffn_Wd, L0_ffn_W1, L0_ffn_W2):
    import concourse.bacc as bacc
    from concourse.bass_utils import run_bass_kernel_spmd

    def heads(w):
        return np.asarray(w).transpose(1, 0, 2).reshape(D, D)

    def rows(w):
        w = np.asarray(w)
        return w.reshape(KC, P, w.shape[1]).transpose(1, 0, 2).reshape(P, -1)

    qkvg = np.concatenate([heads(L0_xattn_W_Q), heads(L0_xattn_W_K), heads(L0_xattn_W_V),
                           np.asarray(L0_xattn_g_w).T], axis=1)
    wa = np.concatenate([rows(qkvg), rows(np.asarray(L0_xattn_out_w).T), rows(L0_ffn_Wg)], axis=1)
    bias = np.concatenate([np.asarray(L0_xattn_g_b), np.asarray(L0_xattn_out_b)])
    bias = np.stack([bias, bias])
    gains = np.stack([np.concatenate([np.asarray(g_xattn), np.asarray(g_ffn)])] * P)
    ups = np.concatenate([np.asarray(L0_ffn_W1).reshape(2, P, F), np.asarray(L0_ffn_Wu).reshape(2 * E, P, F)])
    downs = np.concatenate([np.asarray(L0_ffn_W2).reshape(2, 2, P, D), np.asarray(L0_ffn_Wd).reshape(2 * E, 2, P, D)])
    wf = np.concatenate([ups, downs.transpose(0, 2, 1, 3).reshape(2 * E + 2, P, F)])
    c32, c16 = tables()
    arrays = dict(x=x, ctx=ctx_1024, wa=wa, bias=bias, gains=gains, wf=wf, c32=c32, c16=c16)
    arrays = {f"{k}_in": np.ascontiguousarray(np.asarray(v)) for k, v in arrays.items()}

    nc = bacc.Bacc("TRN2", target_bir_lowering=False, num_devices=1)
    args = [nc.dram_tensor(n, a.shape, mybir.dt.from_np(a.dtype), kind="ExternalInput").ap()
            for n, a in arrays.items()]
    out = nc.dram_tensor("out", (B, L, D), F32, kind="ExternalOutput").ap()
    build(nc, *args, out)
    r = run_bass_kernel_spmd(nc, [arrays], core_ids=[0])
    return r.results[0]["out"]
```
